# Optimizing a Trainium2 kernel written in Bass

```python
import numpy as np
import jax
import jax.numpy as jnp

def _softmax(x, axis=-1):
    return jax.nn.softmax(x, axis=axis)

def _gelu(x):
    return jax.nn.gelu(x, approximate=True)

def _silu(x):
    return jax.nn.silu(x)

def _sigmoid(x):
    return jax.nn.sigmoid(x)

def _layernorm(x, axis=-1, eps=1e-05):
    m = jnp.mean(x, axis=axis, keepdims=True)
    v = jnp.var(x, axis=axis, keepdims=True)
    return (x - m) / jnp.sqrt(v + eps)

def _scatter_add(tgt, idx, src, axis=0):
    return tgt.at[idx].add(src)

def _segment_sum(src, seg, n):
    return jax.ops.segment_sum(src, seg, n)
kernel_name = 'mk_gnn_preln_d4_gnn_r32_1e4fd7'

def setup_inputs(seed: int=0):
    np.random.seed(seed)
    _w = jnp.asarray

    def _rec_inputs():
        import jax
        import jax.numpy as jnp
        _gk = jax.random.key(seed)
        x = -0.0003929 + 0.9999 * jax.random.normal(jax.random.fold_in(_gk, 1), (3125, 256), jnp.float32)
        src = jax.random.randint(jax.random.fold_in(_gk, 2), (50000,), 0, 3125, jnp.int32)
        dst = jax.random.randint(jax.random.fold_in(_gk, 3), (50000,), 0, 3125, jnp.int32)
        _o = jnp.argsort(dst, stable=True)
        src = src[_o]
        dst = dst[_o]
        edge_attr_64 = 0.000279952 + 1.00013 * jax.random.normal(jax.random.fold_in(_gk, 12), (50000, 64), jnp.float32)
        edge_weight = 0.00540447 + 1.00226 * jax.random.normal(jax.random.fold_in(_gk, 14), (50000,), jnp.float32)
        return (x, src, dst, edge_attr_64, edge_weight)
    x, src, dst, edge_attr_64, edge_weight = _rec_inputs()

    def _L0_gnn_setup():
        import jax, jax.numpy as jnp
        import numpy as np
        from itertools import combinations
        NDIM = 256
        BATCH = 2048

        def _build_mat(rots, idx_i, idx_j, ndim):

            def step(mat, t):
                i, j, theta = t
                c = jnp.cos(theta)
                s = jnp.sin(theta)
                ri = mat[i]
                rj = mat[j]
                mat = mat.at[i].set(c * ri - s * rj)
                mat = mat.at[j].set(s * ri + c * rj)
                return (mat, None)
            mat0 = jnp.eye(ndim, dtype=rots.dtype)
            mat, _ = jax.lax.scan(step, mat0, (idx_i, idx_j, rots))
            return mat.T
        key = jax.random.key(seed)
        k1, k2 = jax.random.split(key)
        pairs = np.array(list(combinations(range(NDIM), 2)), dtype=np.int32)
        return {'x': jax.random.normal(k1, (BATCH, NDIM), dtype=jnp.float32), 'rots': jax.random.normal(k2, (pairs.shape[0],), dtype=jnp.float32), 'idx_i': jnp.asarray(pairs[:, 0]), 'idx_j': jnp.asarray(pairs[:, 1])}
    _L0_gnn_all = _L0_gnn_setup()
    _L0_gnn_in = {k: v for k, v in _L0_gnn_all.items() if k in ()}
    del _L0_gnn_all

    def _L1_gnn_setup():
        import jax, jax.numpy as jnp
        import numpy as np
        N, E = (625, 10000)
        IN_CH, EDGE_DIM = (256, 64)
        HEADS, OUT_CH = (8, 32)
        HC = HEADS * OUT_CH
        key = jax.random.key(seed)
        ks = jax.random.split(key, 12)
        s_in = 1.0 / np.sqrt(IN_CH)
        s_e = 1.0 / np.sqrt(EDGE_DIM)
        return {'x': jax.random.normal(ks[0], (N, IN_CH), dtype=jnp.float32), 'edge_index': jax.random.randint(ks[1], (2, E), 0, N, dtype=jnp.int64), 'edge_attr': jax.random.normal(ks[2], (E, EDGE_DIM), dtype=jnp.float32), 'Wq': jax.random.uniform(ks[3], (HC, IN_CH), jnp.float32, -s_in, s_in), 'bq': jnp.zeros((HC,), jnp.float32), 'Wk': jax.random.uniform(ks[4], (HC, IN_CH), jnp.float32, -s_in, s_in), 'bk': jnp.zeros((HC,), jnp.float32), 'Wv': jax.random.uniform(ks[5], (HC, IN_CH), jnp.float32, -s_in, s_in), 'bv': jnp.zeros((HC,), jnp.float32), 'We': jax.random.uniform(ks[6], (HC, EDGE_DIM), jnp.float32, -s_e, s_e), 'Wskip': jax.random.uniform(ks[7], (HC, IN_CH), jnp.float32, -s_in, s_in), 'bskip': jnp.zeros((HC,), jnp.float32)}
    _L1_gnn_all = _L1_gnn_setup()
    _L1_gnn_in = {k: v for k, v in _L1_gnn_all.items() if k in ('Wq', 'bq', 'Wk', 'bk', 'Wv', 'bv', 'We', 'Wskip', 'bskip')}
    del _L1_gnn_all

    def _L2_gnn_setup():
        import jax, jax.numpy as jnp
        import numpy as np
        N = 50000
        E = 25000
        D_IN = 256
        HID = 32
        HEADS = 8
        D_OUT = 64
        NEG_SLOPE = 0.2

        def _gat_conv(x, src, dst, W, att_src, att_dst, bias, heads, out_dim, concat):
            n = x.shape[0]
            h = (x @ W.T).reshape(n, heads, out_dim)
            a_s = jnp.sum(h * att_src, axis=-1)
            a_d = jnp.sum(h * att_dst, axis=-1)
            logits = jax.nn.leaky_relu(a_s[src] + a_d[dst], NEG_SLOPE)
            m = jax.ops.segment_max(logits, dst, num_segments=n)
            e = jnp.exp(logits - m[dst])
            den = jax.ops.segment_sum(e, dst, num_segments=n)
            alpha = e / (den[dst] + 1e-16)
            out = jax.ops.segment_sum(alpha[:, :, None] * h[src], dst, num_segments=n)
            out = out.reshape(n, heads * out_dim) if concat else out.mean(axis=1)
            return out + bias
        key = jax.random.key(seed)
        ks = jax.random.split(key, 12)
        x = jax.random.normal(ks[0], (N, D_IN), jnp.float32)
        edge_index = jax.random.randint(ks[1], (2, E), 0, N, dtype=jnp.int32)
        g = lambda k, shape, fan_in: jax.random.normal(k, shape, jnp.float32) / np.sqrt(fan_in)
        W0 = g(ks[2], (HEADS * HID, D_IN), D_IN)
        att_src0 = g(ks[3], (1, HEADS, HID), HID)
        att_dst0 = g(ks[4], (1, HEADS, HID), HID)
        b0 = jnp.zeros((HEADS * HID,), jnp.float32)
        W1 = g(ks[5], (1 * D_OUT, HEADS * HID), HEADS * HID)
        att_src1 = g(ks[6], (1, 1, D_OUT), D_OUT)
        att_dst1 = g(ks[7], (1, 1, D_OUT), D_OUT)
        b1 = jnp.zeros((D_OUT,), jnp.float32)
        return {'x': x, 'edge_index': edge_index, 'W0': W0, 'att_src0': att_src0, 'att_dst0': att_dst0, 'b0': b0, 'W1': W1, 'att_src1': att_src1, 'att_dst1': att_dst1, 'b1': b1}
    _L2_gnn_all = _L2_gnn_setup()
    _L2_gnn_in = {k: v for k, v in _L2_gnn_all.items() if k in ('W0', 'att_src0', 'att_dst0', 'b0', 'W1', 'att_src1', 'att_dst1', 'b1')}
    del _L2_gnn_all

    def _L3_gnn_setup():
        import jax, jax.numpy as jnp
        import numpy as np
        N, E = (50000, 25000)
        HID, EDIM, HEADS = (256, 64, 8)
        C = HID // HEADS
        NEG_SLOPE = 0.2
        LN_EPS = 1e-05

        def _gat_block(x, edge_index, edge_attr, W, W_e, att_src, att_dst, att_edge, bias, gamma, beta):
            n = x.shape[0]
            src, dst = (edge_index[0], edge_index[1])
            xp = (x @ W).reshape(n, HEADS, C)
            a_src = jnp.einsum('nhc,hc->nh', xp, att_src)
            a_dst = jnp.einsum('nhc,hc->nh', xp, att_dst)
            ep = (edge_attr @ W_e).reshape(-1, HEADS, C)
            a_edge = jnp.einsum('ehc,hc->eh', ep, att_edge)
            alpha = a_src[src] + a_dst[dst] + a_edge
            alpha = jax.nn.leaky_relu(alpha, NEG_SLOPE)
            m = jax.ops.segment_max(alpha, dst, num_segments=n)
            m = jnp.where(jnp.isfinite(m), m, 0.0)
            ea = jnp.exp(alpha - m[dst])
            den = jax.ops.segment_sum(ea, dst, num_segments=n)
            attn = ea / (den[dst] + 1e-16)
            msg = xp[src] * attn[:, :, None]
            out = jax.ops.segment_sum(msg, dst, num_segments=n)
            h = out.reshape(n, HEADS * C) + bias
            y = x + h
            mu = jnp.mean(y, axis=-1, keepdims=True)
            var = jnp.var(y, axis=-1, keepdims=True)
            return (y - mu) * jax.lax.rsqrt(var + LN_EPS) * gamma + beta
        key = jax.random.key(seed)
        ks = jax.random.split(key, 12)
        s = 1.0 / np.sqrt(HID)
        se = 1.0 / np.sqrt(EDIM)
        return {'x': jax.random.normal(ks[0], (N, HID), jnp.float32), 'edge_index': jax.random.randint(ks[1], (2, E), 0, N, jnp.int32), 'edge_attr': jax.random.normal(ks[2], (E, EDIM), jnp.float32), 'W': jax.random.uniform(ks[3], (HID, HEADS * C), jnp.float32, -s, s), 'W_e': jax.random.uniform(ks[4], (EDIM, HEADS * C), jnp.float32, -se, se), 'att_src': jax.random.normal(ks[5], (HEADS, C), jnp.float32) * 0.1, 'att_dst': jax.random.normal(ks[6], (HEADS, C), jnp.float32) * 0.1, 'att_edge': jax.random.normal(ks[7], (HEADS, C), jnp.float32) * 0.1, 'bias': jnp.zeros((HEADS * C,), jnp.float32), 'gamma': jnp.ones((HID,), jnp.float32), 'beta': jnp.zeros((HID,), jnp.float32)}
    _L3_gnn_all = _L3_gnn_setup()
    _L3_gnn_in = {k: v for k, v in _L3_gnn_all.items() if k in ('W', 'W_e', 'att_src', 'att_dst', 'att_edge', 'bias', 'gamma', 'beta')}
    del _L3_gnn_all
    return {'x': x, 'src': src, 'dst': dst, 'edge_attr_64': edge_attr_64, 'edge_weight': edge_weight, 'L1_gnn_Wq': _L1_gnn_in['Wq'], 'L1_gnn_bq': _L1_gnn_in['bq'], 'L1_gnn_Wk': _L1_gnn_in['Wk'], 'L1_gnn_bk': _L1_gnn_in['bk'], 'L1_gnn_Wv': _L1_gnn_in['Wv'], 'L1_gnn_bv': _L1_gnn_in['bv'], 'L1_gnn_We': _L1_gnn_in['We'], 'L1_gnn_Wskip': _L1_gnn_in['Wskip'], 'L1_gnn_bskip': _L1_gnn_in['bskip'], 'L2_gnn_W0': _L2_gnn_in['W0'], 'L2_gnn_att_src0': _L2_gnn_in['att_src0'], 'L2_gnn_att_dst0': _L2_gnn_in['att_dst0'], 'L2_gnn_b0': _L2_gnn_in['b0'], 'L2_gnn_W1': _L2_gnn_in['W1'], 'L2_gnn_att_src1': _L2_gnn_in['att_src1'], 'L2_gnn_att_dst1': _L2_gnn_in['att_dst1'], 'L2_gnn_b1': _L2_gnn_in['b1'], 'L3_gnn_W': _L3_gnn_in['W'], 'L3_gnn_W_e': _L3_gnn_in['W_e'], 'L3_gnn_att_src': _L3_gnn_in['att_src'], 'L3_gnn_att_dst': _L3_gnn_in['att_dst'], 'L3_gnn_att_edge': _L3_gnn_in['att_edge'], 'L3_gnn_bias': _L3_gnn_in['bias'], 'L3_gnn_gamma': _L3_gnn_in['gamma'], 'L3_gnn_beta': _L3_gnn_in['beta']}

def reference(x, src, dst, edge_attr_64, edge_weight, L1_gnn_Wq, L1_gnn_bq, L1_gnn_Wk, L1_gnn_bk, L1_gnn_Wv, L1_gnn_bv, L1_gnn_We, L1_gnn_Wskip, L1_gnn_bskip, L2_gnn_W0, L2_gnn_att_src0, L2_gnn_att_dst0, L2_gnn_b0, L2_gnn_W1, L2_gnn_att_src1, L2_gnn_att_dst1, L2_gnn_b1, L3_gnn_W, L3_gnn_W_e, L3_gnn_att_src, L3_gnn_att_dst, L3_gnn_att_edge, L3_gnn_bias, L3_gnn_gamma, L3_gnn_beta):
    import jax
    import jax.numpy as jnp

    def _L0_gnn_ref(x, rots, idx_i, idx_j):
        import jax, jax.numpy as jnp
        import numpy as np
        from itertools import combinations
        NDIM = 256
        BATCH = 2048

        def _build_mat(rots, idx_i, idx_j, ndim):

            def step(mat, t):
                i, j, theta = t
                c = jnp.cos(theta)
                s = jnp.sin(theta)
                ri = mat[i]
                rj = mat[j]
                mat = mat.at[i].set(c * ri - s * rj)
                mat = mat.at[j].set(s * ri + c * rj)
                return (mat, None)
            mat0 = jnp.eye(ndim, dtype=rots.dtype)
            mat, _ = jax.lax.scan(step, mat0, (idx_i, idx_j, rots))
            return mat.T
        m = _build_mat(rots, idx_i, idx_j, x.shape[-1])
        return x @ m

    def _L1_gnn_ref(x, edge_index, edge_attr, Wq, bq, Wk, bk, Wv, bv, We, Wskip, bskip):
        import jax, jax.numpy as jnp
        import numpy as np
        N, E = (625, 10000)
        IN_CH, EDGE_DIM = (256, 64)
        HEADS, OUT_CH = (8, 32)
        HC = HEADS * OUT_CH
        n = x.shape[0]
        src, dst = (edge_index[0], edge_index[1])
        q = (x @ Wq.T + bq).reshape(n, HEADS, OUT_CH)
        k = (x @ Wk.T + bk).reshape(n, HEADS, OUT_CH)
        v = (x @ Wv.T + bv).reshape(n, HEADS, OUT_CH)
        e = (edge_attr @ We.T).reshape(-1, HEADS, OUT_CH)
        k_e = k[src] + e
        v_e = v[src] + e
        alpha = jnp.einsum('ehc,ehc->eh', q[dst], k_e) / jnp.sqrt(jnp.float32(OUT_CH))
        m = jax.ops.segment_max(alpha, dst, num_segments=n)
        m = jnp.where(jnp.isfinite(m), m, 0.0)
        p = jnp.exp(alpha - m[dst])
        s = jax.ops.segment_sum(p, dst, num_segments=n)
        w = p / (s[dst] + 1e-16)
        out = jax.ops.segment_sum(v_e * w[:, :, None], dst, num_segments=n)
        out = out.reshape(n, HC) + (x @ Wskip.T + bskip)
        return out

    def _L2_gnn_ref(x, edge_index, W0, att_src0, att_dst0, b0, W1, att_src1, att_dst1, b1):
        import jax, jax.numpy as jnp
        import numpy as np
        N = 50000
        E = 25000
        D_IN = 256
        HID = 32
        HEADS = 8
        D_OUT = 64
        NEG_SLOPE = 0.2

        def _gat_conv(x, src, dst, W, att_src, att_dst, bias, heads, out_dim, concat):
            n = x.shape[0]
            h = (x @ W.T).reshape(n, heads, out_dim)
            a_s = jnp.sum(h * att_src, axis=-1)
            a_d = jnp.sum(h * att_dst, axis=-1)
            logits = jax.nn.leaky_relu(a_s[src] + a_d[dst], NEG_SLOPE)
            m = jax.ops.segment_max(logits, dst, num_segments=n)
            e = jnp.exp(logits - m[dst])
            den = jax.ops.segment_sum(e, dst, num_segments=n)
            alpha = e / (den[dst] + 1e-16)
            out = jax.ops.segment_sum(alpha[:, :, None] * h[src], dst, num_segments=n)
            out = out.reshape(n, heads * out_dim) if concat else out.mean(axis=1)
            return out + bias
        n = x.shape[0]
        loop = jnp.arange(n, dtype=edge_index.dtype)
        ei = jnp.concatenate([edge_index, jnp.stack([loop, loop])], axis=1)
        src, dst = (ei[0], ei[1])
        out1 = jax.nn.elu(_gat_conv(x, src, dst, W0, att_src0, att_dst0, b0, HEADS, HID, True))
        _ = _gat_conv(out1, src, dst, W1, att_src1, att_dst1, b1, 1, D_OUT, False)
        return out1

    def _L3_gnn_ref(x, edge_index, edge_attr, W, W_e, att_src, att_dst, att_edge, bias, gamma, beta):
        import jax, jax.numpy as jnp
        import numpy as np
        N, E = (50000, 25000)
        HID, EDIM, HEADS = (256, 64, 8)
        C = HID // HEADS
        NEG_SLOPE = 0.2
        LN_EPS = 1e-05

        def _gat_block(x, edge_index, edge_attr, W, W_e, att_src, att_dst, att_edge, bias, gamma, beta):
            n = x.shape[0]
            src, dst = (edge_index[0], edge_index[1])
            xp = (x @ W).reshape(n, HEADS, C)
            a_src = jnp.einsum('nhc,hc->nh', xp, att_src)
            a_dst = jnp.einsum('nhc,hc->nh', xp, att_dst)
            ep = (edge_attr @ W_e).reshape(-1, HEADS, C)
            a_edge = jnp.einsum('ehc,hc->eh', ep, att_edge)
            alpha = a_src[src] + a_dst[dst] + a_edge
            alpha = jax.nn.leaky_relu(alpha, NEG_SLOPE)
            m = jax.ops.segment_max(alpha, dst, num_segments=n)
            m = jnp.where(jnp.isfinite(m), m, 0.0)
            ea = jnp.exp(alpha - m[dst])
            den = jax.ops.segment_sum(ea, dst, num_segments=n)
            attn = ea / (den[dst] + 1e-16)
            msg = xp[src] * attn[:, :, None]
            out = jax.ops.segment_sum(msg, dst, num_segments=n)
            h = out.reshape(n, HEADS * C) + bias
            y = x + h
            mu = jnp.mean(y, axis=-1, keepdims=True)
            var = jnp.var(y, axis=-1, keepdims=True)
            return (y - mu) * jax.lax.rsqrt(var + LN_EPS) * gamma + beta
        return _gat_block(x, edge_index, edge_attr, W, W_e, att_src, att_dst, att_edge, bias, gamma, beta)
    edge_index = jnp.stack([src, dst])
    h = jnp.maximum(_layernorm(x, axis=-1), 0.0)
    x = x + _L0_gnn_ref(h, edge_weight, src, dst)
    h = jnp.maximum(_layernorm(x, axis=-1), 0.0)
    x = x + _L1_gnn_ref(h, edge_index, edge_attr_64, L1_gnn_Wq, L1_gnn_bq, L1_gnn_Wk, L1_gnn_bk, L1_gnn_Wv, L1_gnn_bv, L1_gnn_We, L1_gnn_Wskip, L1_gnn_bskip)
    h = jnp.maximum(_layernorm(x, axis=-1), 0.0)
    x = x + _L2_gnn_ref(h, edge_index, L2_gnn_W0, L2_gnn_att_src0, L2_gnn_att_dst0, L2_gnn_b0, L2_gnn_W1, L2_gnn_att_src1, L2_gnn_att_dst1, L2_gnn_b1)
    h = jnp.maximum(_layernorm(x, axis=-1), 0.0)
    x = x + _L3_gnn_ref(h, edge_index, edge_attr_64, L3_gnn_W, L3_gnn_W_e, L3_gnn_att_src, L3_gnn_att_dst, L3_gnn_att_edge, L3_gnn_bias, L3_gnn_gamma, L3_gnn_beta)
    return x

_drawn_inputs = setup_inputs


def setup_inputs(seed=0):
    import zlib

    import numpy as np

    out = dict(_drawn_inputs(seed))
    spreads = {'L1_gnn_bq': (0.0, 0.7),
     'L1_gnn_bk': (0.0, 2.0),
     'L1_gnn_bv': (0.0, 0.1),
     'L1_gnn_bskip': (0.0, 0.1),
     'L2_gnn_b0': (0.0, 0.1),
     'L2_gnn_b1': (0.0, 0.1),
     'L3_gnn_bias': (0.0, 0.1),
     'L3_gnn_gamma': (1.0, 0.2),
     'L3_gnn_beta': (0.0, 0.1)}
    factors = {'L1_gnn_Wk': 2.736,
     'L2_gnn_att_dst0': 2.942,
     'L3_gnn_W_e': 3.805,
     'L3_gnn_att_src': 5.22,
     'L3_gnn_att_dst': 57.139,
     'L3_gnn_att_edge': 3.691}
    for name, (base, spread) in spreads.items():
        noise = np.random.default_rng([zlib.crc32(name.encode()), seed]).standard_normal(out[name].shape)
        drawn = base * np.exp(spread * noise) if base else spread * noise
        out[name] = jnp.asarray(drawn.astype(out[name].dtype))
    for name, factor in factors.items():
        out[name] = (out[name] * factor).astype(out[name].dtype)
    return out
```

```python
from contextlib import ExitStack, contextmanager
import math

import numpy as np
import concourse.bass as bass
from concourse import mybir

F32 = mybir.dt.float32
I32 = mybir.dt.int32
ALU = mybir.AluOpType
ACT = mybir.ActivationFunctionType
AX = mybir.AxisListType

P = 125
N = 3125
NT = N // P
E = 50000
ET = E // P
D = 256
ED = 64
H = 8
C = D // H
ROT = 256

SLOT = 128
FILL = SLOT - 1
LIST_BLOCKS = -(-(2 * E // FILL + 10) // 8) * 8
FIELDS = 8
R1, R2, ALPHA, BETA, WR, EVENT, SIN, COS = range(FIELDS)
SKIP = float(1 << 20)
UB = 2
LEVELS = 7
TWO_PI_HI = 6.28125
TWO_PI_LO = 2 * math.pi - TWO_PI_HI
PI = 3.1415925


class Tally:

    def __init__(self, eng, sem, base=0):
        self.eng, self.sem, self.base, self.n = eng, sem, base, 0

    def up(self, ins):
        ins.then_inc(self.sem, 1)
        self.n += 1

    def then(self, ins):
        self.up(ins)
        self.eng.wait_ge(self.sem, self.base + self.n)


@contextmanager
def phase(nc):
    with ExitStack() as ph:
        taken = []

        def take(name):
            taken.append(nc.alloc_semaphore(name))
            return taken[-1]
        ph.sem = take
        yield ph
        nc.clear_and_free_semaphores(taken)
        nc.all_engine_barrier()


def peeled(eng, count, body):
    body(0)
    with eng.Fori(1, count) as i:
        body(i)


def pool_wait(pool, sem, value):
    pool.wait_ge(sem, value)
    pool.nop(nofuse=True)


def constants_phase(nc, con):
    with phase(nc) as ph:
        ii = ph.enter_context(nc.sbuf_tensor("c_iota_i", [128, 256], I32))
        pi = ph.enter_context(nc.sbuf_tensor("c_part_i", [128, 1], I32))
        made = ph.sem("c_made")
        dv = ph.sem("c_dve")
        with nc.Block() as block:
            @block.gpsimd
            def _(pool):
                pool.iota(ii[:], [[1, 256]], base=0, channel_multiplier=0).then_inc(made, 1)
                pool.iota(pi[:], [[1, 1]], base=0, channel_multiplier=1).then_inc(made, 1)

            @block.vector
            def _(dve):
                c = Tally(dve, dv)
                c.up(dve.memset(con["ones"][:], 1.0))
                dve.wait_ge(made, 2)
                c.up(dve.tensor_copy(con["iota"][:], ii[:]))
                c.then(dve.tensor_copy(con["part"][:, 0:1], pi[:]))
                c.up(dve.tensor_scalar(con["part"][:, 1:2], con["part"][:, 0:1], 128.0, None, ALU.add))
                c.up(dve.tensor_scalar(con["iota1"][:], con["iota"][:, 0:128], 1.0, None, ALU.add))
                c.up(dve.tensor_scalar(con["ident"][:], con["iota"][:, 0:128], con["part"][:, 0:1], None, ALU.is_equal))
                c.then(dve.tensor_scalar(con["after"][:], con["iota"][:, 0:128], con["part"][:, 0:1], None, ALU.is_gt))


def rotation_list_phase(nc, con, w_e, src_e, dst_e, rlist):
    with phase(nc) as ph:
        sb = lambda n, s, d=F32: ph.enter_context(nc.sbuf_tensor(n, s, d))
        sem = lambda n: ph.sem(n)
        ident, after, ones = con["ident"], con["after"], con["ones"]
        srcf, dstf, w = sb("l0_src", [P, ET]), sb("l0_dst", [P, ET]), sb("l0_w", [P, ET])
        srci, dsti = sb("l0_srci", [P, ET], I32), sb("l0_dsti", [P, ET], I32)
        ti = sb("l0_ti", [P, ET], I32)
        ta, tb, tc, act_, ev, ver, rolei = (sb(f"l0_{n}", [P, ET]) for n in ("ta", "tb", "tc", "active", "event", "ver", "rolei"))
        pos = sb("l0_pos", [P, ET], I32)
        pay = sb("l0_pay", [P, ET, FIELDS])
        pad = sb("l0_pad", [128, LIST_BLOCKS + 1, FIELDS])
        off, col, cnt = sb("l0_off", [1, ET]), sb("l0_col", [1, ET]), sb("l0_cnt", [1, 2])
        pstage = sb("l0_pstage", [P, 2, 4, FIELDS])
        istage = sb("l0_istage", [P, 2, 4], I32)
        psq = ph.enter_context(nc.psum_tensor("l0_psq", [128, 512], F32))
        psc = ph.enter_context(nc.psum_tensor("l0_psc", [128, 512], F32))
        (loaded, padset, filled, dv, angles, waves, versions, offsets, counted, placed, payset, staged) = (
            sem(f"l0_{n}") for n in ("loaded", "padset", "filled", "dve", "angles", "waves", "versions", "offsets",
                                     "counted", "placed", "payset", "staged"))
        scattered = [sem(f"l0_scattered{g}") for g in range(2)]

        with nc.Block() as block:
            @block.sync
            def _(sp):
                sp.dma_start(srci[:], src_e).then_inc(loaded, 16)
                sp.dma_start(dsti[:], dst_e).then_inc(loaded, 16)
                sp.dma_start(w[:], w_e).then_inc(loaded, 16)
                sp.wait_ge(padset, 2)
                sp.dma_start(rlist.rearrange("(p n) f -> p (n f)", p=128),
                             pad[:].rearrange("p n f -> p (n f)")).then_inc(filled, 16)

            @block.scalar
            def _(act):
                act.wait_ge(angles, 2)
                act.activation(pay[:, :, SIN], tb[:], ACT.Sin).then_inc(waves, 1)
                act.activation(pay[:, :, COS], tc[:], ACT.Sin).then_inc(waves, 1)

            @block.tensor
            def _(pe):
                pe.wait_ge(versions, 1)
                pe.matmul(psc[0:1, 0:ET], ones[0:P, 0:1], ver[:], start=True, stop=True).then_inc(counted, 1)
                pe.matmul(psq[0:P, 0:ET], after[0:P, 0:P], ver[:], start=True, stop=False)
                pe.wait_ge(offsets, 1)
                pe.matmul(psq[0:P, 0:ET], ones[0:1, 0:P], off[:], start=False, stop=True).then_inc(counted, 1)

            @block.vector
            def _(dve):
                c = Tally(dve, dv)
                dve.wait_ge(loaded, 48)
                c.up(dve.tensor_copy(srcf[:], srci[:]))
                c.then(dve.tensor_copy(dstf[:], dsti[:]))
                c.then(dve.tensor_tensor(ta[:], srcf[:], dstf[:], ALU.min))
                c.then(dve.tensor_scalar(act_[:], ta[:], float(ROT), None, ALU.is_lt))
                c.then(dve.tensor_tensor(ta[:], srcf[:], dstf[:], ALU.not_equal))
                c.then(dve.scalar_tensor_tensor(rolei[:], srcf[:], float(ROT), ta[:], ALU.is_lt, ALU.mult))
                c.then(dve.scalar_tensor_tensor(ev[:], dstf[:], float(ROT), rolei[:], ALU.is_lt, ALU.mult))
                c.up(dve.tensor_copy(pay[:, :, EVENT], ev[:]))
                dve.tensor_tensor(ver[:], act_[:], ev[:], ALU.add).then_inc(versions, 1)
                dve.wait_ge(counted, 1)
                c.then(dve.tensor_copy(col[:], psc[0:1, 0:ET]))
                c.then(dve.memset(ta[0:1, :], 1.0))
                c.then(dve.tensor_tensor_scan(off[:], ta[0:1, :], col[:], 0.0, ALU.mult, ALU.add))
                c.then(dve.tensor_copy(cnt[:, 0:1], off[:, ET - 1:ET]))
                dve.tensor_tensor(off[:], off[:], col[:], ALU.subtract).then_inc(offsets, 1)
                c.then(dve.tensor_scalar(cnt[:, 1:2], cnt[:, 0:1], 1.0 / (FILL * UB), 2.6, ALU.mult, ALU.add))
                c.up(dve.tensor_copy(con["iterations"][:], cnt[:, 1:2]))
                c.then(dve.tensor_scalar(ti[:], w[:], 1 / (2 * math.pi), None, ALU.mult))
                c.then(dve.tensor_copy(ta[:], ti[:]))
                c.then(dve.scalar_tensor_tensor(tb[:], ta[:], -TWO_PI_HI, w[:], ALU.mult, ALU.add))
                c.then(dve.scalar_tensor_tensor(tb[:], ta[:], -TWO_PI_LO, tb[:], ALU.mult, ALU.add))

                def wrap(x, bound, sign):
                    c.then(dve.tensor_scalar(ta[:], x, sign * PI, -sign * 2 * math.pi,
                                             ALU.is_gt if sign > 0 else ALU.is_lt, ALU.mult))
                    c.then(dve.tensor_tensor(x, x, ta[:], ALU.add))
                wrap(tb[:], PI, 1)
                wrap(tb[:], PI, -1)
                c.then(dve.tensor_scalar(tc[:], tb[:], math.pi / 2, None, ALU.add))
                wrap(tc[:], PI, 1)
                dve.tensor_scalar(tb[:], tb[:], PI, -PI, ALU.min, ALU.max).then_inc(angles, 1)
                dve.tensor_scalar(tc[:], tc[:], PI, -PI, ALU.min, ALU.max).then_inc(angles, 1)
                dve.wait_ge(counted, 2)
                c.then(dve.tensor_copy(ver[:], psq[0:P, 0:ET]))
                c.then(dve.tensor_scalar(ti[:], ver[:], 1.0 / FILL, None, ALU.mult))
                c.then(dve.tensor_copy(ta[:], ti[:]))
                c.then(dve.scalar_tensor_tensor(w[:], ta[:], float(FILL), ver[:], ALU.mult, ALU.is_gt))
                c.then(dve.tensor_tensor(ta[:], ta[:], w[:], ALU.subtract))
                c.then(dve.tensor_scalar(w[:], ta[:], float(FILL), float(FILL), ALU.mult, ALU.add))
                c.then(dve.tensor_tensor(w[:], w[:], ver[:], ALU.is_le))
                c.then(dve.tensor_tensor(ta[:], ta[:], w[:], ALU.add))
                c.then(dve.scalar_tensor_tensor(ta[:], ta[:], 1.0, ver[:], ALU.add, ALU.add))
                c.then(dve.tensor_scalar(w[:], act_[:], -SKIP, SKIP, ALU.mult, ALU.add))
                c.then(dve.tensor_tensor(ta[:], ta[:], w[:], ALU.add))
                dve.tensor_copy(pos[:], ta[:]).then_inc(placed, 1)
                c.up(dve.tensor_scalar(pay[:, :, R1], srcf[:], float(ROT - 1), None, ALU.min))
                c.then(dve.tensor_scalar(pay[:, :, R2], dstf[:], float(ROT - 1), None, ALU.min))
                c.then(dve.tensor_tensor(ver[:], pay[:, :, R1], pay[:, :, R2], ALU.subtract))
                c.then(dve.tensor_tensor(ver[:], ver[:], rolei[:], ALU.mult))
                c.up(dve.tensor_tensor(pay[:, :, WR], ver[:], pay[:, :, R2], ALU.add))
                c.then(dve.tensor_scalar(w[:], rolei[:], -1.0, 1.0, ALU.mult, ALU.add))
                dve.wait_ge(waves, 2)
                sn, cs = pay[:, :, SIN], pay[:, :, COS]
                c.up(dve.tensor_tensor(tb[:], cs, rolei[:], ALU.mult))
                c.then(dve.tensor_tensor(tc[:], sn, w[:], ALU.mult))
                c.then(dve.tensor_tensor(pay[:, :, ALPHA], tb[:], tc[:], ALU.add))
                c.up(dve.tensor_tensor(tb[:], sn, rolei[:], ALU.mult))
                c.then(dve.tensor_tensor(tc[:], cs, w[:], ALU.mult))
                dve.tensor_tensor(pay[:, :, BETA], tc[:], tb[:], ALU.subtract).then_inc(payset, 1)

            @block.gpsimd
            def _(pool):
                pool.memset(pad[:], 0.0).then_inc(padset, 1)
                pool.wait_ge(padset, 1)
                pool.memset(pad[:, :, WR], -1.0).then_inc(padset, 1)
                pool.wait_ge(placed, 1)
                pool.wait_ge(payset, 1)
                pool.wait_ge(filled, 16)

                def body(i):
                    for g in range(2):
                        if not isinstance(i, int):
                            pool_wait(pool, scattered[g], i * 64)
                        at = (i * 2 + g) * 4
                        pool.tensor_copy(pstage[:, g], pay[:, bass.ds(at, 4), :]).then_inc(staged, 1)
                        pool.tensor_copy(istage[:, g], pos[:, bass.ds(at, 4)]).then_inc(staged, 1)
                        pool_wait(pool, staged, i * 4 + g * 2 + 2)
                        for u in range(4):
                            pool.indirect_dma_start(
                                out=rlist, out_offset=bass.IndirectOffsetOnAxis(ap=istage[:, g, u:u + 1], axis=0),
                                in_=pstage[:, g, u, :], in_offset=None, bounds_check=LIST_BLOCKS * SLOT + SLOT - 1,
                                oob_is_err=False).then_inc(scattered[g], 16)
                peeled(pool, ET // 8, body)
                for g in range(2):
                    pool.wait_ge(scattered[g], 64 * (ET // 8))


def rotation_phase(nc, con, rlist, MT):
    with phase(nc) as ph:
        sb = lambda n, s, d=F32: ph.enter_context(nc.sbuf_tensor(n, s, d))
        sem = lambda n: ph.sem(n)
        ident, after, ones, iota, iota1, part = (con[k] for k in ("ident", "after", "ones", "iota", "iota1", "part"))
        U = range(UB)
        cur, prev = sb("r_cur", [128, UB, FIELDS]), sb("r_prev", [128, UB, FIELDS])
        fld, tmp = sb("r_fld", [128, UB, 8]), sb("r_tmp", [128, UB, 16])
        mask, late = sb("r_mask", [128, UB, 128]), sb("r_late", [128, 128])
        key = sb("r_key", [128, UB, 2, 128])
        lt = sb("r_lt", [128, UB, 2, 128])
        neu = sb("r_neu", [128, UB, 384])
        gat = sb("r_gat", [128, UB, 2, 256])
        last = sb("r_last", [128, UB, 256])
        owt = sb("r_owt", [128, UB, 2, 128])
        ft, ub = sb("r_ft", [128, UB, 2, 128]), sb("r_ub", [128, UB, 256])
        M = sb("r_M", [128, 2, 256])
        ps_w = [ph.enter_context(nc.psum_tensor(f"r_psw{u}", [128, 512], F32)) for u in U]
        ps_n = [ph.enter_context(nc.psum_tensor(f"r_psn{u}", [128, 512], F32)) for u in U]
        ps_a = [ph.enter_context(nc.psum_tensor(f"r_psa{u}", [128, 512], F32)) for u in U]
        ps_m = [ph.enter_context(nc.psum_tensor(f"r_psm{u}", [128, 512], F32)) for u in U]
        dv = sem("r_dve")
        loaded, writes, rows, lset, built, uset, level, evac, fset, fsub, vset, vcp, mset, applied = (
            [sem(f"r_{n}{u}") for u in U] for n in ("loaded", "writes", "rows", "lset", "built", "uset", "level", "evac",
                                                    "fset", "fsub", "vset", "vcp", "mset", "applied"))
        minit, tset = sem("r_minit"), sem("r_tset")

        def count(eng):
            return eng.value_load(con["iterations"][0:1, 0:1], min_val=2, max_val=LIST_BLOCKS // UB)

        with nc.Block() as block:
            @block.sync
            def _(sp):
                def body(i):
                    for u in U:
                        if not isinstance(i, int):
                            sp.wait_ge(built[u], i)
                        row = (i * UB + u) * SLOT
                        sp.dma_start(cur[:, u, :], rlist[bass.ds(row + 1, SLOT), :]).then_inc(loaded[u], 16)
                        sp.dma_start(prev[:, u, :], rlist[bass.ds(row, SLOT), :]).then_inc(loaded[u], 16)
                peeled(sp, count(sp), body)

            @block.vector
            def _(dve):
                PER = UB * 27
                init = Tally(dve, dv)
                init.up(dve.memset(M[:], 0.0))
                for u in U:
                    init.up(dve.memset(fld[:, u, :], 0.0))
                dve.wait_ge(dv, init.n)
                init.up(dve.tensor_copy(M[:, 0, 0:128], ident[:]))
                dve.tensor_copy(M[:, 1, 128:256], ident[:]).then_inc(minit, 1)
                dve.wait_ge(minit, 1)
                start = init.n

                def build(c, i, u):
                    s, b = cur[:, u, :], tmp[:, u, :]
                    f = fld[:, u, :]
                    pr = prev[:, u, :]
                    isb = pr[:, EVENT:EVENT + 1]
                    dve.wait_ge(loaded[u], i * 32 + 32)
                    c.up(dve.scalar_tensor_tensor(f[:, R1:R2 + 1], pr[:, R1:R2 + 1], isb, s[:, R1:R2 + 1], ALU.mult, ALU.add))
                    c.up(dve.scalar_tensor_tensor(f[:, ALPHA:BETA + 1], pr[:, SIN:COS + 1], isb, s[:, ALPHA:BETA + 1], ALU.mult, ALU.add))
                    c.then(dve.tensor_scalar(b[:, 0:1], pr[:, R2:R2 + 1], 1.0, None, ALU.add))
                    dve.scalar_tensor_tensor(f[:, WR:WR + 1], b[:, 0:1], isb, s[:, WR:WR + 1], ALU.mult, ALU.add).then_inc(writes[u], 1)
                    c.then(dve.tensor_tensor(b[:, 1:2], part[:, 0:1], isb, ALU.subtract))
                    c.up(dve.scalar_tensor_tensor(mask[:, u, :], iota[:, 0:128], b[:, 1:2], iota1[:], ALU.is_lt, ALU.mult))
                    dve.wait_ge(writes[u], i + 1)
                    dve.wait_ge(rows[u], i + 1)
                    dve.wait_ge(dv, c.base + c.n)
                    W = ps_w[u][:, 0:128]
                    c.up(dve.scalar_tensor_tensor(key[:, u, 0, :], W, f[:, R1:R1 + 1], mask[:, u, :], ALU.is_equal, ALU.mult))
                    c.then(dve.scalar_tensor_tensor(key[:, u, 1, :], W, f[:, R2:R2 + 1], mask[:, u, :], ALU.is_equal, ALU.mult))
                    c.up(dve.scalar_tensor_tensor(late[:], W, f[:, WR:WR + 1], after[:], ALU.is_equal, ALU.mult, accum_out=b[:, 8:9]))
                    c.then(dve.tensor_reduce(b[:, 2:4], key[:, u], AX.X, ALU.max))
                    c.up(dve.tensor_scalar(b[:, 4:6], b[:, 2:4], 0.5, None, ALU.max))
                    c.then(dve.scalar_tensor_tensor(b[:, 6:8], b[:, 2:4], 0.5, f[:, ALPHA:BETA + 1], ALU.is_lt, ALU.mult))
                    for o in range(2):
                        c.up(dve.tensor_scalar(lt[:, u, o, :], key[:, u, o, :], b[:, 4 + o:5 + o], f[:, ALPHA + o:ALPHA + o + 1],
                                               ALU.is_equal, ALU.mult))
                    dve.wait_ge(dv, c.base + c.n)
                    dve.tensor_tensor(neu[:, u, 256:384], lt[:, u, 0, :], lt[:, u, 1, :], ALU.add).then_inc(lset[u], 1)
                    for o in range(2):
                        c.up(dve.tensor_scalar(gat[:, u, o, :], iota[:], f[:, R1 + o:R1 + o + 1], b[:, 6 + o:7 + o],
                                               ALU.is_equal, ALU.mult))
                    c.then(dve.tensor_scalar(b[:, 9:10], b[:, 8:9], 0.5, None, ALU.is_lt))
                    c.up(dve.tensor_scalar(last[:, u, :], iota[:], f[:, WR:WR + 1], b[:, 9:10], ALU.is_equal, ALU.mult))
                    for h in range(2):
                        c.up(dve.tensor_scalar(owt[:, u, h, :], W, part[:, h:h + 1], None, ALU.is_equal))
                    dve.wait_ge(dv, c.base + c.n)
                    dve.tensor_tensor(gat[:, u, 0, :], gat[:, u, 0, :], gat[:, u, 1, :], ALU.add).then_inc(built[u], 1)

                def apply(c, i, u):
                    dve.wait_ge(fset[u], i + 1)
                    dve.tensor_tensor(ft[:, u], ps_a[u][:, 0:256].rearrange("p (h t) -> p h t", h=2), owt[:, u], ALU.subtract).then_inc(fsub[u], 1)
                    dve.wait_ge(mset[u], i + 1)
                    dve.tensor_tensor(M[:], M[:], ps_m[u][:].rearrange("p (h c) -> p h c", h=2), ALU.add).then_inc(applied[u], 1)
                    dve.wait_ge(applied[u], i + 1)

                def body(i):
                    c = Tally(dve, dv, start + i * per[0])
                    for u in U:
                        build(c, i, u)
                    for u in U:
                        apply(c, i, u)
                    assert per[0] in (0, c.n) or i == 0
                    per[0] = c.n
                per = [0]
                peeled(dve, count(dve), body)
                dve.wait_ge(tset, 1)
                dve.tensor_copy(MT[:], ps_w[0][:].rearrange("p (h c) -> p h c", h=2)).then_inc(tset, 1)

            @block.scalar
            def _(act):
                def body(i):
                    for u in U:
                        act.wait_ge(uset[u], i + 1)
                        act.copy(neu[:, u, 0:128], ps_w[u][:, 128:256]).then_inc(evac[u], 1)
                    for k in range(LEVELS):
                        for u in U:
                            act.wait_ge(level[u], i * LEVELS + k + 1)
                            act.copy(neu[:, u, :] if k < LEVELS - 1 else neu[:, u, 128:256],
                                     ps_n[u][:, 0:384] if k < LEVELS - 1 else ps_n[u][:, 128:256]).then_inc(evac[u], 1)
                    for u in U:
                        act.wait_ge(vset[u], i + 1)
                        act.copy(ub[:, u, :], ps_a[u][:, 256:512]).then_inc(vcp[u], 1)
                peeled(act, count(act), body)

            @block.gpsimd
            def _(pool):
                def body(i):
                    for u in U:
                        if not isinstance(i, int):
                            pool_wait(pool, fset[u], i)
                        pool.tensor_copy(neu[:, u, 128:256], ident[:]).then_inc(lset[u], 1)
                peeled(pool, count(pool), body)

            @block.tensor
            def _(pe):
                def body(i):
                    for u in U:
                        pe.wait_ge(writes[u], i + 1)
                        pe.matmul(ps_w[u][:, 0:128], fld[:, u, WR:WR + 1].to_broadcast([128, 128]), ident[:], start=True, stop=True).then_inc(rows[u], 1)
                    for u in U:
                        pe.wait_ge(lset[u], 2 * i + 2)
                        pe.wait_ge(built[u], i + 1)
                        pe.transpose(ps_w[u][:, 128:256], neu[:, u, 256:384], ident[:]).then_inc(uset[u], 1)
                    for k in range(LEVELS):
                        for u in U:
                            pe.wait_ge(evac[u], i * (LEVELS + 1) + k + 1)
                            n = neu[:, u, :]
                            z = ps_n[u][:, 128:256]
                            pe.matmul(z, n[:, 256:384], n[:, 128:256], start=True, stop=False)
                            mm = pe.matmul(z, ident[:], n[:, 128:256], start=False, stop=True)
                            if k < LEVELS - 1:
                                pe.matmul(ps_n[u][:, 0:128], n[:, 256:384], n[:, 0:128], start=True, stop=True)
                                mm = pe.matmul(ps_n[u][:, 256:384], n[:, 0:128], n[:, 256:384], start=True, stop=True)
                            mm.then_inc(level[u], 1)
                    for u in U:
                        pe.wait_ge(evac[u], (i + 1) * (LEVELS + 1))
                        for h in range(2):
                            mm = pe.matmul(ps_a[u][:, h * 128:h * 128 + 128], gat[:, u, 0, h * 128:h * 128 + 128], neu[:, u, 128:256],
                                           start=True, stop=True)
                        mm.then_inc(fset[u], 1)
                    for u in U:
                        pe.wait_ge(fsub[u], i + 1)
                        if u:
                            pe.wait_ge(applied[u - 1], i + 1)
                        elif not isinstance(i, int):
                            pe.wait_ge(applied[UB - 1], i)
                        else:
                            pe.wait_ge(minit, 1)
                        for h in range(2):
                            mm = pe.matmul(ps_a[u][:, 256:512], ft[:, u, h, :], M[:, h, :], start=(h == 0), stop=(h == 1))
                        mm.then_inc(vset[u], 1)
                        pe.wait_ge(vcp[u], i + 1)
                        for h in range(2):
                            mm = pe.matmul(ps_m[u][:, h * 256:h * 256 + 256], last[:, u, h * 128:h * 128 + 128], ub[:, u, :],
                                           start=True, stop=True)
                        mm.then_inc(mset[u], 1)
                n = count(pe)
                peeled(pe, n, body)
                pe.wait_ge(applied[UB - 1], n)
                for a in range(2):
                    for b in range(2):
                        mm = pe.transpose(ps_w[0][:, a * 256 + b * 128:a * 256 + b * 128 + 128], M[:, b, a * 128:a * 128 + 128], ident[:])
                mm.then_inc(tset, 1)


STEPS = ET + NT - 1
SQ = STEPS // 4
CH = 16
CE = E // CH
CT = CE // P
BIG = 2.0 ** 90
AW = 272
G = 4
EPS = 1e-5


def graph_phase(nc, con, g, src2, dst2, dst_e, dst_flat):
    with phase(nc) as ph:
        sb = lambda n, s, d=F32: ph.enter_context(nc.sbuf_tensor(n, s, d))
        sem = lambda n: ph.sem(n)
        ident, ones, part = con["ident"], con["ones"], con["part"]
        B = NT - 1
        lasti, lastf, lt = sb("g_lasti", [B, ET], I32), sb("g_lastf", [B, ET]), sb("g_lt", [B, ET])
        cut = sb("g_cut", [B, 4])
        stepi, stepf, comp = sb("g_stepi", [B, STEPS], I32), sb("g_stepf", [B, STEPS]), sb("g_comp", [B, STEPS])
        trow = sb("g_trow", [1, STEPS])
        pk = sb("g_pk", [1, STEPS // 4, 2])
        tcol, kcol, kidx = sb("g_tcol", [SQ, 4]), sb("g_kcol", [SQ, 4]), sb("g_kidx", [SQ, 4], I32)
        got, gf = sb("g_got", [SQ, 2, 4, P], I32), sb("g_gf", [SQ, 2, 4, P])
        dn = sb("g_dn", [128, CE + 2], I32)
        flag = sb("g_flag", [128, 2])
        ps_t = ph.enter_context(nc.psum_tensor("g_pst", [128, 512], F32))
        ps_c = ph.enter_context(nc.psum_tensor("g_psc", [128, 512], F32))
        ps_x = [ph.enter_context(nc.psum_tensor(f"g_psx{a}", [128, 512], F32)) for a in range(2)]
        ps_f = ph.enter_context(nc.psum_tensor("g_psf", [128, 512], F32))
        dv, iot, loaded, dset, compared, counted, kset, gathered, fset, turned, flagged, flagrow, evac = (
            sem(f"g_{n}") for n in ("dve", "iota", "loaded", "dset", "compared", "counted", "kset", "gathered", "fset",
                                    "turned", "flagged", "flagrow", "evac"))
        pads = sem("g_pads")
        with nc.Block() as block:
            @block.sync
            def _(sp):
                sp.dma_start(lasti[:], dst_e[P - 1:P, :].to_broadcast([B, ET])).then_inc(loaded, 16)
                sp.dma_start(g["srci"][:], g["src_e"]).then_inc(loaded, 16)
                sp.dma_start(g["dsti"][:], dst_e).then_inc(loaded, 16)
                sp.wait_ge(pads, 1)
                mid = bass.AP(dst_flat.tensor, dst_flat.offset + CE - 1, [[CE, CH - 2], [1, CE + 2]])
                flat = dst_flat.rearrange("(a n) -> a n", a=1)
                for h in range(H):
                    sp.dma_start(dn[H + h:128 - H:H, :], mid).then_inc(dset, 16)
                    sp.dma_start(dn[h:h + 1, 1:CE + 2], flat[:, 0:CE + 1]).then_inc(dset, 16)
                    sp.dma_start(dn[128 - H + h:128 - H + h + 1, 0:CE + 1], flat[:, E - CE - 1:E]).then_inc(dset, 16)

            @block.gpsimd
            def _(pool):
                pool.iota(stepi[:], [[1, STEPS]], base=0, channel_multiplier=0).then_inc(iot, 1)
                pool.wait_ge(kset, 1)
                for j in range(4):
                    for a, table in enumerate((src2, dst2)):
                        pool.indirect_dma_start(out=got[:, a, j, :], out_offset=None, in_=table,
                                                in_offset=bass.IndirectOffsetOnAxis(ap=kidx[:, j:j + 1], axis=0)).then_inc(gathered, 16)

            @block.tensor
            def _(pe):
                pe.wait_ge(compared, 1)
                pe.matmul(ps_t[0:1, 0:STEPS], ones[0:B, 0:1], comp[:], start=True, stop=True)
                for j in range(4):
                    mm = pe.matmul(ps_c[0:SQ, j:j + 1], comp[:, j * SQ:(j + 1) * SQ], ones[0:B, 0:1], start=True, stop=True)
                mm.then_inc(counted, 1)
                pe.wait_ge(fset, 1)
                for a in range(2):
                    for j in range(4):
                        mm = pe.transpose(ps_x[a][0:P, j * SQ:(j + 1) * SQ], gf[:, a, j, :], ident[0:SQ, 0:SQ])
                mm.then_inc(turned, 1)
                pe.wait_ge(flagged, 1)
                for a in range(2):
                    mm = pe.transpose(ps_f[0:1, a * 128:a * 128 + 128], flag[:, a:a + 1], ident[:])
                mm.then_inc(flagrow, 1)

            @block.vector
            def _(dve):
                c = Tally(dve, dv)
                dve.memset(dn[:, 0:CE + 2:CE + 1], -1).then_inc(pads, 1)
                dve.wait_ge(loaded, 48)
                dve.wait_ge(iot, 1)
                c.up(dve.tensor_copy(stepf[:], stepi[:]))
                c.then(dve.tensor_copy(lastf[:], lasti[:]))
                c.then(dve.tensor_scalar(cut[:, 0:1], part[0:B, 0:1], float(P), float(P), ALU.mult, ALU.add))
                c.then(dve.tensor_scalar(lt[:], lastf[:], cut[:, 0:1], None, ALU.is_lt))
                c.then(dve.tensor_reduce(cut[:, 1:2], lt[:], AX.X, ALU.add))
                c.then(dve.tensor_scalar(cut[:, 2:3], cut[:, 1:2], float(ET - 1), part[0:B, 0:1], ALU.min, ALU.add))
                dve.tensor_scalar(comp[:], stepf[:], cut[:, 2:3], None, ALU.is_gt).then_inc(compared, 1)
                dve.wait_ge(counted, 1)
                c.up(dve.tensor_copy(trow[:], ps_t[0:1, 0:STEPS]))
                c.then(dve.tensor_copy(tcol[:], ps_c[0:SQ, 0:4]))
                for j in range(4):
                    c.up(dve.tensor_scalar(kcol[:, j:j + 1], part[0:SQ, 0:1], float(j * SQ), tcol[:, j:j + 1], ALU.add, ALU.subtract))
                dve.wait_ge(dv, c.n)
                dve.tensor_copy(kidx[:], kcol[:]).then_inc(kset, 1)
                tg = trow[:].rearrange("a (q j) -> a q j", j=4)
                c.then(dve.scalar_tensor_tensor(pk[:, :, 0], tg[:, :, 3], 32.0, tg[:, :, 2], ALU.mult, ALU.add))
                c.then(dve.scalar_tensor_tensor(pk[:, :, 1], pk[:, :, 0], 32.0, tg[:, :, 1], ALU.mult, ALU.add))
                c.then(dve.scalar_tensor_tensor(pk[:, :, 0], pk[:, :, 1], 32.0, tg[:, :, 0], ALU.mult, ALU.add))
                c.up(dve.tensor_copy(g["tword"][:], pk[:, :, 0]))
                dve.wait_ge(dset, 48 * H)
                c.up(dve.tensor_tensor(g["startf"][:], dn[:, 1:CE + 1], dn[:, 0:CE], ALU.not_equal))
                c.then(dve.tensor_tensor(g["endf"][:], dn[:, 1:CE + 1], dn[:, 2:CE + 2], ALU.not_equal))
                c.up(dve.tensor_scalar(g["keep"][:], g["startf"][:], -1.0, 1.0, ALU.mult, ALU.add))
                c.up(dve.tensor_scalar(g["endf"][:], g["endf"][:], -BIG, None, ALU.mult))
                dve.wait_ge(dv, c.n)
                c.then(dve.tensor_scalar(g["startf"][:], g["startf"][:], -BIG, None, ALU.mult))
                c.up(dve.tensor_reduce(flag[:, 0:1], g["startf"][:], AX.X, ALU.min))
                dve.tensor_reduce(flag[:, 1:2], g["endf"][:], AX.X, ALU.min).then_inc(flagged, 1)
                dve.wait_ge(gathered, 128)
                c.then(dve.tensor_copy(gf[:], got[:]))
                c.then(dve.tensor_scalar(kcol[:], tcol[:], -float(P), None, ALU.mult))
                for j in range(4):
                    ins = dve.tensor_scalar(gf[:, 1, j, :], gf[:, 1, j, :], kcol[:, j:j + 1], None, ALU.add)
                    c.up(ins)
                dve.wait_ge(dv, c.n)
                dve.sem_inc(fset, 1)
                dve.wait_ge(turned, 1)
                c.up(dve.tensor_copy(g["srcs"][:], ps_x[0][0:P, 0:STEPS]))
                c.up(dve.tensor_copy(g["dstl"][:], ps_x[1][0:P, 0:STEPS]))
                dve.wait_ge(flagrow, 1)
                row = g["chunk"]
                for a in range(2):
                    c.up(dve.tensor_copy(row[:, a].rearrange("a (h c) -> a h c", h=H),
                                         ps_f[0:1, a * 128:a * 128 + 128].rearrange("a (c h) -> a h c", h=H)))
                dve.wait_ge(dv, c.n)
                c.up(dve.memset(row[:, 0].rearrange("a (h c) -> a h c", h=H)[:, :, 0:1], -BIG))
                c.then(dve.memset(row[:, 1].rearrange("a (h c) -> a h c", h=H)[:, :, CH - 1:CH], -BIG))
                c.then(dve.tensor_scalar(row[:, 2], row[:, 0], 1.0 / BIG, 1.0, ALU.mult, ALU.add))


def dense_phase(nc, con, g, layer, X, acc, weight, width, bias, tables):
    U = 5
    with phase(nc) as ph:
        sb = lambda n, s, d=F32: ph.enter_context(nc.sbuf_tensor(f"d{layer}_{n}", s, d))
        sem = lambda n: ph.sem(f"d{layer}_{n}")
        ident = con["ident"]
        st = sb("st", [P, NT, 6])
        mean, dif, var, rstd, nb = (sb(n, [P, NT]) for n in ("mean", "dif", "var", "rstd", "nb"))
        hn, ht = sb("hn", [P, U, D]), sb("ht", [128, U, 2, P])
        stage = sb("stage", [P, U, width])
        banks = -(-width // 512)
        ps_t = [ph.enter_context(nc.psum_tensor(f"d{layer}_pst{b}", [128, 512], F32)) for b in range(2)]
        ps_o = [ph.enter_context(nc.psum_tensor(f"d{layer}_pso{b}", [128, 512 * banks], F32)) for b in range(3)]
        dv, spread, rooted, ready, hset, tset, tcopied, mmdone, evac = (
            sem(n) for n in ("dve", "spread", "rooted", "ready", "hset", "tset", "tcopied", "mmdone", "evac"))
        stored = [sem(f"stored{u}") for u in range(U)]
        stores = len(tables)
        with nc.Block() as block:
            @block.vector
            def _(dve):
                with dve.Fori(0, NT) as n:
                    dve.bn_stats(st[:, bass.ds(n, 1), :].rearrange("p a s -> p (a s)"),
                                 X[:, bass.ds(n, 1), :].rearrange("p a d -> p (a d)")).then_inc(dv, 1)
                dve.wait_ge(dv, NT)
                c = Tally(dve, dv, NT)
                me, mo = st[:, :, 1], st[:, :, 4]
                c.up(dve.tensor_tensor(mean[:], me, mo, ALU.add))
                c.up(dve.tensor_tensor(dif[:], me, mo, ALU.subtract))
                c.then(dve.tensor_tensor(var[:], st[:, :, 2], st[:, :, 5], ALU.add))
                c.up(dve.tensor_scalar(mean[:], mean[:], 0.5, None, ALU.mult))
                c.then(dve.scalar_tensor_tensor(dif[:], dif[:], 0.25, dif[:], ALU.mult, ALU.mult))
                c.then(dve.scalar_tensor_tensor(var[:], var[:], 1.0 / D, dif[:], ALU.mult, ALU.add))
                dve.tensor_scalar(var[:], var[:], EPS, None, ALU.add).then_inc(spread, 1)
                dve.wait_ge(rooted, 1)
                c.then(dve.reciprocal(rstd[:], dif[:]))
                dve.scalar_tensor_tensor(nb[:], mean[:], -1.0, rstd[:], ALU.mult, ALU.mult).then_inc(ready, 1)

                def body(i):
                    for u in range(U):
                        n = i * U + u
                        x = X[:, bass.ds(n, 1), :].rearrange("p a d -> p (a d)")
                        dve.wait_ge(mmdone, n + 1)
                        if stores and not isinstance(i, int):
                            dve.wait_ge(stored[u], 16 * stores * i)
                        o = ps_o[u % 3][0:P, 0:width]
                        if layer == 0:
                            dve.tensor_tensor(x, x, o, ALU.add).then_inc(evac, 1)
                        elif layer == 1:
                            dve.tensor_tensor(stage[:, u, :], o, bias[:], ALU.add).then_inc(evac, 1)
                            dve.wait_ge(evac, n + 1)
                            dve.tensor_tensor(x, x, stage[:, u, 3 * D:4 * D], ALU.add).then_inc(dv, 1)
                        else:
                            if layer == 3:
                                dve.tensor_tensor(acc[:, bass.ds(n, 1), 0:D].rearrange("p a d -> p (a d)"), hn[:, u, :], bias[:], ALU.add).then_inc(dv, 1)
                            dve.tensor_copy(stage[:, u, :], o).then_inc(evac, 1)
                dve.wait_ge(ready, 1)
                peeled(dve, NT // U, body)

            @block.scalar
            def _(act):
                act.wait_ge(spread, 1)
                act.activation(dif[:], var[:], ACT.Sqrt).then_inc(rooted, 1)
                act.wait_ge(ready, 1)

                def body(i):
                    for u in range(U):
                        n = i * U + u
                        if not isinstance(i, int):
                            act.wait_ge(evac, n - U + 1)
                        act.activation(hn[:, u, :], X[:, bass.ds(n, 1), :].rearrange("p a d -> p (a d)"), ACT.Relu,
                                       bias=nb[:, bass.ds(n, 1)], scale=rstd[:, bass.ds(n, 1)]).then_inc(hset, 1)
                    for u in range(U):
                        n = i * U + u
                        act.wait_ge(tset, n + 1)
                        act.copy(ht[:, u], ps_t[u % 2][:, 0:2 * P].rearrange("p (a m) -> p a m", a=2)).then_inc(tcopied, 1)
                peeled(act, NT // U, body)

            @block.tensor
            def _(pe):
                def turn(i, u):
                    n = i * U + u
                    pe.wait_ge(hset, n + 1)
                    if u >= 2 or not isinstance(i, int):
                        pe.wait_ge(tcopied, n if u == 0 else n - 1)
                    for a in range(2):
                        mm = pe.transpose(ps_t[u % 2][:, a * P:(a + 1) * P], hn[:, u, a * 128:(a + 1) * 128], ident[0:P, 0:P])
                    mm.then_inc(tset, 1)

                def multiply(i, u):
                    n = i * U + u
                    pe.wait_ge(tcopied, n + 1)
                    if u >= 3 or not isinstance(i, int):
                        pe.wait_ge(evac, n - 2 if u >= 3 else n - 1)
                    for lo in range(0, width, 512):
                        hi = min(width, lo + 512)
                        for a in range(2):
                            mm = pe.matmul(ps_o[u % 3][0:P, lo:hi], ht[:, u, a, :], weight[:, a, lo:hi], start=(a == 0), stop=(a == 1))
                    mm.then_inc(mmdone, 1)

                def body(i):
                    for u in range(U):
                        turn(i, u)
                        if u:
                            multiply(i, u - 1)
                    multiply(i, U - 1)
                peeled(pe, NT // U, body)

            if stores:
                @block.sync
                def _(sp):
                    def body(i):
                        for u in range(U):
                            n = i * U + u
                            sp.wait_ge(evac, n + 1)
                            for table, lo, hi in tables:
                                sp.dma_start(table[bass.ds(n * P, P), :], stage[:, u, lo:hi]).then_inc(stored[u], 16)
                    peeled(sp, NT // U, body)
                    for u in range(U):
                        sp.wait_ge(stored[u], 16 * stores * (NT // U))


def score_phase(nc, con, g, layer, alpha, selfs, by_src, by_dst, attr_t, we):
    first = layer == 1
    width = D if first else 2 * H
    ewidth = D if first else H
    edges = layer != 2
    with phase(nc) as ph:
        sb = lambda n, s, d=F32: ph.enter_context(nc.sbuf_tensor(f"s{layer}_{n}", s, d))
        sem = lambda n: ph.sem(f"s{layer}_{n}")
        istage = sb("istage", [P, 2, 2, G], I32)
        rows = sb("rows", [P, 2, 2, G, width])
        attr = sb("attr", [ED, 2, G * P])
        ps_e = [ph.enter_context(nc.psum_tensor(f"s{layer}_pse{b}", [128, 1024], F32)) for b in range(2)]
        staged, = (sem("staged"),)
        gathered, used, attrset, eset, dv = ([sem(f"{n}{b}") for b in range(2)] for n in ("gathered", "used", "attrset", "eset", "dve"))

        with nc.Block() as block:
            @block.gpsimd
            def _(pool):
                def body(i):
                    for b in range(2):
                        if not isinstance(i, int):
                            pool_wait(pool, used[b], i)
                        at = (i * 2 + b) * G
                        pool.tensor_copy(istage[:, b, 0], g["srci"][:, bass.ds(at, G)]).then_inc(staged, 1)
                        pool.tensor_copy(istage[:, b, 1], g["dsti"][:, bass.ds(at, G)]).then_inc(staged, 1)
                        pool_wait(pool, staged, i * 4 + b * 2 + 2)
                        for u in range(G):
                            for a, table in enumerate((by_src, by_dst)):
                                pool.indirect_dma_start(out=rows[:, b, a, u, :], out_offset=None, in_=table,
                                                        in_offset=bass.IndirectOffsetOnAxis(ap=istage[:, b, a, u:u + 1], axis=0)
                                                        ).then_inc(gathered[b], 16)
                peeled(pool, ET // (2 * G), body)

            if edges:
                @block.sync
                def _(sp):
                    def body(i):
                        for b in range(2):
                            if not isinstance(i, int):
                                sp.wait_ge(eset[b], i)
                            sp.dma_start(attr[:, b, :], attr_t[:, bass.ds((i * 2 + b) * G * P, G * P)]).then_inc(attrset[b], 16)
                    peeled(sp, ET // (2 * G), body)

                @block.tensor
                def _(pe):
                    def body(i):
                        for b in range(2):
                            pe.wait_ge(attrset[b], 16 * i + 16)
                            if not isinstance(i, int):
                                pe.wait_ge(used[b], i)
                            for u in range(G):
                                mm = pe.matmul(ps_e[b][0:P, u * ewidth:(u + 1) * ewidth], attr[:, b, u * P:(u + 1) * P], we,
                                               start=True, stop=True)
                            mm.then_inc(eset[b], 1)
                    peeled(pe, ET // (2 * G), body)

            @block.vector
            def _(dve):
                def body(i):
                    for b in range(2):
                        s, t = rows[:, b, 0], rows[:, b, 1]
                        at = (i * 2 + b) * G
                        out = alpha[:, bass.ds(at, G), :]
                        dve.wait_ge(gathered[b], 128 * i + 128)
                        if edges:
                            dve.wait_ge(eset[b], i + 1)
                            e = ps_e[b][0:P, 0:G * ewidth].rearrange("p (u d) -> p u d", u=G)
                        if first:
                            dve.tensor_tensor(s, s, e, ALU.add).then_inc(dv[b], 1)
                            dve.wait_ge(dv[b], 2 * i + 1)
                            dve.tensor_tensor(s, s, t, ALU.mult).then_inc(dv[b], 1)
                            dve.wait_ge(dv[b], 2 * i + 2)
                            dve.tensor_reduce(out, s.rearrange("p u (h c) -> p u h c", h=H), AX.X, ALU.add).then_inc(used[b], 1)
                        else:
                            add = s[:, :, 0:H]
                            if layer == 3:
                                dve.tensor_tensor(s[:, :, 0:H], s[:, :, 0:H], e, ALU.add).then_inc(dv[b], 1)
                            else:
                                dve.tensor_tensor(selfs[:, bass.ds(at, G), :], t[:, :, 0:H], t[:, :, H:], ALU.add).then_inc(dv[b], 1)
                            dve.wait_ge(dv[b], i + 1)
                            dve.tensor_tensor(out, add, t[:, :, H:], ALU.add).then_inc(used[b], 1)
                peeled(dve, ET // (2 * G), body)


def softmax_phase(nc, con, g, layer, alpha, selfs):
    with_self = layer == 2
    with phase(nc) as ph:
        sb = lambda n, s, d=F32: ph.enter_context(nc.sbuf_tensor(f"m{layer}_{n}", s, d))
        sem = lambda n: ph.sem(f"m{layer}_{n}")
        ident = con["ident"]
        at = sb("at", [128, CE])
        run_w, back_w = (sb(n, [128, ET * H]) for n in ("run", "back"))
        run, back = run_w[:, 0:CE], back_w[:, 0:CE]
        own = sb("own", [128, CE]) if with_self else None
        row, carry, shift, init = sb("row", [1, 128]), sb("carry", [1, 128]), sb("shift", [1, 128]), sb("init", [128, 1])
        ps = [ph.enter_context(nc.psum_tensor(f"m{layer}_ps{b}", [128, 512], F32)) for b in range(4)]
        ps_r = ph.enter_context(nc.psum_tensor(f"m{layer}_psr", [128, 512], F32))
        ps_c = ph.enter_context(nc.psum_tensor(f"m{layer}_psc", [128, 512], F32))
        dv, turned, copied, ended, rowed, shifted, colled, shiftd, powered, weighed, back_t, back_c = (
            sem(n) for n in ("dve", "turned", "copied", "ended", "rowed", "shifted", "colled", "shiftd", "powered", "weighed",
                             "back_t", "back_c"))
        arrays = [(alpha, at, back_w)] + ([(selfs, own, run_w)] if with_self else [])
        by_step = lambda x: x[0:P, :].rearrange("p (s m) -> p s m", s=CT)
        groups = [(a, s0, min(4, CT - s0)) for a in range(len(arrays)) for s0 in range(0, CT, 4)]
        scale = 1.0 / math.sqrt(C) if layer == 1 else 1.0
        chains = 4
        regrouped = sem("regrouped")

        with nc.Block() as block:
            @block.tensor
            def _(pe):
                pe.wait_ge(regrouped, len(arrays))
                for n, (a, s0, k) in enumerate(groups):
                    if n >= 4:
                        pe.wait_ge(copied, n - 3)
                    for j in range(k):
                        mm = pe.transpose(ps[n % 4][:, j * P:(j + 1) * P], by_step(arrays[a][2])[:, s0 + j], ident[0:P, 0:P])
                    mm.then_inc(turned, 1)
                for n in range(chains):
                    pe.wait_ge(ended, n + 1)
                    v = (run[:, CE - 1:CE] if n % 2 == 0 else back[:, 0:1])
                    pe.transpose(ps_r[0:1, 0:128], v, ident[:]).then_inc(rowed, 1)
                    pe.wait_ge(shifted, n + 1)
                    pe.transpose(ps_c[:, 0:1], shift[:], ident[0:1, 0:1]).then_inc(colled, 1)
                pe.wait_ge(weighed, 1)
                for n, (a, s0, k) in enumerate(groups):
                    if n >= 4:
                        pe.wait_ge(back_c, n - 3)
                    for j in range(k):
                        mm = pe.transpose(ps[n % 4][0:P, j * 128:(j + 1) * 128], arrays[a][1][:, (s0 + j) * P:(s0 + j + 1) * P], ident[:])
                    mm.then_inc(back_t, 1)

            @block.scalar
            def _(act):
                for n, (a, s0, k) in enumerate(groups):
                    act.wait_ge(turned, n + 1)
                    act.mul(arrays[a][1][:, s0 * P:(s0 + k) * P], ps[n % 4][:, 0:k * P], scale).then_inc(copied, 1)
                act.wait_ge(shiftd, 1)
                act.activation(at[:], at[:], ACT.Exp).then_inc(powered, 1)
                if with_self:
                    act.activation(own[:], own[:], ACT.Exp).then_inc(powered, 1)
                for n, (a, s0, k) in enumerate(groups):
                    act.wait_ge(back_t, n + 1)
                    view = arrays[a][0][:].rearrange("p (c s) h -> p s c h", c=CH)
                    act.copy(view[:, s0:s0 + k], ps[n % 4][0:P, 0:k * 128].rearrange("p (s c h) -> p s c h", s=k, h=H)).then_inc(back_c, 1)

            @block.vector
            def _(dve):
                c = Tally(dve, dv)
                for x, _, by in arrays:
                    dve.tensor_copy(by_step(by).rearrange("p s (c h) -> p s c h", h=H),
                                    x[:].rearrange("p (c s) h -> p s c h", c=CH)).then_inc(regrouped, 1)
                dve.wait_ge(copied, len(groups))
                if layer != 1:
                    for _, x, _ in arrays:
                        c.up(dve.scalar_tensor_tensor(x[:], x[:], 0.2, x[:], ALU.mult, ALU.max))
                    dve.wait_ge(dv, c.n)
                peak = at
                if with_self:
                    c.then(dve.tensor_tensor(back[:], at[:], own[:], ALU.max))
                    peak = back

                def scan(n, out, flags, src, start, op0, op1, flip):
                    o, f, s = (x[:, ::-1] if flip else x[:, :] for x in (out, flags, src))
                    dve.tensor_tensor_scan(o, f, s, start, op0, op1).then_inc(ended, 1)
                    dve.wait_ge(rowed, n + 1)
                    c.then(dve.tensor_copy(row[:].rearrange("a (h c) -> a h c", h=H), ps_r[0:1, 0:128].rearrange("a (c h) -> a h c", h=H)))
                    fl = g["chunk"][:, 1 if flip else (2 if op0 == ALU.mult else 0)]
                    r, y = (row[:, ::-1], carry[:, ::-1]) if flip else (row[:, :], carry[:, :])
                    c.up(dve.tensor_tensor_scan(y, fl[:, ::-1] if flip else fl, r, start, op0, op1))
                    c.then(dve.memset(shift[:], start))
                    y3 = carry[:].rearrange("a (h c) -> a c h", h=H)
                    s3 = shift[:].rearrange("a (c h) -> a c h", h=H)
                    if flip:
                        dve.tensor_copy(s3[:, 0:CH - 1], y3[:, 1:CH]).then_inc(shifted, 1)
                    else:
                        dve.tensor_copy(s3[:, 1:CH], y3[:, 0:CH - 1]).then_inc(shifted, 1)
                    dve.wait_ge(colled, n + 1)
                    c.then(dve.tensor_copy(init[:], ps_c[:, 0:1]))
                    c.then(dve.tensor_tensor_scan(o, f, s, init[:], op0, op1))

                scan(0, run, g["startf"], peak, -BIG, ALU.add, ALU.max, False)
                scan(1, back, g["endf"], run, -BIG, ALU.add, ALU.max, True)
                if with_self:
                    c.up(dve.tensor_tensor(own[:], own[:], back[:], ALU.subtract))
                c.up(dve.tensor_tensor(at[:], at[:], back[:], ALU.subtract))
                dve.wait_ge(dv, c.n)
                dve.sem_inc(shiftd, 1)
                dve.wait_ge(powered, 2 if with_self else 1)
                scan(2, run, g["keep"], at, 0.0, ALU.mult, ALU.add, False)
                scan(3, back, g["endf"], run, -BIG, ALU.add, ALU.max, True)
                if with_self:
                    c.then(dve.tensor_tensor(back[:], back[:], own[:], ALU.add))
                c.then(dve.tensor_scalar(back[:], back[:], 1e-16, None, ALU.add))
                c.then(dve.reciprocal(back[:], back[:]))
                c.up(dve.tensor_tensor(at[:], at[:], back[:], ALU.mult))
                if with_self:
                    c.then(dve.tensor_tensor(own[:], own[:], back[:], ALU.mult))
                    c.up(dve.scalar_tensor_tensor(own[:], g["endf"][:], -1.0 / BIG, own[:], ALU.mult, ALU.mult))
                dve.wait_ge(dv, c.n)
                dve.sem_inc(weighed, 1)


def message_phase(nc, con, g, layer, acc, weights, selfs, table, attr_t, we):
    first, with_self = layer == 1, layer == 2
    mw = D + H + 1 if with_self else D
    with phase(nc) as ph:
        sb = lambda n, s, d=F32: ph.enter_context(nc.sbuf_tensor(f"a{layer}_{n}", s, d))
        sem = lambda n: ph.sem(f"a{layer}_{n}")
        istage = sb("istage", [P, 2, G], I32)
        rows = sb("rows", [P, 2, G, D])
        wst = sb("wst", [P, 2, G, H])
        msg = sb("msg", [P, 2, G, mw])
        hot = sb("hot", [P, 2, G, P])
        attr = sb("attr", [ED, 2, G, P])
        ps_o = [ph.enter_context(nc.psum_tensor(f"a{layer}_pso{u}", [128, 512], F32)) for u in range(G)]
        ps_e = [ph.enter_context(nc.psum_tensor(f"a{layer}_pse{b}", [128, 1024], F32)) for b in range(2)]
        staged, edone, setup = sem("staged"), sem("edone"), sem("setup")
        gathered, used, wset, aset, eset, hset, mset, summed, added = (
            [sem(f"{n}{b}") for b in range(2)] for n in ("gathered", "used", "wset", "aset", "eset", "hset", "mset", "summed", "added"))
        ROUNDS = STEPS // (2 * G)
        WD = 2 if with_self else 1

        def tiles(eng, at):
            word = eng.value_load(g["tword"][0:1, bass.ds(at, 1)], min_val=0, max_val=32 ** 4 - 1)
            return [nc.s_assert_within(eng.snap((word >> (5 * u)) & 31), 0, NT - 1,
                                       skip_runtime_bounds_check_because="a count of NT - 1 borders") for u in range(G)]

        with nc.Block() as block:
            @block.gpsimd
            def _(pool):
                def body(i):
                    for b in range(2):
                        if not isinstance(i, int):
                            pool_wait(pool, used[b], i)
                        pool.tensor_copy(istage[:, b], g["srcs"][:, bass.ds((i * 2 + b) * G, G)]).then_inc(staged, 1)
                        pool_wait(pool, staged, i * 2 + b + 1)
                        for u in range(G):
                            pool.indirect_dma_start(out=rows[:, b, u, :], out_offset=None, in_=table,
                                                    in_offset=bass.IndirectOffsetOnAxis(ap=istage[:, b, u:u + 1], axis=0)
                                                    ).then_inc(gathered[b], 16)
                peeled(pool, ROUNDS, body)

            @block.sync
            def _(sp):
                def body(i):
                    for b in range(2):
                        at = i * 2 + b
                        ts = tiles(sp, at)
                        if not isinstance(i, int):
                            sp.wait_ge(used[b], i)
                            if with_self:
                                sp.wait_ge(summed[b], i)
                            if first:
                                sp.wait_ge(eset[b], i)
                        elif with_self:
                            sp.wait_ge(setup, 1)
                        sp.nop(nofuse=True)
                        for u in range(G):
                            k = nc.s_assert_within(sp.snap(at * G + u - ts[u]), 0, ET - 1,
                                                   skip_runtime_bounds_check_because="the staircase stays inside the edge tiles")
                            sp.dma_start(wst[:, b, u, :], weights[:, bass.ds(k, 1), :].rearrange("p a h -> p (a h)")).then_inc(wset[b], 16)
                            if with_self:
                                sp.dma_start(msg[:, b, u, D:D + H], selfs[:, bass.ds(k, 1), :].rearrange("p a h -> p (a h)")).then_inc(wset[b], 16)
                            if first:
                                sp.dma_start(attr[:, b, u, :], attr_t[:, bass.ds(k * P, P)]).then_inc(aset[b], 16)
                peeled(sp, ROUNDS, body)

            @block.vector
            def _(dve):
                def message(i, b):
                    at = (i * 2 + b) * G
                    if not isinstance(i, int):
                        dve.wait_ge(summed[b], i)
                    where = g["dstl"][:, bass.ds(at, G)]
                    dve.tensor_tensor(hot[:, b], con["iota"][0:P, 0:P].unsqueeze(1).to_broadcast([P, G, P]),
                                      where.unsqueeze(2).to_broadcast([P, G, P]), ALU.is_equal).then_inc(hset[b], 1)
                    dve.wait_ge(gathered[b], 64 * i + 64)
                    v = rows[:, b]
                    if first:
                        dve.wait_ge(eset[b], i + 1)
                        dve.tensor_tensor(v, v, ps_e[b][0:P, :].rearrange("p (u d) -> p u d", u=G), ALU.add).then_inc(edone, 1)
                        dve.wait_ge(edone, 2 * i + b + 1)
                    dve.wait_ge(wset[b], 64 * WD * (i + 1))
                    dve.tensor_tensor(msg[:, b, :, 0:D].rearrange("p u (h c) -> p u h c", h=H), v.rearrange("p u (h c) -> p u h c", h=H),
                                      wst[:, b].unsqueeze(3).to_broadcast([P, G, H, C]), ALU.mult).then_inc(used[b], 1)

                def add(i, b, n):
                    ts = tiles(dve, i * 2 + b)
                    dve.wait_ge(summed[b], n)
                    for u in range(G):
                        row = acc[:, bass.ds(ts[u], 1), 0:mw].rearrange("p a d -> p (a d)")
                        dve.tensor_tensor(row, row, ps_o[u][0:P, 0:mw], ALU.add).then_inc(added[b], 1)
                        dve.wait_ge(added[b], 4 * n - 3 + u)

                def body(i):
                    message(i, 0)
                    if not isinstance(i, int):
                        add(i - 1, 1, i)
                    message(i, 1)
                    add(i, 0, i + 1)
                if with_self:
                    for u in range(2):
                        ins = dve.memset(msg[:, u, :, D + H:], 1.0)
                    ins.then_inc(setup, 1)
                    dve.wait_ge(setup, 1)
                peeled(dve, ROUNDS, body)
                add(ROUNDS - 1, 1, ROUNDS)

            @block.tensor
            def _(pe):
                def edges(i, b):
                    pe.wait_ge(aset[b], 64 * i + 64)
                    if not isinstance(i, int):
                        pe.wait_ge(used[b], i)
                    for u in range(G):
                        mm = pe.matmul(ps_e[b][0:P, u * D:(u + 1) * D], attr[:, b, u, :], we, start=True, stop=True)
                    mm.then_inc(eset[b], 1)

                def body(i):
                    for b in range(2):
                        if first:
                            edges(i, b)
                        pe.wait_ge(hset[b], i + 1)
                        pe.wait_ge(used[b], i + 1)
                        if b:
                            pe.wait_ge(added[0], 4 * i + 4)
                        elif not isinstance(i, int):
                            pe.wait_ge(added[1], 4 * i)
                        for u in range(G):
                            mm = pe.matmul(ps_o[u][0:P, 0:mw], hot[:, b, u, :], msg[:, b, u, :], start=True, stop=True)
                        mm.then_inc(summed[b], 1)
                peeled(pe, ROUNDS, body)


def attention_end_phase(nc, con, X, acc, table, bias):
    U = 5
    with phase(nc) as ph:
        sb = lambda n, s, d=F32: ph.enter_context(nc.sbuf_tensor(f"e_{n}", s, d))
        sem = lambda n: ph.sem(f"e_{n}")
        h2, neg = sb("h2", [P, U, D]), sb("neg", [P, U, D])
        ws = sb("ws", [P, NT, H])
        alone = sb("alone", [P, NT])
        dv, loaded, low, powered, done = (sem(n) for n in ("dve", "loaded", "low", "powered", "done"))
        lo = [sem(f"loaded{u}") for u in range(U)]
        with nc.Block() as block:
            @block.sync
            def _(sp):
                def body(i):
                    for u in range(U):
                        n = i * U + u
                        if not isinstance(i, int):
                            sp.wait_ge(done, n - U + 1)
                        sp.dma_start(h2[:, u, :], table[bass.ds(n * P, P), :]).then_inc(lo[u], 16)
                peeled(sp, NT // U, body)

            @block.scalar
            def _(act):
                def body(i):
                    for u in range(U):
                        act.wait_ge(low, i * U + u + 1)
                        act.activation(neg[:, u, :], neg[:, u, :], ACT.Exp).then_inc(powered, 1)
                peeled(act, NT // U, body)

            @block.vector
            def _(dve):
                c = Tally(dve, dv)
                c.then(dve.tensor_scalar(alone[:], acc[:, :, D + H], 0.5, None, ALU.is_lt))
                c.then(dve.tensor_tensor(ws[:], acc[:, :, D:D + H], alone[:].unsqueeze(2).to_broadcast([P, NT, H]), ALU.add))
                start = c.n
                PER = 3 * U

                def body(i):
                    c = Tally(dve, dv, i * PER + start)
                    for u in range(U):
                        n = i * U + u
                        z = acc[:, bass.ds(n, 1), 0:D].rearrange("p a d -> p (a d)")
                        m = h2[:, u, :]
                        dve.wait_ge(lo[u], 16 * i + 16)
                        c.then(dve.tensor_tensor(m.rearrange("p (h c) -> p h c", h=H), m.rearrange("p (h c) -> p h c", h=H),
                                                 ws[:, bass.ds(n, 1), :].rearrange("p a h -> p (a h)").unsqueeze(2).to_broadcast([P, H, C]), ALU.mult))
                        c.then(dve.tensor_tensor(m, m, bias[:], ALU.add))
                        c.then(dve.tensor_tensor(z, z, m, ALU.add))
                        if not isinstance(i, int):
                            dve.wait_ge(done, n - U + 1)
                        dve.tensor_scalar(neg[:, u, :], z, 0.0, None, ALU.min).then_inc(low, 1)
                    for u in range(U):
                        n = i * U + u
                        z = acc[:, bass.ds(n, 1), 0:D].rearrange("p a d -> p (a d)")
                        x = X[:, bass.ds(n, 1), :].rearrange("p a d -> p (a d)")
                        dve.wait_ge(powered, n + 1)
                        dve.scalar_tensor_tensor(z, z, 0.0, neg[:, u, :], ALU.max, ALU.add).then_inc(low2[u], 1)
                        dve.wait_ge(low2[u], i + 1)
                        dve.scalar_tensor_tensor(x, z, -1.0, x, ALU.add, ALU.add).then_inc(done, 1)
                low2 = [ph.sem(f"e_sum{u}") for u in range(U)]
                peeled(dve, NT // U, body)


def final_phase(nc, con, X, acc, gamma, beta, out):
    U = 5
    with phase(nc) as ph:
        sb = lambda n, s, d=F32: ph.enter_context(nc.sbuf_tensor(f"f_{n}", s, d))
        sem = lambda n: ph.sem(f"f_{n}")
        st = sb("st", [P, NT, 6])
        mean, dif, var, rstd, nb = (sb(n, [P, NT]) for n in ("mean", "dif", "var", "rstd", "nb"))
        y = sb("y", [P, U, D])
        dv, spread, rooted, ready, normed, done = (sem(n) for n in ("dve", "spread", "rooted", "ready", "normed", "done"))
        stored = [sem(f"stored{u}") for u in range(U)]
        with nc.Block() as block:
            @block.vector
            def _(dve):
                with dve.Fori(0, NT) as n:
                    dve.bn_stats(st[:, bass.ds(n, 1), :].rearrange("p a s -> p (a s)"),
                                 acc[:, bass.ds(n, 1), 0:D].rearrange("p a d -> p (a d)")).then_inc(dv, 1)
                dve.wait_ge(dv, NT)
                c = Tally(dve, dv, NT)
                me, mo = st[:, :, 1], st[:, :, 4]
                c.up(dve.tensor_tensor(mean[:], me, mo, ALU.add))
                c.up(dve.tensor_tensor(dif[:], me, mo, ALU.subtract))
                c.then(dve.tensor_tensor(var[:], st[:, :, 2], st[:, :, 5], ALU.add))
                c.up(dve.tensor_scalar(mean[:], mean[:], 0.5, None, ALU.mult))
                c.then(dve.scalar_tensor_tensor(dif[:], dif[:], 0.25, dif[:], ALU.mult, ALU.mult))
                c.then(dve.scalar_tensor_tensor(var[:], var[:], 1.0 / D, dif[:], ALU.mult, ALU.add))
                dve.tensor_scalar(var[:], var[:], EPS, None, ALU.add).then_inc(spread, 1)
                dve.wait_ge(rooted, 1)
                c.then(dve.reciprocal(rstd[:], dif[:]))
                dve.scalar_tensor_tensor(nb[:], mean[:], -1.0, rstd[:], ALU.mult, ALU.mult).then_inc(ready, 1)
                start = NT + c.n

                def body(i):
                    c = Tally(dve, dv, i * 2 * U + start)
                    for u in range(U):
                        n = i * U + u
                        dve.wait_ge(normed, n + 1)
                        c.then(dve.tensor_tensor(y[:, u, :], y[:, u, :], gamma[:], ALU.mult))
                        c.then(dve.tensor_tensor(y[:, u, :], y[:, u, :], beta[:], ALU.add))
                        dve.tensor_tensor(y[:, u, :], y[:, u, :], X[:, bass.ds(n, 1), :].rearrange("p a d -> p (a d)"), ALU.add).then_inc(done, 1)
                peeled(dve, NT // U, body)

            @block.scalar
            def _(act):
                act.wait_ge(spread, 1)
                act.activation(dif[:], var[:], ACT.Sqrt).then_inc(rooted, 1)
                act.wait_ge(ready, 1)

                def body(i):
                    for u in range(U):
                        n = i * U + u
                        if not isinstance(i, int):
                            act.wait_ge(stored[u], 16 * i)
                        act.activation(y[:, u, :], acc[:, bass.ds(n, 1), 0:D].rearrange("p a d -> p (a d)"), ACT.Identity,
                                       bias=nb[:, bass.ds(n, 1)], scale=rstd[:, bass.ds(n, 1)]).then_inc(normed, 1)
                peeled(act, NT // U, body)

            @block.sync
            def _(sp):
                def body(i):
                    for u in range(U):
                        n = i * U + u
                        sp.wait_ge(done, n + 1)
                        sp.dma_start(out[bass.ds(n * P, P), :], y[:, u, :]).then_inc(stored[u], 16)
                peeled(sp, NT // U, body)
                for u in range(U):
                    sp.wait_ge(stored[u], 16 * (NT // U))


def weights_phase(nc, con, a, w):
    with phase(nc) as ph:
        sb = lambda n, s, d=F32: ph.enter_context(nc.sbuf_tensor(f"w_{n}", s, d))
        att = {n: sb(n, [128, D]) for n in ("l2s", "l2d", "l3s", "l3d", "l3e")}
        wedge = sb("wedge", [ED, D])
        prod = sb("prod", [128, 9, D])
        loaded, folded = ph.sem("w_loaded"), ph.sem("w_folded")
        with nc.Block() as block:
            @block.sync
            def _(sp):
                rows = lambda x: x.rearrange("(a p) n -> p a n", p=128)
                loads = [(w["l1"][:], rows(a["w1"])), (w["l2"][:, :, 0:D], rows(a["w2"])), (w["l3"][:, :, 0:D], rows(a["w3"])),
                         (w["we1"][:], a["we1"]), (wedge[:], a["we3"]), (w["x"][:], a["x"].rearrange("(n p) d -> p n d", p=P))]
                for k in ("b1", "b2", "b3", "gamma", "beta"):
                    loads.append((w[k][:], a[k].to_broadcast([P, a[k].shape[1]])))
                for k in att:
                    loads.append((att[k][:], a[k].to_broadcast([128, D])))
                for dst, src in loads:
                    sp.dma_start(dst, src).then_inc(loaded, 16)
                con["loads"] = len(loads)

            @block.vector
            def _(dve):
                dve.wait_ge(loaded, 16 * con["loads"])
                jobs = []
                for name, s, d in (("l2", "l2s", "l2d"), ("l3", "l3s", "l3d")):
                    for half in range(2):
                        for j, v in enumerate((s, d)):
                            jobs.append((w[name][:, half, 0:D], att[v][:], w[name][:, half, D + j * H:D + (j + 1) * H], 128))
                jobs.append((wedge[:], att["l3e"][0:ED, :], w["we3"][:], ED))
                for n, (x, v, o, p) in enumerate(jobs):
                    dve.tensor_tensor(prod[0:p, n, :], x, v, ALU.mult).then_inc(folded, 1)
                dve.wait_ge(folded, len(jobs))
                for n, (x, v, o, p) in enumerate(jobs):
                    dve.tensor_reduce(o, prod[0:p, n, :].rearrange("p (h c) -> p h c", h=H), AX.X, ALU.add).then_inc(folded, 1)


def zero_phase(nc, acc, name):
    with phase(nc) as ph:
        z = ph.sem(name)
        with nc.Block() as block:
            @block.vector
            def _(dve):
                dve.memset(acc[:], 0.0).then_inc(z, 1)


def program(nc, a, out):
    with ExitStack() as ctx:
        sb = lambda n, s, d=F32: ctx.enter_context(nc.sbuf_tensor(n, s, d))
        dram = lambda n, r, c: nc.dram_tensor(n, (r, c), F32, kind="Internal").ap()
        con = {k: sb("con_" + k, [128, n]) for k, n in
               (("ident", 128), ("iota", 256), ("iota1", 128), ("after", 128), ("ones", 128), ("part", 2))}
        con["iterations"] = sb("con_iterations", [1, 1], I32)
        w = {"l1": sb("wt1", [128, 2, 4 * D]), "l2": sb("wt2", [128, 2, D + 2 * H]), "l3": sb("wt3", [128, 2, D + 2 * H]),
             "we1": sb("we1", [ED, D]), "we3": sb("we3", [ED, H]), "x": sb("x", [P, NT, D])}
        for k, n in (("b1", 4 * D), ("b2", D), ("b3", D), ("gamma", D), ("beta", D)):
            w[k] = sb("row_" + k, [P, n])
        MT = sb("MT", [128, 2, ROT])
        X = w["x"]
        rlist = dram("rotation_list", (LIST_BLOCKS + 1) * SLOT, FIELDS)
        constants_phase(nc, con)
        weights_phase(nc, con, a, w)
        rotation_list_phase(nc, con, a["w_e"], a["src_e"], a["dst_e"], rlist)
        rotation_phase(nc, con, rlist, MT)
        dense_phase(nc, con, None, 0, X, None, MT, ROT, None, [])

        acc = sb("acc", [P, NT, AW])
        g = {"srci": sb("g_src", [P, ET], I32), "dsti": sb("g_dst", [P, ET], I32), "srcs": sb("g_srcs", [P, STEPS], I32),
             "dstl": sb("g_dstl", [P, STEPS]), "tword": sb("g_tword", [1, STEPS // 4], I32),
             "startf": sb("g_start", [128, CE]), "endf": sb("g_end", [128, CE]), "keep": sb("g_keep", [128, CE]),
             "chunk": sb("g_chunk", [1, 3, 128]), "src_e": a["src_e"]}
        rows2 = lambda x: x.rearrange("(k p) -> k p", p=P)
        graph_phase(nc, con, g, rows2(a["src"]), rows2(a["dst"]), a["dst_e"], a["dst"])
        alpha, selfs = sb("alpha", [P, ET, H]), sb("selfs", [P, ET, H])

        tq, tk, tv = (dram(n, N, D) for n in ("table_q", "table_k", "table_v"))
        dense_phase(nc, con, g, 1, X, None, w["l1"], 4 * D, w["b1"], [(tq, 0, D), (tk, D, 2 * D), (tv, 2 * D, 3 * D)])
        score_phase(nc, con, g, 1, alpha, None, tk, tq, a["attr_t"], w["we1"][:])
        softmax_phase(nc, con, g, 1, alpha, None)
        message_phase(nc, con, g, 1, X, alpha, None, tv, a["attr_t"], w["we1"][:])

        t2, a2 = dram("table_h2", N, D), dram("table_a2", N, 2 * H)
        dense_phase(nc, con, g, 2, X, None, w["l2"], D + 2 * H, None, [(t2, 0, D), (a2, D, D + 2 * H)])
        zero_phase(nc, acc, "zero_acc")
        score_phase(nc, con, g, 2, alpha, selfs, a2, a2, None, None)
        softmax_phase(nc, con, g, 2, alpha, selfs)
        message_phase(nc, con, g, 2, acc, alpha, selfs, t2, None, None)
        attention_end_phase(nc, con, X, acc, t2, w["b2"])

        t3, a3 = dram("table_h3", N, D), dram("table_a3", N, 2 * H)
        dense_phase(nc, con, g, 3, X, acc, w["l3"], D + 2 * H, w["b3"], [(t3, 0, D), (a3, D, D + 2 * H)])
        score_phase(nc, con, g, 3, alpha, None, a3, a3, a["attr_t"], w["we3"][:])
        softmax_phase(nc, con, g, 3, alpha, None)
        message_phase(nc, con, g, 3, acc, alpha, None, t3, None, None)
        final_phase(nc, con, X, acc, w["gamma"], w["beta"], out)


def kernel(**inp):
    import concourse.bacc as _bacc
    from concourse.bass_utils import run_bass_kernel_spmd as _run
    nc = _bacc.Bacc("TRN2", target_bir_lowering=False, num_devices=1)
    inp = {k: np.asarray(v) for k, v in inp.items()}
    row = lambda x: x.reshape(1, -1)
    tiles = lambda x: x.reshape(ET, P).T
    host = {
        "x": inp["x"], "src": inp["src"], "dst": inp["dst"],
        "src_e": tiles(inp["src"]), "dst_e": tiles(inp["dst"]), "w_e": tiles(inp["edge_weight"]),
        "attr_t": inp["edge_attr_64"].T,
        "w1": np.concatenate([inp[f"L1_gnn_W{k}"].T for k in ("q", "k", "v", "skip")], axis=1),
        "b1": np.concatenate([row(inp[f"L1_gnn_b{k}"]) for k in ("q", "k", "v", "skip")], axis=1),
        "we1": inp["L1_gnn_We"].T, "w2": inp["L2_gnn_W0"].T, "b2": row(inp["L2_gnn_b0"]),
        "l2s": row(inp["L2_gnn_att_src0"]), "l2d": row(inp["L2_gnn_att_dst0"]),
        "w3": inp["L3_gnn_W"], "we3": inp["L3_gnn_W_e"], "l3s": row(inp["L3_gnn_att_src"]), "l3d": row(inp["L3_gnn_att_dst"]),
        "l3e": row(inp["L3_gnn_att_edge"]), "b3": row(inp["L3_gnn_bias"]), "gamma": row(inp["L3_gnn_gamma"]),
        "beta": row(inp["L3_gnn_beta"]),
    }
    arrays, args = {}, {}
    for n, x in host.items():
        x = np.ascontiguousarray(x)
        arrays[f"in_{n}"] = x
        args[n] = nc.dram_tensor(f"in_{n}", x.shape, mybir.dt.from_np(x.dtype), kind="ExternalInput").ap()
    out = nc.dram_tensor("out_0", (N, D), F32, kind="ExternalOutput").ap()
    program(nc, args, out)
    r = _run(nc, [arrays], core_ids=[0])
    return r.results[0]["out_0"]
```

```python
from contextlib import ExitStack, contextmanager
import math

import numpy as np
import concourse.bass as bass
from concourse import mybir

F32 = mybir.dt.float32
I32 = mybir.dt.int32
ALU = mybir.AluOpType
ACT = mybir.ActivationFunctionType
AX = mybir.AxisListType

P = 125
N = 3125
NT = N // P
E = 50000
ET = E // P
D = 256
ED = 64
H = 8
C = D // H
ROT = 256

SLOT = 128
FILL = SLOT - 1
LIST_BLOCKS = -(-(2 * E // FILL + 10) // 8) * 8
FIELDS = 8
R1, R2, ALPHA, BETA, WR, EVENT, SIN, COS = range(FIELDS)
SKIP = float(1 << 20)
UB = 2
LEVELS = 7
TWO_PI_HI = 6.28125
TWO_PI_LO = 2 * math.pi - TWO_PI_HI
PI = 3.1415925


class Tally:

    def __init__(self, eng, sem, base=0):
        self.eng, self.sem, self.base, self.n = eng, sem, base, 0

    def up(self, ins):
        ins.then_inc(self.sem, 1)
        self.n += 1

    def then(self, ins):
        self.up(ins)
        self.eng.wait_ge(self.sem, self.base + self.n)


@contextmanager
def phase(nc):
    with ExitStack() as ph:
        taken = []

        def take(name):
            taken.append(nc.alloc_semaphore(name))
            return taken[-1]
        ph.sem = take
        yield ph
        nc.clear_and_free_semaphores(taken)
        nc.all_engine_barrier()


def peeled(eng, count, body):
    body(0)
    with eng.Fori(1, count) as i:
        body(i)


def opening(i):
    return isinstance(i, int) and i == 0


def pool_wait(pool, sem, value):
    pool.wait_ge(sem, value)
    pool.nop(nofuse=True)


def constants_phase(nc, con):
    with phase(nc) as ph:
        ii = ph.enter_context(nc.sbuf_tensor("c_iota_i", [128, 256], I32))
        pi = ph.enter_context(nc.sbuf_tensor("c_part_i", [128, 1], I32))
        made = ph.sem("c_made")
        dv = ph.sem("c_dve")
        with nc.Block() as block:
            @block.gpsimd
            def _(pool):
                pool.iota(ii[:], [[1, 256]], base=0, channel_multiplier=0).then_inc(made, 1)
                pool.iota(pi[:], [[1, 1]], base=0, channel_multiplier=1).then_inc(made, 1)

            @block.vector
            def _(dve):
                c = Tally(dve, dv)
                c.up(dve.memset(con["ones"][:], 1.0))
                dve.wait_ge(made, 2)
                c.up(dve.tensor_copy(con["iota"][:], ii[:]))
                c.then(dve.tensor_copy(con["part"][:, 0:1], pi[:]))
                c.up(dve.tensor_scalar(con["part"][:, 1:2], con["part"][:, 0:1], 128.0, None, ALU.add))
                c.up(dve.tensor_scalar(con["iota1"][:], con["iota"][:, 0:128], 1.0, None, ALU.add))
                c.up(dve.tensor_scalar(con["ident"][:], con["iota"][:, 0:128], con["part"][:, 0:1], None, ALU.is_equal))
                c.then(dve.tensor_scalar(con["after"][:], con["iota"][:, 0:128], con["part"][:, 0:1], None, ALU.is_gt))


def rotation_list_phase(nc, con, w_e, src_e, dst_e, rlist):
    with phase(nc) as ph:
        sb = lambda n, s, d=F32: ph.enter_context(nc.sbuf_tensor(n, s, d))
        sem = lambda n: ph.sem(n)
        ident, after, ones = con["ident"], con["after"], con["ones"]
        srcf, dstf, w = sb("l0_src", [P, ET]), sb("l0_dst", [P, ET]), sb("l0_w", [P, ET])
        srci, dsti = sb("l0_srci", [P, ET], I32), sb("l0_dsti", [P, ET], I32)
        ti = sb("l0_ti", [P, ET], I32)
        ta, tb, tc, act_, ev, ver, rolei = (sb(f"l0_{n}", [P, ET]) for n in ("ta", "tb", "tc", "active", "event", "ver", "rolei"))
        pos = sb("l0_pos", [P, ET], I32)
        pay = sb("l0_pay", [P, ET, FIELDS])
        pad = sb("l0_pad", [128, LIST_BLOCKS + 1, FIELDS])
        off, col, cnt = sb("l0_off", [1, ET]), sb("l0_col", [1, ET]), sb("l0_cnt", [1, 2])
        pstage = sb("l0_pstage", [P, 2, 4, FIELDS])
        istage = sb("l0_istage", [P, 2, 4], I32)
        psq = ph.enter_context(nc.psum_tensor("l0_psq", [128, 512], F32))
        psc = ph.enter_context(nc.psum_tensor("l0_psc", [128, 512], F32))
        (loaded, padset, filled, dv, angles, waves, versions, offsets, counted, placed, payset, staged) = (
            sem(f"l0_{n}") for n in ("loaded", "padset", "filled", "dve", "angles", "waves", "versions", "offsets",
                                     "counted", "placed", "payset", "staged"))
        scattered = [sem(f"l0_scattered{g}") for g in range(2)]

        with nc.Block() as block:
            @block.sync
            def _(sp):
                sp.dma_start(srci[:], src_e).then_inc(loaded, 16)
                sp.dma_start(dsti[:], dst_e).then_inc(loaded, 16)
                sp.dma_start(w[:], w_e).then_inc(loaded, 16)
                sp.wait_ge(padset, 2)
                sp.dma_start(rlist.rearrange("(p n) f -> p (n f)", p=128),
                             pad[:].rearrange("p n f -> p (n f)")).then_inc(filled, 16)

            @block.scalar
            def _(act):
                act.wait_ge(angles, 2)
                act.activation(pay[:, :, SIN], tb[:], ACT.Sin).then_inc(waves, 1)
                act.activation(pay[:, :, COS], tc[:], ACT.Sin).then_inc(waves, 1)

            @block.tensor
            def _(pe):
                pe.wait_ge(versions, 1)
                pe.matmul(psc[0:1, 0:ET], ones[0:P, 0:1], ver[:], start=True, stop=True).then_inc(counted, 1)
                pe.matmul(psq[0:P, 0:ET], after[0:P, 0:P], ver[:], start=True, stop=False)
                pe.wait_ge(offsets, 1)
                pe.matmul(psq[0:P, 0:ET], ones[0:1, 0:P], off[:], start=False, stop=True).then_inc(counted, 1)

            @block.vector
            def _(dve):
                c = Tally(dve, dv)
                dve.wait_ge(loaded, 48)
                c.up(dve.tensor_copy(srcf[:], srci[:]))
                c.then(dve.tensor_copy(dstf[:], dsti[:]))
                c.then(dve.tensor_tensor(ta[:], srcf[:], dstf[:], ALU.min))
                c.then(dve.tensor_scalar(act_[:], ta[:], float(ROT), None, ALU.is_lt))
                c.then(dve.tensor_tensor(ta[:], srcf[:], dstf[:], ALU.not_equal))
                c.then(dve.scalar_tensor_tensor(rolei[:], srcf[:], float(ROT), ta[:], ALU.is_lt, ALU.mult))
                c.then(dve.scalar_tensor_tensor(ev[:], dstf[:], float(ROT), rolei[:], ALU.is_lt, ALU.mult))
                c.up(dve.tensor_copy(pay[:, :, EVENT], ev[:]))
                dve.tensor_tensor(ver[:], act_[:], ev[:], ALU.add).then_inc(versions, 1)
                dve.wait_ge(counted, 1)
                c.then(dve.tensor_copy(col[:], psc[0:1, 0:ET]))
                c.then(dve.memset(ta[0:1, :], 1.0))
                c.then(dve.tensor_tensor_scan(off[:], ta[0:1, :], col[:], 0.0, ALU.mult, ALU.add))
                c.then(dve.tensor_copy(cnt[:, 0:1], off[:, ET - 1:ET]))
                dve.tensor_tensor(off[:], off[:], col[:], ALU.subtract).then_inc(offsets, 1)
                c.then(dve.tensor_scalar(cnt[:, 1:2], cnt[:, 0:1], 1.0 / (FILL * UB), 2.6, ALU.mult, ALU.add))
                c.up(dve.tensor_copy(con["iterations"][:], cnt[:, 1:2]))
                c.then(dve.tensor_scalar(ti[:], w[:], 1 / (2 * math.pi), None, ALU.mult))
                c.then(dve.tensor_copy(ta[:], ti[:]))
                c.then(dve.scalar_tensor_tensor(tb[:], ta[:], -TWO_PI_HI, w[:], ALU.mult, ALU.add))
                c.then(dve.scalar_tensor_tensor(tb[:], ta[:], -TWO_PI_LO, tb[:], ALU.mult, ALU.add))

                def wrap(x, bound, sign):
                    c.then(dve.tensor_scalar(ta[:], x, sign * PI, -sign * 2 * math.pi,
                                             ALU.is_gt if sign > 0 else ALU.is_lt, ALU.mult))
                    c.then(dve.tensor_tensor(x, x, ta[:], ALU.add))
                wrap(tb[:], PI, 1)
                wrap(tb[:], PI, -1)
                c.then(dve.tensor_scalar(tc[:], tb[:], math.pi / 2, None, ALU.add))
                wrap(tc[:], PI, 1)
                dve.tensor_scalar(tb[:], tb[:], PI, -PI, ALU.min, ALU.max).then_inc(angles, 1)
                dve.tensor_scalar(tc[:], tc[:], PI, -PI, ALU.min, ALU.max).then_inc(angles, 1)
                dve.wait_ge(counted, 2)
                c.then(dve.tensor_copy(ver[:], psq[0:P, 0:ET]))
                c.then(dve.tensor_scalar(ti[:], ver[:], 1.0 / FILL, None, ALU.mult))
                c.then(dve.tensor_copy(ta[:], ti[:]))
                c.then(dve.scalar_tensor_tensor(w[:], ta[:], float(FILL), ver[:], ALU.mult, ALU.is_gt))
                c.then(dve.tensor_tensor(ta[:], ta[:], w[:], ALU.subtract))
                c.then(dve.tensor_scalar(w[:], ta[:], float(FILL), float(FILL), ALU.mult, ALU.add))
                c.then(dve.tensor_tensor(w[:], w[:], ver[:], ALU.is_le))
                c.then(dve.tensor_tensor(ta[:], ta[:], w[:], ALU.add))
                c.then(dve.scalar_tensor_tensor(ta[:], ta[:], 1.0, ver[:], ALU.add, ALU.add))
                c.then(dve.tensor_scalar(w[:], act_[:], -SKIP, SKIP, ALU.mult, ALU.add))
                c.then(dve.tensor_tensor(ta[:], ta[:], w[:], ALU.add))
                dve.tensor_copy(pos[:], ta[:]).then_inc(placed, 1)
                c.up(dve.tensor_scalar(pay[:, :, R1], srcf[:], float(ROT - 1), None, ALU.min))
                c.then(dve.tensor_scalar(pay[:, :, R2], dstf[:], float(ROT - 1), None, ALU.min))
                c.then(dve.tensor_tensor(ver[:], pay[:, :, R1], pay[:, :, R2], ALU.subtract))
                c.then(dve.tensor_tensor(ver[:], ver[:], rolei[:], ALU.mult))
                c.up(dve.tensor_tensor(pay[:, :, WR], ver[:], pay[:, :, R2], ALU.add))
                c.then(dve.tensor_scalar(w[:], rolei[:], -1.0, 1.0, ALU.mult, ALU.add))
                dve.wait_ge(waves, 2)
                sn, cs = pay[:, :, SIN], pay[:, :, COS]
                c.up(dve.tensor_tensor(tb[:], cs, rolei[:], ALU.mult))
                c.then(dve.tensor_tensor(tc[:], sn, w[:], ALU.mult))
                c.then(dve.tensor_tensor(pay[:, :, ALPHA], tb[:], tc[:], ALU.add))
                c.up(dve.tensor_tensor(tb[:], sn, rolei[:], ALU.mult))
                c.then(dve.tensor_tensor(tc[:], cs, w[:], ALU.mult))
                dve.tensor_tensor(pay[:, :, BETA], tc[:], tb[:], ALU.subtract).then_inc(payset, 1)

            @block.gpsimd
            def _(pool):
                pool.memset(pad[:], 0.0).then_inc(padset, 1)
                pool.wait_ge(padset, 1)
                pool.memset(pad[:, :, WR], -1.0).then_inc(padset, 1)
                pool.wait_ge(placed, 1)
                pool.wait_ge(payset, 1)
                pool.wait_ge(filled, 16)

                def body(i):
                    for g in range(2):
                        if not isinstance(i, int):
                            pool_wait(pool, scattered[g], i * 64)
                        at = (i * 2 + g) * 4
                        pool.tensor_copy(pstage[:, g], pay[:, bass.ds(at, 4), :]).then_inc(staged, 1)
                        pool.tensor_copy(istage[:, g], pos[:, bass.ds(at, 4)]).then_inc(staged, 1)
                        pool_wait(pool, staged, i * 4 + g * 2 + 2)
                        for u in range(4):
                            pool.indirect_dma_start(
                                out=rlist, out_offset=bass.IndirectOffsetOnAxis(ap=istage[:, g, u:u + 1], axis=0),
                                in_=pstage[:, g, u, :], in_offset=None, bounds_check=LIST_BLOCKS * SLOT + SLOT - 1,
                                oob_is_err=False).then_inc(scattered[g], 16)
                peeled(pool, ET // 8, body)
                for g in range(2):
                    pool.wait_ge(scattered[g], 64 * (ET // 8))


def rotation_phase(nc, con, rlist, MT):
    with phase(nc) as ph:
        sb = lambda n, s, d=F32: ph.enter_context(nc.sbuf_tensor(n, s, d))
        sem = lambda n: ph.sem(n)
        ident, after, ones, iota, iota1, part = (con[k] for k in ("ident", "after", "ones", "iota", "iota1", "part"))
        U = range(UB)
        cur, prev = sb("r_cur", [128, UB, FIELDS]), sb("r_prev", [128, UB, FIELDS])
        fld, tmp = sb("r_fld", [128, UB, 8]), sb("r_tmp", [128, UB, 16])
        mask, late = sb("r_mask", [128, UB, 128]), sb("r_late", [128, 128])
        key = sb("r_key", [128, UB, 2, 128])
        lt = sb("r_lt", [128, UB, 2, 128])
        neu = sb("r_neu", [128, UB, 384])
        gat = sb("r_gat", [128, UB, 2, 256])
        last = sb("r_last", [128, UB, 256])
        owt = sb("r_owt", [128, UB, 2, 128])
        ft, ub = sb("r_ft", [128, UB, 2, 128]), sb("r_ub", [128, UB, 256])
        M = sb("r_M", [128, 2, 256])
        ps_w = [ph.enter_context(nc.psum_tensor(f"r_psw{u}", [128, 512], F32)) for u in U]
        ps_n = [ph.enter_context(nc.psum_tensor(f"r_psn{u}", [128, 512], F32)) for u in U]
        ps_a = [ph.enter_context(nc.psum_tensor(f"r_psa{u}", [128, 512], F32)) for u in U]
        ps_m = [ph.enter_context(nc.psum_tensor(f"r_psm{u}", [128, 512], F32)) for u in U]
        dv = sem("r_dve")
        loaded, writes, rows, lset, built, uset, level, evac, fset, fsub, vset, vcp, mset, applied = (
            [sem(f"r_{n}{u}") for u in U] for n in ("loaded", "writes", "rows", "lset", "built", "uset", "level", "evac",
                                                    "fset", "fsub", "vset", "vcp", "mset", "applied"))
        minit, tset = sem("r_minit"), sem("r_tset")

        def count(eng):
            return eng.value_load(con["iterations"][0:1, 0:1], min_val=2, max_val=LIST_BLOCKS // UB)

        with nc.Block() as block:
            @block.sync
            def _(sp):
                def body(i):
                    for u in U:
                        if not isinstance(i, int):
                            sp.wait_ge(built[u], i)
                        row = (i * UB + u) * SLOT
                        sp.dma_start(cur[:, u, :], rlist[bass.ds(row + 1, SLOT), :]).then_inc(loaded[u], 16)
                        sp.dma_start(prev[:, u, :], rlist[bass.ds(row, SLOT), :]).then_inc(loaded[u], 16)
                peeled(sp, count(sp), body)

            @block.vector
            def _(dve):
                PER = UB * 27
                init = Tally(dve, dv)
                init.up(dve.memset(M[:], 0.0))
                for u in U:
                    init.up(dve.memset(fld[:, u, :], 0.0))
                dve.wait_ge(dv, init.n)
                init.up(dve.tensor_copy(M[:, 0, 0:128], ident[:]))
                dve.tensor_copy(M[:, 1, 128:256], ident[:]).then_inc(minit, 1)
                dve.wait_ge(minit, 1)
                start = init.n

                def build(c, i, u):
                    s, b = cur[:, u, :], tmp[:, u, :]
                    f = fld[:, u, :]
                    pr = prev[:, u, :]
                    isb = pr[:, EVENT:EVENT + 1]
                    dve.wait_ge(loaded[u], i * 32 + 32)
                    c.up(dve.scalar_tensor_tensor(f[:, R1:R2 + 1], pr[:, R1:R2 + 1], isb, s[:, R1:R2 + 1], ALU.mult, ALU.add))
                    c.up(dve.scalar_tensor_tensor(f[:, ALPHA:BETA + 1], pr[:, SIN:COS + 1], isb, s[:, ALPHA:BETA + 1], ALU.mult, ALU.add))
                    c.then(dve.tensor_scalar(b[:, 0:1], pr[:, R2:R2 + 1], 1.0, None, ALU.add))
                    dve.scalar_tensor_tensor(f[:, WR:WR + 1], b[:, 0:1], isb, s[:, WR:WR + 1], ALU.mult, ALU.add).then_inc(writes[u], 1)
                    c.then(dve.tensor_tensor(b[:, 1:2], part[:, 0:1], isb, ALU.subtract))
                    c.up(dve.scalar_tensor_tensor(mask[:, u, :], iota[:, 0:128], b[:, 1:2], iota1[:], ALU.is_lt, ALU.mult))
                    dve.wait_ge(writes[u], i + 1)
                    dve.wait_ge(rows[u], i + 1)
                    dve.wait_ge(dv, c.base + c.n)
                    W = ps_w[u][:, 0:128]
                    c.up(dve.scalar_tensor_tensor(key[:, u, 0, :], W, f[:, R1:R1 + 1], mask[:, u, :], ALU.is_equal, ALU.mult))
                    c.then(dve.scalar_tensor_tensor(key[:, u, 1, :], W, f[:, R2:R2 + 1], mask[:, u, :], ALU.is_equal, ALU.mult))
                    c.up(dve.scalar_tensor_tensor(late[:], W, f[:, WR:WR + 1], after[:], ALU.is_equal, ALU.mult, accum_out=b[:, 8:9]))
                    c.then(dve.tensor_reduce(b[:, 2:4], key[:, u], AX.X, ALU.max))
                    c.up(dve.tensor_scalar(b[:, 4:6], b[:, 2:4], 0.5, None, ALU.max))
                    c.then(dve.scalar_tensor_tensor(b[:, 6:8], b[:, 2:4], 0.5, f[:, ALPHA:BETA + 1], ALU.is_lt, ALU.mult))
                    for o in range(2):
                        c.up(dve.tensor_scalar(lt[:, u, o, :], key[:, u, o, :], b[:, 4 + o:5 + o], f[:, ALPHA + o:ALPHA + o + 1],
                                               ALU.is_equal, ALU.mult))
                    dve.wait_ge(dv, c.base + c.n)
                    dve.tensor_tensor(neu[:, u, 256:384], lt[:, u, 0, :], lt[:, u, 1, :], ALU.add).then_inc(lset[u], 1)
                    for o in range(2):
                        c.up(dve.tensor_scalar(gat[:, u, o, :], iota[:], f[:, R1 + o:R1 + o + 1], b[:, 6 + o:7 + o],
                                               ALU.is_equal, ALU.mult))
                    c.then(dve.tensor_scalar(b[:, 9:10], b[:, 8:9], 0.5, None, ALU.is_lt))
                    c.up(dve.tensor_scalar(last[:, u, :], iota[:], f[:, WR:WR + 1], b[:, 9:10], ALU.is_equal, ALU.mult))
                    for h in range(2):
                        c.up(dve.tensor_scalar(owt[:, u, h, :], W, part[:, h:h + 1], None, ALU.is_equal))
                    dve.wait_ge(dv, c.base + c.n)
                    dve.tensor_tensor(gat[:, u, 0, :], gat[:, u, 0, :], gat[:, u, 1, :], ALU.add).then_inc(built[u], 1)

                def apply(c, i, u):
                    dve.wait_ge(fset[u], i + 1)
                    dve.tensor_tensor(ft[:, u], ps_a[u][:, 0:256].rearrange("p (h t) -> p h t", h=2), owt[:, u], ALU.subtract).then_inc(fsub[u], 1)
                    dve.wait_ge(mset[u], i + 1)
                    dve.tensor_tensor(M[:], M[:], ps_m[u][:].rearrange("p (h c) -> p h c", h=2), ALU.add).then_inc(applied[u], 1)
                    dve.wait_ge(applied[u], i + 1)

                def body(i):
                    c = Tally(dve, dv, start + i * per[0])
                    for u in U:
                        build(c, i, u)
                    for u in U:
                        apply(c, i, u)
                    assert per[0] in (0, c.n) or i == 0
                    per[0] = c.n
                per = [0]
                peeled(dve, count(dve), body)
                dve.wait_ge(tset, 1)
                dve.tensor_copy(MT[:], ps_w[0][:].rearrange("p (h c) -> p h c", h=2)).then_inc(tset, 1)

            @block.scalar
            def _(act):
                def body(i):
                    for u in U:
                        act.wait_ge(uset[u], i + 1)
                        act.copy(neu[:, u, 0:128], ps_w[u][:, 128:256]).then_inc(evac[u], 1)
                    for k in range(LEVELS):
                        for u in U:
                            act.wait_ge(level[u], i * LEVELS + k + 1)
                            act.copy(neu[:, u, :] if k < LEVELS - 1 else neu[:, u, 128:256],
                                     ps_n[u][:, 0:384] if k < LEVELS - 1 else ps_n[u][:, 128:256]).then_inc(evac[u], 1)
                    for u in U:
                        act.wait_ge(vset[u], i + 1)
                        act.copy(ub[:, u, :], ps_a[u][:, 256:512]).then_inc(vcp[u], 1)
                peeled(act, count(act), body)

            @block.gpsimd
            def _(pool):
                def body(i):
                    for u in U:
                        if not isinstance(i, int):
                            pool_wait(pool, fset[u], i)
                        pool.tensor_copy(neu[:, u, 128:256], ident[:]).then_inc(lset[u], 1)
                peeled(pool, count(pool), body)

            @block.tensor
            def _(pe):
                def body(i):
                    for u in U:
                        pe.wait_ge(writes[u], i + 1)
                        pe.matmul(ps_w[u][:, 0:128], fld[:, u, WR:WR + 1].to_broadcast([128, 128]), ident[:], start=True, stop=True).then_inc(rows[u], 1)
                    for u in U:
                        pe.wait_ge(lset[u], 2 * i + 2)
                        pe.wait_ge(built[u], i + 1)
                        pe.transpose(ps_w[u][:, 128:256], neu[:, u, 256:384], ident[:]).then_inc(uset[u], 1)
                    for k in range(LEVELS):
                        for u in U:
                            pe.wait_ge(evac[u], i * (LEVELS + 1) + k + 1)
                            n = neu[:, u, :]
                            z = ps_n[u][:, 128:256]
                            pe.matmul(z, n[:, 256:384], n[:, 128:256], start=True, stop=False)
                            mm = pe.matmul(z, ident[:], n[:, 128:256], start=False, stop=True)
                            if k < LEVELS - 1:
                                pe.matmul(ps_n[u][:, 0:128], n[:, 256:384], n[:, 0:128], start=True, stop=True)
                                mm = pe.matmul(ps_n[u][:, 256:384], n[:, 0:128], n[:, 256:384], start=True, stop=True)
                            mm.then_inc(level[u], 1)
                    for u in U:
                        pe.wait_ge(evac[u], (i + 1) * (LEVELS + 1))
                        for h in range(2):
                            mm = pe.matmul(ps_a[u][:, h * 128:h * 128 + 128], gat[:, u, 0, h * 128:h * 128 + 128], neu[:, u, 128:256],
                                           start=True, stop=True)
                        mm.then_inc(fset[u], 1)
                    for u in U:
                        pe.wait_ge(fsub[u], i + 1)
                        if u:
                            pe.wait_ge(applied[u - 1], i + 1)
                        elif not isinstance(i, int):
                            pe.wait_ge(applied[UB - 1], i)
                        else:
                            pe.wait_ge(minit, 1)
                        for h in range(2):
                            mm = pe.matmul(ps_a[u][:, 256:512], ft[:, u, h, :], M[:, h, :], start=(h == 0), stop=(h == 1))
                        mm.then_inc(vset[u], 1)
                        pe.wait_ge(vcp[u], i + 1)
                        for h in range(2):
                            mm = pe.matmul(ps_m[u][:, h * 256:h * 256 + 256], last[:, u, h * 128:h * 128 + 128], ub[:, u, :],
                                           start=True, stop=True)
                        mm.then_inc(mset[u], 1)
                n = count(pe)
                peeled(pe, n, body)
                pe.wait_ge(applied[UB - 1], n)
                for a in range(2):
                    for b in range(2):
                        mm = pe.transpose(ps_w[0][:, a * 256 + b * 128:a * 256 + b * 128 + 128], M[:, b, a * 128:a * 128 + 128], ident[:])
                mm.then_inc(tset, 1)


USED = ET + NT - 1
CH = 16
STEPS = -(-USED // (2 * CH)) * CH * 2 - (CH if -(-USED // CH) % 2 else 0)
SQ = STEPS // 4
CT = STEPS // CH
CE = CT * P
BIG = 2.0 ** 90
AW = 272
G = 4
EPS = 1e-5


def graph_phase(nc, con, g, src2, dst2, dst_e, live):
    with phase(nc) as ph:
        sb = lambda n, s, d=F32: ph.enter_context(nc.sbuf_tensor(n, s, d))
        sem = lambda n: ph.sem(n)
        ident, ones, part = con["ident"], con["ones"], con["part"]
        B = NT - 1
        lasti, lastf, lt = sb("g_lasti", [B, ET], I32), sb("g_lastf", [B, ET]), sb("g_lt", [B, ET])
        cut, cut_q = sb("g_cut", [B, 4]), sb("g_cutq", [SQ, 1])
        stepi, stepf, comp = sb("g_stepi", [B, STEPS], I32), sb("g_stepf", [B, STEPS]), sb("g_comp", [B, STEPS])
        trow = sb("g_trow", [1, STEPS])
        pk, arow = sb("g_pk", [1, STEPS // 4, 2]), sb("g_arow", [1, STEPS])
        lv, la = sb("g_lv", [SQ, 4, P]), sb("g_la", [SQ, 4, P])
        minus = sb("g_minus", [1, 2])
        tcol, kcol, kidx = sb("g_tcol", [SQ, 4]), sb("g_kcol", [SQ, 4]), sb("g_kidx", [SQ, 4], I32)
        got, gf = sb("g_got", [SQ, 2, 4, P], I32), sb("g_gf", [SQ, 2, 4, P])
        dn = sb("g_dn", [128, CE + 2])
        flag = sb("g_flag", [128, 2])
        ps_t = ph.enter_context(nc.psum_tensor("g_pst", [128, 512], F32))
        ps_c = ph.enter_context(nc.psum_tensor("g_psc", [128, 512], F32))
        ps_x = [ph.enter_context(nc.psum_tensor(f"g_psx{a}", [128, 512], F32)) for a in range(2)]
        ps_f = ph.enter_context(nc.psum_tensor("g_psf", [128, 512], F32))
        dv, iot, loaded, dset, compared, counted, kset, gathered, fset, turned, flagged, flagrow, evac = (
            sem(f"g_{n}") for n in ("dve", "iota", "loaded", "dset", "compared", "counted", "kset", "gathered", "fset",
                                    "turned", "flagged", "flagrow", "evac"))
        lived, written = sem("g_lived"), sem("g_written")
        with nc.Block() as block:
            @block.sync
            def _(sp):
                sp.dma_start(lasti[:], dst_e[P - 1:P, :].to_broadcast([B, ET])).then_inc(loaded, 16)
                sp.wait_ge(lived, 1)
                body = live[1:1 + STEPS * P].rearrange("(j p e) -> p j e", j=4, e=P)
                sp.dma_start(body, lv[:]).then_inc(written, 16)
                ends = bass.AP(live.tensor, live.offset, [[STEPS * P + 2, 1], [STEPS * P + 1, 2], [1, 1]])
                sp.dma_start(ends, minus[:].rearrange("a (b c) -> a b c", c=1), allow_slow_non_contiguous=True).then_inc(written, 16)
                sp.wait_ge(written, 32)
                windows = bass.AP(live.tensor, live.offset, [[CE, CH], [1, CE + 2]])
                for h in range(H):
                    sp.dma_start(dn[h:128 - H + h + 1:H, :], windows).then_inc(dset, 16)

            @block.gpsimd
            def _(pool):
                pool.iota(stepi[:], [[1, STEPS]], base=0, channel_multiplier=0).then_inc(iot, 1)
                pool.wait_ge(kset, 1)
                for j in range(4):
                    for a, table in enumerate((src2, dst2)):
                        pool.indirect_dma_start(out=got[:, a, j, :], out_offset=None, in_=table,
                                                in_offset=bass.IndirectOffsetOnAxis(ap=kidx[:, j:j + 1], axis=0)).then_inc(gathered, 16)

            @block.tensor
            def _(pe):
                pe.wait_ge(compared, 1)
                pe.matmul(ps_t[0:1, 0:STEPS], ones[0:B, 0:1], comp[:], start=True, stop=True)
                for j in range(4):
                    mm = pe.matmul(ps_c[0:SQ, j:j + 1], comp[:, j * SQ:(j + 1) * SQ], ones[0:B, 0:1], start=True, stop=True)
                mm.then_inc(counted, 1)
                pe.wait_ge(fset, 1)
                for a in range(2):
                    for j in range(4):
                        mm = pe.transpose(ps_x[a][0:P, j * SQ:(j + 1) * SQ], gf[:, a, j, :], ident[0:SQ, 0:SQ])
                mm.then_inc(turned, 1)
                pe.wait_ge(flagged, 1)
                for a in range(2):
                    mm = pe.transpose(ps_f[0:1, a * 128:a * 128 + 128], flag[:, a:a + 1], ident[:])
                mm.then_inc(flagrow, 1)

            @block.vector
            def _(dve):
                c = Tally(dve, dv)
                c.up(dve.memset(minus[:], -1.0))
                dve.wait_ge(loaded, 16)
                dve.wait_ge(iot, 1)
                c.up(dve.tensor_copy(stepf[:], stepi[:]))
                c.then(dve.tensor_copy(lastf[:], lasti[:]))
                c.then(dve.tensor_scalar(cut[:, 0:1], part[0:B, 0:1], float(P), float(P), ALU.mult, ALU.add))
                c.then(dve.tensor_scalar(lt[:], lastf[:], cut[:, 0:1], None, ALU.is_lt))
                c.then(dve.tensor_reduce(cut[:, 1:2], lt[:], AX.X, ALU.add))
                c.then(dve.tensor_scalar(cut[:, 2:3], cut[:, 1:2], float(ET - 1), part[0:B, 0:1], ALU.min, ALU.add))
                dve.tensor_scalar(comp[:], stepf[:], cut[:, 2:3], None, ALU.is_gt).then_inc(compared, 1)
                dve.wait_ge(counted, 1)
                c.up(dve.tensor_copy(trow[:], ps_t[0:1, 0:STEPS]))
                c.then(dve.tensor_copy(tcol[:], ps_c[0:SQ, 0:4]))
                for j in range(4):
                    c.up(dve.tensor_scalar(kcol[:, j:j + 1], part[0:SQ, 0:1], float(j * SQ), tcol[:, j:j + 1], ALU.add, ALU.subtract))
                dve.wait_ge(dv, c.n)
                c.then(dve.tensor_scalar(kcol[:], kcol[:], float(ET - 1), None, ALU.min))
                dve.tensor_copy(kidx[:], kcol[:]).then_inc(kset, 1)
                c.up(dve.tensor_copy(arow[:], trow[:]))
                dve.wait_ge(dv, c.n)
                c.then(dve.memset(arow[:, USED:], float(STEPS - ET)))
                for row, word in ((trow, "tword"), (arow, "aword")):
                    tg = row[:].rearrange("a (q j) -> a q j", j=4)
                    c.then(dve.scalar_tensor_tensor(pk[:, :, 0], tg[:, :, 3], 64.0, tg[:, :, 2], ALU.mult, ALU.add))
                    c.then(dve.scalar_tensor_tensor(pk[:, :, 1], pk[:, :, 0], 64.0, tg[:, :, 1], ALU.mult, ALU.add))
                    c.then(dve.scalar_tensor_tensor(pk[:, :, 0], pk[:, :, 1], 64.0, tg[:, :, 0], ALU.mult, ALU.add))
                    c.then(dve.tensor_copy(g[word][:], pk[:, :, 0]))
                dve.wait_ge(gathered, 128)
                c.then(dve.tensor_copy(gf[:], got[:]))
                c.up(dve.tensor_scalar(lv[:], gf[:, 1], 1.0, None, ALU.add))
                c.then(dve.tensor_scalar(kcol[:], tcol[:], -float(P), None, ALU.mult))
                c.then(dve.tensor_scalar(cut_q[:], part[0:SQ, 0:1], float(USED - 3 * SQ), SKIP, ALU.is_ge, ALU.mult))
                c.then(dve.tensor_tensor(kcol[:, 3:4], kcol[:, 3:4], cut_q[:], ALU.add))
                for j in range(4):
                    c.up(dve.tensor_scalar(gf[:, 1, j, :], gf[:, 1, j, :], kcol[:, j:j + 1], None, ALU.add))
                dve.wait_ge(dv, c.n)
                dve.sem_inc(fset, 1)
                c.then(dve.tensor_scalar(la[:], gf[:, 1], 0.0, None, ALU.is_ge))
                c.then(dve.scalar_tensor_tensor(la[:], gf[:, 1], float(P), la[:], ALU.is_lt, ALU.mult))
                c.then(dve.tensor_tensor(lv[:], lv[:], la[:], ALU.mult))
                dve.tensor_scalar(lv[:], lv[:], 1.0, None, ALU.subtract).then_inc(lived, 1)
                dve.wait_ge(dset, 16 * H)
                c.up(dve.tensor_tensor(g["startf"][:], dn[:, 1:CE + 1], dn[:, 0:CE], ALU.not_equal))
                c.then(dve.tensor_tensor(g["endf"][:], dn[:, 1:CE + 1], dn[:, 2:CE + 2], ALU.not_equal))
                c.up(dve.tensor_scalar(g["keep"][:], g["startf"][:], -1.0, 1.0, ALU.mult, ALU.add))
                c.up(dve.tensor_scalar(g["endf"][:], g["endf"][:], -BIG, None, ALU.mult))
                dve.wait_ge(dv, c.n)
                c.then(dve.tensor_scalar(g["startf"][:], g["startf"][:], -BIG, None, ALU.mult))
                c.up(dve.tensor_reduce(flag[:, 0:1], g["startf"][:], AX.X, ALU.min))
                dve.tensor_reduce(flag[:, 1:2], g["endf"][:], AX.X, ALU.min).then_inc(flagged, 1)
                dve.wait_ge(turned, 1)
                c.up(dve.tensor_copy(g["srcs"][:], ps_x[0][0:P, 0:STEPS]))
                c.up(dve.tensor_copy(g["dstl"][:], ps_x[1][0:P, 0:STEPS]))
                dve.wait_ge(flagrow, 1)
                row = g["chunk"]
                for a in range(2):
                    c.up(dve.tensor_copy(row[:, a].rearrange("a (h c) -> a h c", h=H),
                                         ps_f[0:1, a * 128:a * 128 + 128].rearrange("a (c h) -> a h c", h=H)))
                dve.wait_ge(dv, c.n)
                c.up(dve.memset(row[:, 0].rearrange("a (h c) -> a h c", h=H)[:, :, 0:1], -BIG))
                c.then(dve.memset(row[:, 1].rearrange("a (h c) -> a h c", h=H)[:, :, CH - 1:CH], -BIG))
                c.then(dve.tensor_scalar(row[:, 2], row[:, 0], 1.0 / BIG, 1.0, ALU.mult, ALU.add))


def dense_phase(nc, con, layer, X, acc, ntab, weight, width, bias, tables):
    U = 5
    with phase(nc) as ph:
        sb = lambda n, s, d=F32: ph.enter_context(nc.sbuf_tensor(f"d{layer}_{n}", s, d))
        sem = lambda n: ph.sem(f"d{layer}_{n}")
        ident = con["ident"]
        st = sb("st", [P, NT, 6])
        mean, dif, var, rstd, nb = (sb(n, [P, NT]) for n in ("mean", "dif", "var", "rstd", "nb"))
        hn, ht = sb("hn", [P, U, D]), sb("ht", [128, U, 2, P])
        stage = sb("stage", [P, U, width])
        banks = -(-width // 512)
        ps_t = [ph.enter_context(nc.psum_tensor(f"d{layer}_pst{b}", [128, 512], F32)) for b in range(2)]
        ps_o = [ph.enter_context(nc.psum_tensor(f"d{layer}_pso{b}", [128, 512 * banks], F32)) for b in range(3)]
        dv, spread, rooted, ready, hset, tset, tcopied, mmdone, evac = (
            sem(n) for n in ("dve", "spread", "rooted", "ready", "hset", "tset", "tcopied", "mmdone", "evac"))
        stored = [sem(f"stored{u}") for u in range(U)]
        stores = len(tables)
        with nc.Block() as block:
            @block.vector
            def _(dve):
                with dve.Fori(0, NT) as n:
                    dve.bn_stats(st[:, bass.ds(n, 1), :].rearrange("p a s -> p (a s)"),
                                 X[:, bass.ds(n, 1), :].rearrange("p a d -> p (a d)")).then_inc(dv, 1)
                dve.wait_ge(dv, NT)
                c = Tally(dve, dv, NT)
                me, mo = st[:, :, 1], st[:, :, 4]
                c.up(dve.tensor_tensor(mean[:], me, mo, ALU.add))
                c.up(dve.tensor_tensor(dif[:], me, mo, ALU.subtract))
                c.then(dve.tensor_tensor(var[:], st[:, :, 2], st[:, :, 5], ALU.add))
                c.up(dve.tensor_scalar(mean[:], mean[:], 0.5, None, ALU.mult))
                c.then(dve.scalar_tensor_tensor(dif[:], dif[:], 0.25, dif[:], ALU.mult, ALU.mult))
                c.then(dve.scalar_tensor_tensor(var[:], var[:], 1.0 / D, dif[:], ALU.mult, ALU.add))
                dve.tensor_scalar(var[:], var[:], EPS, None, ALU.add).then_inc(spread, 1)
                dve.wait_ge(rooted, 1)
                c.then(dve.reciprocal(rstd[:], dif[:]))
                dve.scalar_tensor_tensor(nb[:], mean[:], -1.0, rstd[:], ALU.mult, ALU.mult).then_inc(ready, 1)

                def body(i):
                    for u in range(U):
                        n = i * U + u
                        x = X[:, bass.ds(n, 1), :].rearrange("p a d -> p (a d)")
                        dve.wait_ge(mmdone, n + 1)
                        if stores and not isinstance(i, int):
                            dve.wait_ge(stored[u], 16 * stores * i)
                        o = ps_o[u % 3][0:P, 0:width]
                        if layer == 0:
                            dve.tensor_tensor(x, x, o, ALU.add).then_inc(evac, 1)
                        elif layer == 1:
                            dve.tensor_tensor(stage[:, u, :], o, bias[:], ALU.add).then_inc(evac, 1)
                            dve.wait_ge(evac, n + 1)
                            dve.tensor_copy(ntab[:, bass.ds(n, 1), 0:D].rearrange("p a d -> p (a d)"), stage[:, u, 0:D]).then_inc(dv, 1)
                            dve.tensor_tensor(x, x, stage[:, u, 3 * D:4 * D], ALU.add).then_inc(dv, 1)
                        else:
                            if layer == 3:
                                dve.tensor_tensor(acc[:, bass.ds(n, 1), 0:D].rearrange("p a d -> p (a d)"), hn[:, u, :], bias[:], ALU.add).then_inc(dv, 1)
                            dve.tensor_copy(stage[:, u, :], o).then_inc(evac, 1)
                            dve.wait_ge(evac, n + 1)
                            dve.tensor_copy(ntab[:, bass.ds(n, 1), 0:H].rearrange("p a d -> p (a d)"), stage[:, u, D + H:]).then_inc(dv, 1)
                            if layer == 2:
                                dve.tensor_tensor(ntab[:, bass.ds(n, 1), H:2 * H].rearrange("p a d -> p (a d)"), stage[:, u, D + H:],
                                                  stage[:, u, D:D + H], ALU.add).then_inc(dv, 1)
                dve.wait_ge(ready, 1)
                peeled(dve, NT // U, body)

            @block.scalar
            def _(act):
                act.wait_ge(spread, 1)
                act.activation(dif[:], var[:], ACT.Sqrt).then_inc(rooted, 1)
                act.wait_ge(ready, 1)

                def body(i):
                    for u in range(U):
                        n = i * U + u
                        if not isinstance(i, int):
                            act.wait_ge(evac, n - U + 1)
                        act.activation(hn[:, u, :], X[:, bass.ds(n, 1), :].rearrange("p a d -> p (a d)"), ACT.Relu,
                                       bias=nb[:, bass.ds(n, 1)], scale=rstd[:, bass.ds(n, 1)]).then_inc(hset, 1)
                    for u in range(U):
                        n = i * U + u
                        act.wait_ge(tset, n + 1)
                        act.copy(ht[:, u], ps_t[u % 2][:, 0:2 * P].rearrange("p (a m) -> p a m", a=2)).then_inc(tcopied, 1)
                peeled(act, NT // U, body)

            @block.tensor
            def _(pe):
                def turn(i, u):
                    n = i * U + u
                    pe.wait_ge(hset, n + 1)
                    if u >= 2 or not isinstance(i, int):
                        pe.wait_ge(tcopied, n if u == 0 else n - 1)
                    for a in range(2):
                        mm = pe.transpose(ps_t[u % 2][:, a * P:(a + 1) * P], hn[:, u, a * 128:(a + 1) * 128], ident[0:P, 0:P])
                    mm.then_inc(tset, 1)

                def multiply(i, u):
                    n = i * U + u
                    pe.wait_ge(tcopied, n + 1)
                    if u >= 3 or not isinstance(i, int):
                        pe.wait_ge(evac, n - 2 if u >= 3 else n - 1)
                    for lo in range(0, width, 512):
                        hi = min(width, lo + 512)
                        for a in range(2):
                            mm = pe.matmul(ps_o[u % 3][0:P, lo:hi], ht[:, u, a, :], weight[:, a, lo:hi], start=(a == 0), stop=(a == 1))
                    mm.then_inc(mmdone, 1)

                def body(i):
                    for u in range(U):
                        turn(i, u)
                        if u:
                            multiply(i, u - 1)
                    multiply(i, U - 1)
                peeled(pe, NT // U, body)

            if stores:
                @block.sync
                def _(sp):
                    def body(i):
                        for u in range(U):
                            n = i * U + u
                            sp.wait_ge(evac, n + 1)
                            for table, lo, hi in tables:
                                sp.dma_start(table[bass.ds(n * P, P), :], stage[:, u, lo:hi]).then_inc(stored[u], 16)
                    peeled(sp, NT // U, body)
                    for u in range(U):
                        sp.wait_ge(stored[u], 16 * stores * (NT // U))


def node_tiles(nc, eng, word_row, at):
    word = eng.value_load(word_row[0:1, bass.ds(at, 1)], min_val=0, max_val=64 ** 4 - 1)
    return [(word >> (6 * u)) & 63 for u in range(G)]


def node_tile_of(nc, t):
    return nc.s_assert_within(t, 0, NT - 1, skip_runtime_bounds_check_because="a count of NT - 1 borders")


def load_attributes(nc, sp, g, b, at, attr, attr_t, done):
    back = node_tiles(nc, sp, g["aword"], at)
    for u in range(G):
        k = nc.s_assert_within(at * G + u - back[u], 0, ET - 1,
                               skip_runtime_bounds_check_because="the staircase stays inside the edge tiles")
        sp.dma_start(attr[:, b, u, :], attr_t[:, bass.ds(k * P, P)]).then_inc(done, 16)


def one_hot(dve, con, g, out, at):
    where = g["dstl"][:, bass.ds(at, G)]
    return dve.tensor_tensor(out, con["iota"][0:P, 0:P].unsqueeze(1).to_broadcast([P, G, P]),
                             where.unsqueeze(2).to_broadcast([P, G, P]), ALU.is_equal)


def score_phase(nc, con, g, layer, alpha, selfs, by_src, ntab, attr_t, we):
    first = layer == 1
    width = D if first else H
    nwidth = {1: D, 2: 2 * H, 3: H}[layer]
    edges = layer != 2
    ROUNDS = STEPS // (2 * G)
    with phase(nc) as ph:
        sb = lambda n, s, d=F32: ph.enter_context(nc.sbuf_tensor(f"s{layer}_{n}", s, d))
        sem = lambda n: ph.sem(f"s{layer}_{n}")
        psum = lambda n, w: ph.enter_context(nc.psum_tensor(f"s{layer}_{n}", [128, w], F32))
        istage = sb("istage", [P, 2, G], I32)
        rows = sb("rows", [P, 2, G, width])
        attr = sb("attr", [ED, 2, G, P])
        hot, cold = sb("hot", [P, 2, G, P]), sb("cold", [P, 2, G, P])
        ps_h = [psum(f"psh{b}", 512) for b in range(2)]
        ps_q = [psum("psq", 1024)] * 2 if first else [psum(f"psq{b}", 512) for b in range(2)]
        ps_e = [psum(f"pse{b}", 1024) for b in range(2)] if first else None
        staged = sem("staged")
        gathered, used, attrset, hset, hturned, hcopied, eset, qset, dv = (
            [sem(f"{n}{b}") for b in range(2)] for n in ("gathered", "used", "attrset", "hset", "hturned", "hcopied", "eset", "qset", "dve"))

        with nc.Block() as block:
            @block.gpsimd
            def _(pool):
                def body(i):
                    for b in range(2):
                        if not isinstance(i, int):
                            pool_wait(pool, used[b], i)
                        pool.tensor_copy(istage[:, b], g["srcs"][:, bass.ds((i * 2 + b) * G, G)]).then_inc(staged, 1)
                        pool_wait(pool, staged, i * 2 + b + 1)
                        for u in range(G):
                            pool.indirect_dma_start(out=rows[:, b, u, :], out_offset=None, in_=by_src,
                                                    in_offset=bass.IndirectOffsetOnAxis(ap=istage[:, b, u:u + 1], axis=0)
                                                    ).then_inc(gathered[b], 16)
                peeled(pool, ROUNDS, body)

            if edges:
                @block.sync
                def _(sp):
                    def body(i):
                        for b in range(2):
                            if not isinstance(i, int):
                                sp.wait_ge(qset[b], i)
                                sp.nop(nofuse=True)
                            load_attributes(nc, sp, g, b, i * 2 + b, attr, attr_t, attrset[b])
                    peeled(sp, ROUNDS, body)

            @block.scalar
            def _(act):
                def body(i):
                    for b in range(2):
                        act.wait_ge(hturned[b], i + 1)
                        act.copy(cold[:, b].rearrange("p u e -> p (u e)"), ps_h[b][0:P, 0:G * P]).then_inc(hcopied[b], 1)
                peeled(act, ROUNDS, body)

            @block.tensor
            def _(pe):
                def turn(i, b):
                    pe.wait_ge(hset[b], i + 1)
                    for u in range(G):
                        mm = pe.transpose(ps_h[b][0:P, u * P:(u + 1) * P], hot[:, b, u, :], con["ident"][0:P, 0:P])
                    mm.then_inc(hturned[b], 1)

                def spread(i, b):
                    ts = node_tiles(nc, pe, g["tword"], i * 2 + b)
                    if edges:
                        pe.wait_ge(attrset[b], 64 * i + 64)
                    if not isinstance(i, int):
                        pe.wait_ge(used[b], i)
                    if first:
                        for u in range(G):
                            mm = pe.matmul(ps_e[b][0:P, u * D:(u + 1) * D], attr[:, b, u, :], we, start=True, stop=True)
                        mm.then_inc(eset[b], 1)
                        if b:
                            pe.wait_ge(used[0], i + 1)
                        elif not isinstance(i, int):
                            pe.wait_ge(used[1], i)
                    pe.wait_ge(hcopied[b], i + 1)
                    for u in range(G):
                        o = ps_q[b][0:P, u * nwidth:(u + 1) * nwidth]
                        if layer == 3:
                            pe.matmul(o, attr[:, b, u, :], we, start=True, stop=False)
                        t = node_tile_of(nc, ts[u])
                        mm = pe.matmul(o, cold[:, b, u, :], ntab[:, bass.ds(t, 1), 0:nwidth].rearrange("p a d -> p (a d)"),
                                       start=layer != 3, stop=True)
                    mm.then_inc(qset[b], 1)

                def body(i):
                    for b in range(2):
                        turn(i, b)
                        spread(i, b)
                peeled(pe, ROUNDS, body)

            @block.vector
            def _(dve):
                def point(i, b):
                    one_hot(dve, con, g, hot[:, b], (i * 2 + b) * G).then_inc(hset[b], 1)

                def score(i, b):
                    s = rows[:, b]
                    at = (i * 2 + b) * G
                    out = alpha[:, bass.ds(at, G), :]
                    q = ps_q[b][0:P, 0:G * nwidth].rearrange("p (u d) -> p u d", u=G)
                    dve.wait_ge(gathered[b], 64 * i + 64)
                    if first:
                        dve.wait_ge(eset[b], i + 1)
                        dve.tensor_tensor(s, s, ps_e[b][0:P, :].rearrange("p (u d) -> p u d", u=G), ALU.add).then_inc(dv[b], 1)
                        dve.wait_ge(dv[b], 2 * i + 1)
                        dve.wait_ge(qset[b], i + 1)
                        dve.tensor_tensor(s, s, q, ALU.mult).then_inc(dv[b], 1)
                        dve.wait_ge(dv[b], 2 * i + 2)
                        dve.tensor_reduce(out, s.rearrange("p u (h c) -> p u h c", h=H), AX.X, ALU.add).then_inc(used[b], 1)
                    else:
                        dve.wait_ge(qset[b], i + 1)
                        if layer == 2:
                            dve.tensor_copy(selfs[:, bass.ds(at, G), :], q[:, :, H:]).then_inc(dv[b], 1)
                        dve.tensor_tensor(out, s, q[:, :, 0:H], ALU.add).then_inc(used[b], 1)

                def body(i, last=False):
                    for b in range(2):
                        if b == 0 or not last:
                            n, nb = (i, 1) if b == 0 else (i + 1, 0)
                            if not (isinstance(n, int) and n == 0):
                                dve.wait_ge(hturned[nb], n)
                            point(n, nb)
                        score(i, b)
                point(0, 0)
                body(0)
                with dve.Fori(1, ROUNDS - 1) as i:
                    body(i)
                body(ROUNDS - 1, last=True)


def softmax_phase(nc, con, g, layer, alpha, selfs):
    with_self = layer == 2
    with phase(nc) as ph:
        sb = lambda n, s, d=F32: ph.enter_context(nc.sbuf_tensor(f"m{layer}_{n}", s, d))
        sem = lambda n: ph.sem(f"m{layer}_{n}")
        ident = con["ident"]
        at = sb("at", [128, CE])
        run_w, back_w = (sb(n, [128, STEPS * H]) for n in ("run", "back"))
        run, back = run_w[:, 0:CE], back_w[:, 0:CE]
        own = sb("own", [128, CE]) if with_self else None
        row, carry, shift, init = sb("row", [1, 128]), sb("carry", [1, 128]), sb("shift", [1, 128]), sb("init", [128, 1])
        ps = [ph.enter_context(nc.psum_tensor(f"m{layer}_ps{b}", [128, 512], F32)) for b in range(4)]
        ps_r = ph.enter_context(nc.psum_tensor(f"m{layer}_psr", [128, 512], F32))
        ps_c = ph.enter_context(nc.psum_tensor(f"m{layer}_psc", [128, 512], F32))
        dv, turned, copied, ended, rowed, shifted, colled, shiftd, powered, weighed, back_t, back_c = (
            sem(n) for n in ("dve", "turned", "copied", "ended", "rowed", "shifted", "colled", "shiftd", "powered", "weighed",
                             "back_t", "back_c"))
        arrays = [(alpha, at, back_w)] + ([(selfs, own, run_w)] if with_self else [])
        by_step = lambda x: x[0:P, :].rearrange("p (s m) -> p s m", s=CT)
        groups = [(a, s0, min(4, CT - s0)) for a in range(len(arrays)) for s0 in range(0, CT, 4)]
        scale = 1.0 / math.sqrt(C) if layer == 1 else 1.0
        chains = 4
        regrouped = sem("regrouped")

        with nc.Block() as block:
            @block.tensor
            def _(pe):
                pe.wait_ge(regrouped, len(arrays))
                for n, (a, s0, k) in enumerate(groups):
                    if n >= 4:
                        pe.wait_ge(copied, n - 3)
                    for j in range(k):
                        mm = pe.transpose(ps[n % 4][:, j * P:(j + 1) * P], by_step(arrays[a][2])[:, s0 + j], ident[0:P, 0:P])
                    mm.then_inc(turned, 1)
                for n in range(chains):
                    pe.wait_ge(ended, n + 1)
                    v = (run[:, CE - 1:CE] if n % 2 == 0 else back[:, 0:1])
                    pe.transpose(ps_r[0:1, 0:128], v, ident[:]).then_inc(rowed, 1)
                    pe.wait_ge(shifted, n + 1)
                    pe.transpose(ps_c[:, 0:1], shift[:], ident[0:1, 0:1]).then_inc(colled, 1)
                pe.wait_ge(weighed, 1)
                for n, (a, s0, k) in enumerate(groups):
                    if n >= 4:
                        pe.wait_ge(back_c, n - 3)
                    for j in range(k):
                        mm = pe.transpose(ps[n % 4][0:P, j * 128:(j + 1) * 128], arrays[a][1][:, (s0 + j) * P:(s0 + j + 1) * P], ident[:])
                    mm.then_inc(back_t, 1)

            @block.scalar
            def _(act):
                for n, (a, s0, k) in enumerate(groups):
                    act.wait_ge(turned, n + 1)
                    act.mul(arrays[a][1][:, s0 * P:(s0 + k) * P], ps[n % 4][:, 0:k * P], scale).then_inc(copied, 1)
                act.wait_ge(shiftd, 1)
                act.activation(at[:], at[:], ACT.Exp).then_inc(powered, 1)
                if with_self:
                    act.activation(own[:], own[:], ACT.Exp).then_inc(powered, 1)
                for n, (a, s0, k) in enumerate(groups):
                    act.wait_ge(back_t, n + 1)
                    view = arrays[a][0][:].rearrange("p (c s) h -> p s c h", c=CH)
                    act.copy(view[:, s0:s0 + k], ps[n % 4][0:P, 0:k * 128].rearrange("p (s c h) -> p s c h", s=k, h=H)).then_inc(back_c, 1)

            @block.vector
            def _(dve):
                c = Tally(dve, dv)
                for x, _, by in arrays:
                    dve.tensor_copy(by_step(by).rearrange("p s (c h) -> p s c h", h=H),
                                    x[:].rearrange("p (c s) h -> p s c h", c=CH)).then_inc(regrouped, 1)
                dve.wait_ge(copied, len(groups))
                if layer != 1:
                    for _, x, _ in arrays:
                        c.up(dve.scalar_tensor_tensor(x[:], x[:], 0.2, x[:], ALU.mult, ALU.max))
                    dve.wait_ge(dv, c.n)
                peak = at
                if with_self:
                    c.then(dve.tensor_tensor(back[:], at[:], own[:], ALU.max))
                    peak = back

                def scan(n, out, flags, src, start, op0, op1, flip):
                    o, f, s = (x[:, ::-1] if flip else x[:, :] for x in (out, flags, src))
                    dve.tensor_tensor_scan(o, f, s, start, op0, op1).then_inc(ended, 1)
                    dve.wait_ge(rowed, n + 1)
                    c.then(dve.tensor_copy(row[:].rearrange("a (h c) -> a h c", h=H), ps_r[0:1, 0:128].rearrange("a (c h) -> a h c", h=H)))
                    fl = g["chunk"][:, 1 if flip else (2 if op0 == ALU.mult else 0)]
                    r, y = (row[:, ::-1], carry[:, ::-1]) if flip else (row[:, :], carry[:, :])
                    c.up(dve.tensor_tensor_scan(y, fl[:, ::-1] if flip else fl, r, start, op0, op1))
                    c.then(dve.memset(shift[:], start))
                    y3 = carry[:].rearrange("a (h c) -> a c h", h=H)
                    s3 = shift[:].rearrange("a (c h) -> a c h", h=H)
                    if flip:
                        dve.tensor_copy(s3[:, 0:CH - 1], y3[:, 1:CH]).then_inc(shifted, 1)
                    else:
                        dve.tensor_copy(s3[:, 1:CH], y3[:, 0:CH - 1]).then_inc(shifted, 1)
                    dve.wait_ge(colled, n + 1)
                    c.then(dve.tensor_copy(init[:], ps_c[:, 0:1]))
                    c.then(dve.tensor_tensor_scan(o, f, s, init[:], op0, op1))

                scan(0, run, g["startf"], peak, -BIG, ALU.add, ALU.max, False)
                scan(1, back, g["endf"], run, -BIG, ALU.add, ALU.max, True)
                if with_self:
                    c.up(dve.tensor_tensor(own[:], own[:], back[:], ALU.subtract))
                c.up(dve.tensor_tensor(at[:], at[:], back[:], ALU.subtract))
                dve.wait_ge(dv, c.n)
                dve.sem_inc(shiftd, 1)
                dve.wait_ge(powered, 2 if with_self else 1)
                scan(2, run, g["keep"], at, 0.0, ALU.mult, ALU.add, False)
                scan(3, back, g["endf"], run, -BIG, ALU.add, ALU.max, True)
                if with_self:
                    c.then(dve.tensor_tensor(back[:], back[:], own[:], ALU.add))
                c.then(dve.tensor_scalar(back[:], back[:], 1e-16, None, ALU.add))
                c.then(dve.reciprocal(back[:], back[:]))
                c.up(dve.tensor_tensor(at[:], at[:], back[:], ALU.mult))
                if with_self:
                    c.then(dve.tensor_tensor(own[:], own[:], back[:], ALU.mult))
                    c.up(dve.scalar_tensor_tensor(own[:], g["endf"][:], -1.0 / BIG, own[:], ALU.mult, ALU.mult))
                dve.wait_ge(dv, c.n)
                dve.sem_inc(weighed, 1)


def message_phase(nc, con, g, layer, acc, weights, selfs, table, attr_t, we):
    first, with_self = layer == 1, layer == 2
    mw = D + H + 1 if with_self else D
    pitch = 512 if with_self else D
    B = 4
    ROUNDS = STEPS // (B * G)
    with phase(nc) as ph:
        sb = lambda n, s, d=F32: ph.enter_context(nc.sbuf_tensor(f"a{layer}_{n}", s, d))
        sem = lambda n: ph.sem(f"a{layer}_{n}")
        istage = sb("istage", [P, B, G], I32)
        msg = sb("msg", [P, B, G, mw])
        away, hot = sb("away", [P, 2, G, P]), sb("hot", [P, B, G, P])
        attr = sb("attr", [ED, B, G, P]) if first else None
        ps_o = [ph.enter_context(nc.psum_tensor(f"a{layer}_pso{s}", [128, G * pitch], F32)) for s in range(2)]
        ps_e = [ph.enter_context(nc.psum_tensor(f"a{layer}_pse{s}", [128, G * D], F32)) for s in range(2)] if first else None
        staged, edone, setup, added, distant = sem("staged"), sem("edone"), sem("setup"), sem("added"), sem("distant")
        gathered, oset, aset, eset, hset, mset, summed = (
            [sem(f"{n}{b}") for b in range(B)] for n in ("gathered", "oset", "aset", "eset", "hset", "mset", "summed"))

        with nc.Block() as block:
            @block.gpsimd
            def _(pool):
                def body(i):
                    for b in range(B):
                        if not isinstance(i, int):
                            pool_wait(pool, summed[b], i)
                        pool.tensor_copy(istage[:, b], g["srcs"][:, bass.ds((i * B + b) * G, G)]).then_inc(staged, 1)
                        pool_wait(pool, staged, i * B + b + 1)
                        for u in range(G):
                            pool.indirect_dma_start(out=msg[:, b, u, 0:D], out_offset=None, in_=table,
                                                    in_offset=bass.IndirectOffsetOnAxis(ap=istage[:, b, u:u + 1], axis=0)
                                                    ).then_inc(gathered[b], 16)
                peeled(pool, ROUNDS, body)

            if first:
                @block.sync
                def _(sp):
                    def body(i):
                        for b in range(B):
                            if not isinstance(i, int):
                                sp.wait_ge(eset[b], i)
                                sp.nop(nofuse=True)
                            load_attributes(nc, sp, g, b, i * B + b, attr, attr_t, aset[b])
                    peeled(sp, ROUNDS, body)

            @block.scalar
            def _(act):
                def body(i):
                    for b in range(B):
                        n = i * B + b
                        if not isinstance(i, int):
                            act.wait_ge(summed[b], i)
                        if with_self:
                            act.copy(msg[:, b, :, D:D + H], selfs[:, bass.ds(n * G, G), :]).then_inc(oset[b], 1)
                        if b >= 2:
                            act.wait_ge(hset[b - 2], i + 1)
                        elif not isinstance(i, int):
                            act.wait_ge(hset[b + 2], i)
                        for u in range(G):
                            act.activation(away[:, b % 2, u, :], con["iota"][0:P, 0:P], ACT.Abs, scale=-1.0,
                                           bias=g["dstl"][:, bass.ds(n * G + u, 1)]).then_inc(distant, 1)
                        act.wait_ge(distant, (n + 1) * G)
                        act.activation(hot[:, b], away[:, b % 2], ACT.Relu, scale=-1.0, bias=con["ones"][0:P, 0:1]).then_inc(hset[b], 1)
                peeled(act, ROUNDS, body)

            @block.vector
            def _(dve):
                def message(i, b):
                    n = i * B + b
                    v = msg[:, b, :, 0:D]
                    dve.wait_ge(gathered[b], 16 * G * i + 16 * G)
                    if first:
                        dve.wait_ge(eset[b], i + 1)
                        dve.tensor_tensor(v, v, ps_e[b % 2][0:P, :].rearrange("p (u d) -> p u d", u=G), ALU.add).then_inc(edone, 1)
                        dve.wait_ge(edone, n + 1)
                    v = v.rearrange("p u (h c) -> p u h c", h=H)
                    dve.tensor_tensor(v, v, weights[:, bass.ds(n * G, G), :].unsqueeze(3).to_broadcast([P, G, H, C]), ALU.mult).then_inc(mset[b], 1)

                def add(i, b, n):
                    ts = node_tiles(nc, dve, g["tword"], n)
                    dve.wait_ge(summed[b], i + 1)
                    for u in range(G):
                        row = acc[:, bass.ds(node_tile_of(nc, ts[u]), 1), 0:mw].rearrange("p a d -> p (a d)")
                        dve.tensor_tensor(row, row, ps_o[b % 2][0:P, u * pitch:u * pitch + mw], ALU.add).then_inc(added, 1)
                        dve.wait_ge(added, n * G + u + 1)

                def body(i):
                    for b in range(B):
                        message(i, b)
                        if b >= 2:
                            add(i, b - 2, i * B + b - 2)
                        elif not isinstance(i, int):
                            add(i - 1, b + 2, i * B + b - 2)
                if with_self:
                    dve.memset(msg[:, :, :, D + H:], 1.0).then_inc(setup, 1)
                peeled(dve, ROUNDS, body)
                for b in (B - 2, B - 1):
                    add(ROUNDS - 1, b, (ROUNDS - 1) * B + b)

            @block.tensor
            def _(pe):
                def edges(i, b):
                    n = i * B + b
                    pe.wait_ge(aset[b], 16 * G * i + 16 * G)
                    if b >= 2 or not opening(i):
                        pe.wait_ge(edone, n - 1)
                    for u in range(G):
                        mm = pe.matmul(ps_e[b % 2][0:P, u * D:(u + 1) * D], attr[:, b, u, :], we, start=True, stop=True)
                    mm.then_inc(eset[b], 1)

                def total(i, b):
                    n = i * B + b
                    pe.wait_ge(hset[b], i + 1)
                    pe.wait_ge(mset[b], i + 1)
                    if with_self:
                        pe.wait_ge(oset[b], i + 1)
                    if b >= 2 or not opening(i):
                        pe.wait_ge(added, (n - 1) * G)
                    for u in range(G):
                        mm = pe.matmul(ps_o[b % 2][0:P, u * pitch:u * pitch + mw], hot[:, b, u, :], msg[:, b, u, :], start=True, stop=True)
                    mm.then_inc(summed[b], 1)

                def body(i, last=False):
                    for b in range(B):
                        total(i, b)
                        if first and b < 2:
                            edges(i, b + 2)
                        elif first and not last:
                            edges(i + 1, b - 2)
                if first:
                    edges(0, 0)
                    edges(0, 1)
                if with_self:
                    pe.wait_ge(setup, 1)
                body(0)
                with pe.Fori(1, ROUNDS - 1) as i:
                    body(i)
                body(ROUNDS - 1, last=True)


def attention_end_phase(nc, con, X, acc, table, bias):
    U = 5
    with phase(nc) as ph:
        sb = lambda n, s, d=F32: ph.enter_context(nc.sbuf_tensor(f"e_{n}", s, d))
        sem = lambda n: ph.sem(f"e_{n}")
        h2, neg = sb("h2", [P, U, D]), sb("neg", [P, U, D])
        ws = sb("ws", [P, NT, H])
        alone = sb("alone", [P, NT])
        dv, loaded, low, powered, done = (sem(n) for n in ("dve", "loaded", "low", "powered", "done"))
        lo = [sem(f"loaded{u}") for u in range(U)]
        with nc.Block() as block:
            @block.sync
            def _(sp):
                def body(i):
                    for u in range(U):
                        n = i * U + u
                        if not isinstance(i, int):
                            sp.wait_ge(done, n - U + 1)
                        sp.dma_start(h2[:, u, :], table[bass.ds(n * P, P), :]).then_inc(lo[u], 16)
                peeled(sp, NT // U, body)

            @block.scalar
            def _(act):
                def body(i):
                    for u in range(U):
                        act.wait_ge(low, i * U + u + 1)
                        act.activation(neg[:, u, :], neg[:, u, :], ACT.Exp).then_inc(powered, 1)
                peeled(act, NT // U, body)

            @block.vector
            def _(dve):
                c = Tally(dve, dv)
                c.then(dve.tensor_scalar(alone[:], acc[:, :, D + H], 0.5, None, ALU.is_lt))
                c.then(dve.tensor_tensor(ws[:], acc[:, :, D:D + H], alone[:].unsqueeze(2).to_broadcast([P, NT, H]), ALU.add))
                start = c.n
                PER = 3 * U

                def body(i):
                    c = Tally(dve, dv, i * PER + start)
                    for u in range(U):
                        n = i * U + u
                        z = acc[:, bass.ds(n, 1), 0:D].rearrange("p a d -> p (a d)")
                        m = h2[:, u, :]
                        dve.wait_ge(lo[u], 16 * i + 16)
                        c.then(dve.tensor_tensor(m.rearrange("p (h c) -> p h c", h=H), m.rearrange("p (h c) -> p h c", h=H),
                                                 ws[:, bass.ds(n, 1), :].rearrange("p a h -> p (a h)").unsqueeze(2).to_broadcast([P, H, C]), ALU.mult))
                        c.then(dve.tensor_tensor(m, m, bias[:], ALU.add))
                        c.then(dve.tensor_tensor(z, z, m, ALU.add))
                        if not isinstance(i, int):
                            dve.wait_ge(done, n - U + 1)
                        dve.tensor_scalar(neg[:, u, :], z, 0.0, None, ALU.min).then_inc(low, 1)
                    for u in range(U):
                        n = i * U + u
                        z = acc[:, bass.ds(n, 1), 0:D].rearrange("p a d -> p (a d)")
                        x = X[:, bass.ds(n, 1), :].rearrange("p a d -> p (a d)")
                        dve.wait_ge(powered, n + 1)
                        dve.scalar_tensor_tensor(z, z, 0.0, neg[:, u, :], ALU.max, ALU.add).then_inc(low2[u], 1)
                        dve.wait_ge(low2[u], i + 1)
                        dve.scalar_tensor_tensor(x, z, -1.0, x, ALU.add, ALU.add).then_inc(done, 1)
                low2 = [ph.sem(f"e_sum{u}") for u in range(U)]
                peeled(dve, NT // U, body)


def final_phase(nc, con, X, acc, gamma, beta, out):
    U = 5
    with phase(nc) as ph:
        sb = lambda n, s, d=F32: ph.enter_context(nc.sbuf_tensor(f"f_{n}", s, d))
        sem = lambda n: ph.sem(f"f_{n}")
        st = sb("st", [P, NT, 6])
        mean, dif, var, rstd, nb = (sb(n, [P, NT]) for n in ("mean", "dif", "var", "rstd", "nb"))
        y = sb("y", [P, U, D])
        dv, spread, rooted, ready, normed, done = (sem(n) for n in ("dve", "spread", "rooted", "ready", "normed", "done"))
        stored = [sem(f"stored{u}") for u in range(U)]
        with nc.Block() as block:
            @block.vector
            def _(dve):
                with dve.Fori(0, NT) as n:
                    dve.bn_stats(st[:, bass.ds(n, 1), :].rearrange("p a s -> p (a s)"),
                                 acc[:, bass.ds(n, 1), 0:D].rearrange("p a d -> p (a d)")).then_inc(dv, 1)
                dve.wait_ge(dv, NT)
                c = Tally(dve, dv, NT)
                me, mo = st[:, :, 1], st[:, :, 4]
                c.up(dve.tensor_tensor(mean[:], me, mo, ALU.add))
                c.up(dve.tensor_tensor(dif[:], me, mo, ALU.subtract))
                c.then(dve.tensor_tensor(var[:], st[:, :, 2], st[:, :, 5], ALU.add))
                c.up(dve.tensor_scalar(mean[:], mean[:], 0.5, None, ALU.mult))
                c.then(dve.scalar_tensor_tensor(dif[:], dif[:], 0.25, dif[:], ALU.mult, ALU.mult))
                c.then(dve.scalar_tensor_tensor(var[:], var[:], 1.0 / D, dif[:], ALU.mult, ALU.add))
                dve.tensor_scalar(var[:], var[:], EPS, None, ALU.add).then_inc(spread, 1)
                dve.wait_ge(rooted, 1)
                c.then(dve.reciprocal(rstd[:], dif[:]))
                dve.scalar_tensor_tensor(nb[:], mean[:], -1.0, rstd[:], ALU.mult, ALU.mult).then_inc(ready, 1)
                start = NT + c.n

                def body(i):
                    c = Tally(dve, dv, i * 2 * U + start)
                    for u in range(U):
                        n = i * U + u
                        dve.wait_ge(normed, n + 1)
                        c.then(dve.tensor_tensor(y[:, u, :], y[:, u, :], gamma[:], ALU.mult))
                        c.then(dve.tensor_tensor(y[:, u, :], y[:, u, :], beta[:], ALU.add))
                        dve.tensor_tensor(y[:, u, :], y[:, u, :], X[:, bass.ds(n, 1), :].rearrange("p a d -> p (a d)"), ALU.add).then_inc(done, 1)
                peeled(dve, NT // U, body)

            @block.scalar
            def _(act):
                act.wait_ge(spread, 1)
                act.activation(dif[:], var[:], ACT.Sqrt).then_inc(rooted, 1)
                act.wait_ge(ready, 1)

                def body(i):
                    for u in range(U):
                        n = i * U + u
                        if not isinstance(i, int):
                            act.wait_ge(stored[u], 16 * i)
                        act.activation(y[:, u, :], acc[:, bass.ds(n, 1), 0:D].rearrange("p a d -> p (a d)"), ACT.Identity,
                                       bias=nb[:, bass.ds(n, 1)], scale=rstd[:, bass.ds(n, 1)]).then_inc(normed, 1)
                peeled(act, NT // U, body)

            @block.sync
            def _(sp):
                def body(i):
                    for u in range(U):
                        n = i * U + u
                        sp.wait_ge(done, n + 1)
                        sp.dma_start(out[bass.ds(n * P, P), :], y[:, u, :]).then_inc(stored[u], 16)
                peeled(sp, NT // U, body)
                for u in range(U):
                    sp.wait_ge(stored[u], 16 * (NT // U))


def weights_phase(nc, con, a, w):
    with phase(nc) as ph:
        sb = lambda n, s, d=F32: ph.enter_context(nc.sbuf_tensor(f"w_{n}", s, d))
        att = {n: sb(n, [128, D]) for n in ("l2s", "l2d", "l3s", "l3d", "l3e")}
        wedge = sb("wedge", [ED, D])
        prod = sb("prod", [128, 9, D])
        loaded, folded = ph.sem("w_loaded"), ph.sem("w_folded")
        with nc.Block() as block:
            @block.sync
            def _(sp):
                rows = lambda x: x.rearrange("(a p) n -> p a n", p=128)
                loads = [(w["l1"][:], rows(a["w1"])), (w["l2"][:, :, 0:D], rows(a["w2"])), (w["l3"][:, :, 0:D], rows(a["w3"])),
                         (w["we1"][:], a["we1"]), (wedge[:], a["we3"]), (w["x"][:], a["x"].rearrange("(n p) d -> p n d", p=P))]
                for k in ("b1", "b2", "b3", "gamma", "beta"):
                    loads.append((w[k][:], a[k].to_broadcast([P, a[k].shape[1]])))
                for k in att:
                    loads.append((att[k][:], a[k].to_broadcast([128, D])))
                for dst, src in loads:
                    sp.dma_start(dst, src).then_inc(loaded, 16)
                con["loads"] = len(loads)

            @block.vector
            def _(dve):
                dve.wait_ge(loaded, 16 * con["loads"])
                jobs = []
                for name, s, d in (("l2", "l2s", "l2d"), ("l3", "l3s", "l3d")):
                    for half in range(2):
                        for j, v in enumerate((s, d)):
                            jobs.append((w[name][:, half, 0:D], att[v][:], w[name][:, half, D + j * H:D + (j + 1) * H], 128))
                jobs.append((wedge[:], att["l3e"][0:ED, :], w["we3"][:], ED))
                for n, (x, v, o, p) in enumerate(jobs):
                    dve.tensor_tensor(prod[0:p, n, :], x, v, ALU.mult).then_inc(folded, 1)
                dve.wait_ge(folded, len(jobs))
                for n, (x, v, o, p) in enumerate(jobs):
                    dve.tensor_reduce(o, prod[0:p, n, :].rearrange("p (h c) -> p h c", h=H), AX.X, ALU.add).then_inc(folded, 1)


def zero_phase(nc, acc, name):
    with phase(nc) as ph:
        z = ph.sem(name)
        with nc.Block() as block:
            @block.vector
            def _(dve):
                dve.memset(acc[:], 0.0).then_inc(z, 1)


def program(nc, a, out):
    with ExitStack() as ctx:
        sb = lambda n, s, d=F32: ctx.enter_context(nc.sbuf_tensor(n, s, d))
        dram = lambda n, r, c: nc.dram_tensor(n, (r, c), F32, kind="Internal").ap()
        con = {k: sb("con_" + k, [128, n]) for k, n in
               (("ident", 128), ("iota", 256), ("iota1", 128), ("after", 128), ("ones", 128), ("part", 2))}
        con["iterations"] = sb("con_iterations", [1, 1], I32)
        w = {"l1": sb("wt1", [128, 2, 4 * D]), "l2": sb("wt2", [128, 2, D + 2 * H]), "l3": sb("wt3", [128, 2, D + 2 * H]),
             "we1": sb("we1", [ED, D]), "we3": sb("we3", [ED, H]), "x": sb("x", [P, NT, D])}
        for k, n in (("b1", 4 * D), ("b2", D), ("b3", D), ("gamma", D), ("beta", D)):
            w[k] = sb("row_" + k, [P, n])
        MT = sb("MT", [128, 2, ROT])
        X = w["x"]
        rlist = dram("rotation_list", (LIST_BLOCKS + 1) * SLOT, FIELDS)
        constants_phase(nc, con)
        weights_phase(nc, con, a, w)
        rotation_list_phase(nc, con, a["w_e"], a["src_e"], a["dst_e"], rlist)
        rotation_phase(nc, con, rlist, MT)
        dense_phase(nc, con, 0, X, None, None, MT, ROT, None, [])

        acc = sb("acc", [P, NT, AW])
        g = {"srcs": sb("g_srcs", [P, STEPS], I32), "dstl": sb("g_dstl", [P, STEPS]),
             "tword": sb("g_tword", [1, STEPS // 4], I32), "aword": sb("g_aword", [1, STEPS // 4], I32),
             "startf": sb("g_start", [128, CE]), "endf": sb("g_end", [128, CE]), "keep": sb("g_keep", [128, CE]),
             "chunk": sb("g_chunk", [1, 3, 128])}
        rows2 = lambda x: x.rearrange("(k p) -> k p", p=P)
        live = nc.dram_tensor("live_targets", (STEPS * P + 2,), F32, kind="Internal").ap()
        graph_phase(nc, con, g, rows2(a["src"]), rows2(a["dst"]), a["dst_e"], live)
        alpha = sb("alpha", [P, STEPS, H])

        tk, tv = dram("table_k", N, D), dram("table_v", N, D)
        dense_phase(nc, con, 1, X, None, acc, w["l1"], 4 * D, w["b1"], [(tk, D, 2 * D), (tv, 2 * D, 3 * D)])
        score_phase(nc, con, g, 1, alpha, None, tk, acc, a["attr_t"], w["we1"][:])
        softmax_phase(nc, con, g, 1, alpha, None)
        message_phase(nc, con, g, 1, X, alpha, None, tv, a["attr_t"], w["we1"][:])

        selfs, ntab = sb("selfs", [P, STEPS, H]), sb("node_scores", [P, NT, 2 * H])
        t2, a2 = dram("table_h2", N, D), dram("table_a2", N, H)
        dense_phase(nc, con, 2, X, None, ntab, w["l2"], D + 2 * H, None, [(t2, 0, D), (a2, D, D + H)])
        zero_phase(nc, acc, "zero_acc")
        score_phase(nc, con, g, 2, alpha, selfs, a2, ntab, None, None)
        softmax_phase(nc, con, g, 2, alpha, selfs)
        message_phase(nc, con, g, 2, acc, alpha, selfs, t2, None, None)
        attention_end_phase(nc, con, X, acc, t2, w["b2"])

        t3, a3 = dram("table_h3", N, D), dram("table_a3", N, H)
        dense_phase(nc, con, 3, X, acc, ntab, w["l3"], D + 2 * H, w["b3"], [(t3, 0, D), (a3, D, D + H)])
        score_phase(nc, con, g, 3, alpha, None, a3, ntab, a["attr_t"], w["we3"][:])
        softmax_phase(nc, con, g, 3, alpha, None)
        message_phase(nc, con, g, 3, acc, alpha, None, t3, None, None)
        final_phase(nc, con, X, acc, w["gamma"], w["beta"], out)


def kernel(**inp):
    import concourse.bacc as _bacc
    from concourse.bass_utils import run_bass_kernel_spmd as _run
    nc = _bacc.Bacc("TRN2", target_bir_lowering=False, num_devices=1)
    inp = {k: np.asarray(v) for k, v in inp.items()}
    row = lambda x: x.reshape(1, -1)
    tiles = lambda x: x.reshape(ET, P).T
    host = {
        "x": inp["x"], "src": inp["src"], "dst": inp["dst"],
        "src_e": tiles(inp["src"]), "dst_e": tiles(inp["dst"]), "w_e": tiles(inp["edge_weight"]),
        "attr_t": inp["edge_attr_64"].T,
        "w1": np.concatenate([inp[f"L1_gnn_W{k}"].T for k in ("q", "k", "v", "skip")], axis=1),
        "b1": np.concatenate([row(inp[f"L1_gnn_b{k}"]) for k in ("q", "k", "v", "skip")], axis=1),
        "we1": inp["L1_gnn_We"].T, "w2": inp["L2_gnn_W0"].T, "b2": row(inp["L2_gnn_b0"]),
        "l2s": row(inp["L2_gnn_att_src0"]), "l2d": row(inp["L2_gnn_att_dst0"]),
        "w3": inp["L3_gnn_W"], "we3": inp["L3_gnn_W_e"], "l3s": row(inp["L3_gnn_att_src"]), "l3d": row(inp["L3_gnn_att_dst"]),
        "l3e": row(inp["L3_gnn_att_edge"]), "b3": row(inp["L3_gnn_bias"]), "gamma": row(inp["L3_gnn_gamma"]),
        "beta": row(inp["L3_gnn_beta"]),
    }
    arrays, args = {}, {}
    for n, x in host.items():
        x = np.ascontiguousarray(x)
        arrays[f"in_{n}"] = x
        args[n] = nc.dram_tensor(f"in_{n}", x.shape, mybir.dt.from_np(x.dtype), kind="ExternalInput").ap()
    out = nc.dram_tensor("out_0", (N, D), F32, kind="ExternalOutput").ap()
    program(nc, args, out)
    r = _run(nc, [arrays], core_ids=[0])
    return r.results[0]["out_0"]
```

```python
from contextlib import ExitStack, contextmanager
import math

import numpy as np
import concourse.bass as bass
from concourse import mybir

F32 = mybir.dt.float32
I32 = mybir.dt.int32
BF16 = mybir.dt.bfloat16
ALU = mybir.AluOpType
ACT = mybir.ActivationFunctionType
AX = mybir.AxisListType

P = 125
N = 3125
NT = N // P
E = 50000
ET = E // P
D = 256
ED = 64
H = 8
C = D // H
ROT = 256

SLOT = 128
FILL = SLOT - 1
LIST_BLOCKS = -(-(2 * E // FILL + 10) // 8) * 8
FIELDS = 12
R1, R2, ALPHA, BETA, WR = range(5)
NEXT = 5
EVENT, SPARE = 10, 11
SKIP = float(1 << 20)
UB = 2
GROUPS = 512
SCATTER_TILES = 8
LEVELS = 7
TWO_PI_HI = 6.28125
TWO_PI_LO = 2 * math.pi - TWO_PI_HI
PI = 3.1415925


class Tally:

    def __init__(self, eng, sem, base=0):
        self.eng, self.sem, self.base, self.n = eng, sem, base, 0

    def up(self, ins):
        ins.then_inc(self.sem, 1)
        self.n += 1

    def then(self, ins):
        self.up(ins)
        self.eng.wait_ge(self.sem, self.base + self.n)


@contextmanager
def phase(nc):
    with ExitStack() as ph:
        taken = []

        def take(name):
            taken.append(nc.alloc_semaphore(name))
            return taken[-1]
        ph.sem = take
        yield ph
        nc.clear_and_free_semaphores(taken)
        nc.all_engine_barrier()


def peeled(eng, count, body):
    body(0)
    with eng.Fori(1, count) as i:
        body(i)


def opening(i):
    return isinstance(i, int) and i == 0


def pool_wait(pool, sem, value):
    pool.wait_ge(sem, value)
    pool.nop(nofuse=True)


def constants_phase(nc, con):
    with phase(nc) as ph:
        ii = ph.enter_context(nc.sbuf_tensor("c_iota_i", [128, 256], I32))
        pi = ph.enter_context(nc.sbuf_tensor("c_part_i", [128, 1], I32))
        made = ph.sem("c_made")
        dv = ph.sem("c_dve")
        with nc.Block() as block:
            @block.gpsimd
            def _(pool):
                pool.iota(ii[:], [[1, 256]], base=0, channel_multiplier=0).then_inc(made, 1)
                pool.iota(pi[:], [[1, 1]], base=0, channel_multiplier=1).then_inc(made, 1)

            @block.vector
            def _(dve):
                c = Tally(dve, dv)
                c.up(dve.memset(con["ones"][:], 1.0))
                dve.wait_ge(made, 2)
                c.up(dve.tensor_copy(con["iota"][:], ii[:]))
                c.then(dve.tensor_copy(con["part"][:, 0:1], pi[:]))
                c.up(dve.tensor_scalar(con["part"][:, 1:2], con["part"][:, 0:1], 128.0, None, ALU.add))
                c.up(dve.tensor_scalar(con["iota1"][:], con["iota"][:, 0:128], 1.0, None, ALU.add))
                c.up(dve.tensor_scalar(con["ident"][:], con["iota"][:, 0:128], con["part"][:, 0:1], None, ALU.is_equal))
                c.then(dve.tensor_scalar(con["after"][:], con["iota"][:, 0:128], con["part"][:, 0:1], None, ALU.is_gt))


def rotation_list_phase(nc, con, w_e, src_e, dst_e, rlist, pay, pos, due):
    with phase(nc) as ph:
        sb = lambda n, s, d=F32: ph.enter_context(nc.sbuf_tensor(n, s, d))
        sem = lambda n: ph.sem(n)
        ident, after, ones = con["ident"], con["after"], con["ones"]
        srcf, dstf, w = sb("l0_src", [P, ET]), sb("l0_dst", [P, ET]), sb("l0_w", [P, ET])
        srci, dsti = sb("l0_srci", [P, ET], I32), sb("l0_dsti", [P, ET], I32)
        ti = sb("l0_ti", [P, ET], I32)
        ta, tb, tc, act_, ev, ver, rolei = (sb(f"l0_{n}", [P, ET]) for n in ("ta", "tb", "tc", "active", "event", "ver", "rolei"))
        sn, cs = sb("l0_sin", [P, ET]), sb("l0_cos", [P, ET])
        pad = sb("l0_pad", [128, LIST_BLOCKS + 1, FIELDS])
        off, col, cnt = sb("l0_off", [1, ET]), sb("l0_col", [1, ET]), sb("l0_cnt", [1, 2])
        bound, needs = sb("l0_bound", [128, 1]), sb("l0_needs", [128, GROUPS // 128])
        early = sb("l0_early", [128, ET])
        ps_b = ph.enter_context(nc.psum_tensor("l0_psb", [128, 512], F32))
        ps_r = ph.enter_context(nc.psum_tensor("l0_psr", [128, GROUPS], F32))
        psq = ph.enter_context(nc.psum_tensor("l0_psq", [128, 512], F32))
        psc = ph.enter_context(nc.psum_tensor("l0_psc", [128, 512], F32))
        (loaded, padset, filled, dv, angles, waves, versions, offsets, counted, spread, needed, rowed) = (
            sem(f"l0_{n}") for n in ("loaded", "padset", "filled", "dve", "angles", "waves", "versions", "offsets",
                                     "counted", "spread", "needed", "rowed"))

        with nc.Block() as block:
            @block.sync
            def _(sp):
                sp.dma_start(srci[:], src_e).then_inc(loaded, 16)
                sp.dma_start(dsti[:], dst_e).then_inc(loaded, 16)
                sp.dma_start(w[:], w_e).then_inc(loaded, 16)
                sp.wait_ge(padset, 2)
                sp.dma_start(rlist.rearrange("(p n) f -> p (n f)", p=128),
                             pad[:].rearrange("p n f -> p (n f)")).then_inc(filled, 16)
                sp.wait_ge(filled, 16)

            @block.scalar
            def _(act):
                act.wait_ge(angles, 2)
                act.activation(sn[:], tb[:], ACT.Sin).then_inc(waves, 1)
                act.activation(cs[:], tc[:], ACT.Sin).then_inc(waves, 1)

            @block.tensor
            def _(pe):
                pe.wait_ge(versions, 1)
                pe.matmul(psc[0:1, 0:ET], ones[0:P, 0:1], ver[:], start=True, stop=True).then_inc(counted, 1)
                pe.matmul(psq[0:P, 0:ET], after[0:P, 0:P], ver[:], start=True, stop=False)
                pe.wait_ge(offsets, 1)
                pe.matmul(psq[0:P, 0:ET], ones[0:1, 0:P], off[:], start=False, stop=True).then_inc(counted, 1)
                pe.matmul(ps_b[:, 0:ET], ones[0:1, 0:128], off[:], start=True, stop=True).then_inc(spread, 1)
                pe.wait_ge(needed, 1)
                for j in range(GROUPS // 128):
                    mm = pe.transpose(ps_r[0:1, j * 128:j * 128 + 128], needs[:, j:j + 1], ident[:])
                mm.then_inc(rowed, 1)

            @block.vector
            def _(dve):
                c = Tally(dve, dv)
                dve.wait_ge(loaded, 48)
                c.up(dve.tensor_copy(srcf[:], srci[:]))
                c.then(dve.tensor_copy(dstf[:], dsti[:]))
                c.then(dve.tensor_tensor(ta[:], srcf[:], dstf[:], ALU.min))
                c.then(dve.tensor_scalar(act_[:], ta[:], float(ROT), None, ALU.is_lt))
                c.then(dve.tensor_tensor(ta[:], srcf[:], dstf[:], ALU.not_equal))
                c.then(dve.scalar_tensor_tensor(rolei[:], srcf[:], float(ROT), ta[:], ALU.is_lt, ALU.mult))
                c.then(dve.scalar_tensor_tensor(ev[:], dstf[:], float(ROT), rolei[:], ALU.is_lt, ALU.mult))
                c.up(dve.tensor_copy(pay[:, :, EVENT], ev[:]))
                dve.tensor_tensor(ver[:], act_[:], ev[:], ALU.add).then_inc(versions, 1)
                dve.wait_ge(counted, 1)
                c.then(dve.tensor_copy(col[:], psc[0:1, 0:ET]))
                c.then(dve.memset(ta[0:1, :], 1.0))
                c.then(dve.tensor_tensor_scan(off[:], ta[0:1, :], col[:], 0.0, ALU.mult, ALU.add))
                c.then(dve.tensor_copy(cnt[:, 0:1], off[:, ET - 1:ET]))
                dve.tensor_tensor(off[:], off[:], col[:], ALU.subtract).then_inc(offsets, 1)
                c.then(dve.tensor_scalar(cnt[:, 0:1], cnt[:, 0:1], 1.0 / (FILL * 2 * UB), 0.001, ALU.mult, ALU.add))
                c.then(dve.tensor_copy(con["rounds"][:], cnt[:, 0:1]))
                c.then(dve.tensor_copy(cnt[:, 1:2], con["rounds"][:]))
                c.then(dve.tensor_tensor(cnt[:, 0:1], cnt[:, 1:2], cnt[:, 0:1], ALU.is_gt))
                c.then(dve.tensor_tensor(cnt[:, 1:2], cnt[:, 1:2], cnt[:, 0:1], ALU.subtract))
                c.then(dve.tensor_scalar(cnt[:, 1:2], cnt[:, 1:2], 1.0, None, ALU.max))
                c.up(dve.tensor_copy(con["rounds"][:], cnt[:, 1:2]))
                dve.wait_ge(spread, 1)
                for j in range(GROUPS // 128):
                    c.then(dve.tensor_scalar(bound[:], con["part"][:, 0:1], float(UB * SLOT), float(UB * SLOT * (j * 128 + 1)), ALU.mult, ALU.add))
                    c.then(dve.scalar_tensor_tensor(early[:], ps_b[:, 0:ET], bound[:], con["ones"][:, 0:1].to_broadcast([128, ET]),
                                                    ALU.is_lt, ALU.mult, accum_out=needs[:, j:j + 1]))
                c.then(dve.tensor_scalar(needs[:], needs[:], 1.0 / SCATTER_TILES, 0.99, ALU.mult, ALU.add))
                dve.tensor_scalar(needs[:], needs[:], float(ET // SCATTER_TILES), None, ALU.min).then_inc(needed, 1)
                c.then(dve.tensor_scalar(ti[:], w[:], 1 / (2 * math.pi), None, ALU.mult))
                c.then(dve.tensor_copy(ta[:], ti[:]))
                c.then(dve.scalar_tensor_tensor(tb[:], ta[:], -TWO_PI_HI, w[:], ALU.mult, ALU.add))
                c.then(dve.scalar_tensor_tensor(tb[:], ta[:], -TWO_PI_LO, tb[:], ALU.mult, ALU.add))

                def wrap(x, bound, sign):
                    c.then(dve.tensor_scalar(ta[:], x, sign * PI, -sign * 2 * math.pi,
                                             ALU.is_gt if sign > 0 else ALU.is_lt, ALU.mult))
                    c.then(dve.tensor_tensor(x, x, ta[:], ALU.add))
                wrap(tb[:], PI, 1)
                wrap(tb[:], PI, -1)
                c.then(dve.tensor_scalar(tc[:], tb[:], math.pi / 2, None, ALU.add))
                wrap(tc[:], PI, 1)
                dve.tensor_scalar(tb[:], tb[:], PI, -PI, ALU.min, ALU.max).then_inc(angles, 1)
                dve.tensor_scalar(tc[:], tc[:], PI, -PI, ALU.min, ALU.max).then_inc(angles, 1)
                dve.wait_ge(counted, 2)
                c.then(dve.tensor_copy(ver[:], psq[0:P, 0:ET]))
                c.then(dve.tensor_scalar(ti[:], ver[:], 1.0 / FILL, None, ALU.mult))
                c.then(dve.tensor_copy(ta[:], ti[:]))
                c.then(dve.scalar_tensor_tensor(w[:], ta[:], float(FILL), ver[:], ALU.mult, ALU.is_gt))
                c.then(dve.tensor_tensor(ta[:], ta[:], w[:], ALU.subtract))
                c.then(dve.tensor_scalar(w[:], ta[:], float(FILL), float(FILL), ALU.mult, ALU.add))
                c.then(dve.tensor_tensor(w[:], w[:], ver[:], ALU.is_le))
                c.then(dve.tensor_tensor(ta[:], ta[:], w[:], ALU.add))
                c.then(dve.scalar_tensor_tensor(ta[:], ta[:], 1.0, ver[:], ALU.add, ALU.add))
                c.then(dve.tensor_scalar(w[:], act_[:], -SKIP, SKIP, ALU.mult, ALU.add))
                c.then(dve.tensor_tensor(ta[:], ta[:], w[:], ALU.add))
                c.up(dve.tensor_copy(pos[:], ta[:]))
                dve.wait_ge(rowed, 1)
                c.up(dve.tensor_copy(due[:], ps_r[0:1, :]))
                c.up(dve.tensor_scalar(pay[:, :, R1], srcf[:], float(ROT - 1), None, ALU.min))
                c.then(dve.tensor_scalar(pay[:, :, R2], dstf[:], float(ROT - 1), None, ALU.min))
                c.then(dve.tensor_tensor(ver[:], pay[:, :, R1], pay[:, :, R2], ALU.subtract))
                c.then(dve.tensor_tensor(ver[:], ver[:], rolei[:], ALU.mult))
                c.up(dve.tensor_tensor(pay[:, :, WR], ver[:], pay[:, :, R2], ALU.add))
                c.then(dve.tensor_scalar(w[:], rolei[:], -1.0, 1.0, ALU.mult, ALU.add))
                dve.wait_ge(waves, 2)
                c.up(dve.tensor_tensor(tb[:], cs[:], rolei[:], ALU.mult))
                c.then(dve.tensor_tensor(tc[:], sn[:], w[:], ALU.mult))
                c.then(dve.tensor_tensor(pay[:, :, ALPHA], tb[:], tc[:], ALU.add))
                c.up(dve.memset(pay[:, :, SPARE], 0.0))
                c.up(dve.tensor_tensor(pay[:, :, NEXT + ALPHA], sn[:], ev[:], ALU.mult))
                c.up(dve.tensor_tensor(pay[:, :, NEXT + BETA], cs[:], ev[:], ALU.mult))
                c.up(dve.tensor_tensor(pay[:, :, NEXT + R1], pay[:, :, R1], ev[:], ALU.mult))
                c.then(dve.tensor_tensor(pay[:, :, NEXT + R2], pay[:, :, R2], ev[:], ALU.mult))
                c.up(dve.tensor_tensor(pay[:, :, NEXT + WR], pay[:, :, NEXT + R2], ev[:], ALU.add))
                c.up(dve.tensor_tensor(tb[:], sn[:], rolei[:], ALU.mult))
                c.then(dve.tensor_tensor(tc[:], cs[:], w[:], ALU.mult))
                c.up(dve.tensor_tensor(pay[:, :, BETA], tc[:], tb[:], ALU.subtract))

            @block.gpsimd
            def _(pool):
                pool.memset(pad[:], 0.0).then_inc(padset, 1)
                pool.wait_ge(padset, 1)
                pool.memset(pad[:, :, WR], -1.0).then_inc(padset, 1)


def rotation_phase(nc, con, rlist, MT, pay, pos, due):
    with phase(nc) as ph:
        sb = lambda n, s, d=F32: ph.enter_context(nc.sbuf_tensor(n, s, d))
        sem = lambda n: ph.sem(n)
        ident, after, iota, iota1, part = (con[k] for k in ("ident", "after", "iota", "iota1", "part"))
        U = range(UB)
        cur, prev = sb("r_cur", [128, 2, UB, FIELDS]), sb("r_prev", [128, 2, UB, FIELDS])
        fld = sb("r_fld", [128, 2, UB, NEXT])
        reach, later, final = (sb(f"r_{n}", [128, UB]) for n in ("reach", "later", "final"))
        near, level_of, outer = (sb(f"r_{n}", [128, UB, 2]) for n in ("near", "key_at", "outer"))
        mask, late = sb("r_mask", [128, UB, 128]), sb("r_late", [128, UB, 128])
        key, lt = sb("r_key", [128, UB, 2, 128]), sb("r_lt", [128, UB, 2, 128])
        neu = sb("r_neu", [128, 2, UB, 3, 128])
        gat = sb("r_gat", [128, 2, UB, 2, 256])
        last = sb("r_last", [128, 2, UB, 256])
        owt = sb("r_owt", [128, 2, UB, 2, 128])
        ft, ub = sb("r_ft", [128, UB, 2, 128]), sb("r_ub", [128, UB, 256])
        M = sb("r_M", [128, 2, 256])
        psum = lambda n, w=512: ph.enter_context(nc.psum_tensor(n, [128, w], F32))
        ps_w = [psum(f"r_psw{p}") for p in range(2)]
        ps_n = [psum(f"r_psn{u}") for u in U]
        ps_a = psum("r_psa", 512 * UB)
        ps_m = psum("r_psm")
        dv = sem("r_dve")
        writes, rows, built, uset, zset, fset, fsub, vset, vcp, mset, applied, minit, tset = (
            sem(f"r_{n}") for n in ("writes", "rows", "built", "uset", "zset", "fset", "fsub", "vset", "vcp", "mset", "applied",
                                    "minit", "tset"))
        loaded = [sem(f"r_loaded{p}") for p in range(2)]
        pstage = sb("r_pstage", [P, 2, SCATTER_TILES, FIELDS])
        istage = sb("r_istage", [P, 2, SCATTER_TILES], I32)
        staged = sem("r_staged")
        scattered = [sem(f"r_scattered{g}") for g in range(2)]
        SCATTER_ROUNDS = ET // SCATTER_TILES
        level, evac = ([sem(f"r_{n}{u}") for u in U] for n in ("level", "evac"))
        VERSIONS_AFTER, ROWS_AFTER = (0, 4), (2, 5)
        STAGES = LEVELS + 1

        def count(eng):
            return eng.value_load(con["rounds"][0:1, 0:1], min_val=1, max_val=LIST_BLOCKS // (2 * UB) - 2)

        def following(i, p):
            return (i, 1) if p == 0 else (i + 1, 0)

        def started(i, p):
            return p == 1 or not opening(i)

        with nc.Block() as block:
            @block.sync
            def _(sp):
                def load(i, p):
                    rounds = sp.value_load(due[0:1, bass.ds(i * 2 + p, 1)], min_val=1, max_val=SCATTER_ROUNDS)
                    sp.wait_ge(staged, rounds * 2 + 4)
                    sp.nop(nofuse=True)
                    row = (i * 2 + p) * UB * SLOT
                    for buf, at in ((cur, row + 1), (prev, row)):
                        sp.dma_start(buf[:, p], rlist[bass.ds(at, UB * SLOT), :].rearrange("(u s) f -> s u f", u=UB)).then_inc(loaded[p], 16)
                load(0, 0)
                load(0, 1)

                def body(i):
                    for p in range(2):
                        sp.wait_ge(built, 2 * i + p + 1)
                        load(i + 1, p)
                more = count(sp)
                peeled(sp, more + 1, body)
                for p in range(2):
                    sp.wait_ge(loaded[p], more * 32 + 64)
                sp.nop(nofuse=True)

            @block.gpsimd
            def _(pool):
                def stage(r, h):
                    pool.tensor_copy(pstage[:, h], pay[:, bass.ds(r * SCATTER_TILES, SCATTER_TILES), :]).then_inc(staged, 1)
                    pool.tensor_copy(istage[:, h], pos[:, bass.ds(r * SCATTER_TILES, SCATTER_TILES)]).then_inc(staged, 1)

                def body(i, final=False):
                    for h in range(2):
                        r = 2 * i + h
                        pool_wait(pool, staged, r * 2 + 2)
                        for u in range(SCATTER_TILES):
                            if u == SCATTER_TILES // 2:
                                if h or not opening(i):
                                    pool_wait(pool, scattered[1 - h], 16 * SCATTER_TILES * (i + h))
                                if not (final and h):
                                    stage(r + 1, 1 - h)
                            pool.indirect_dma_start(
                                out=rlist, out_offset=bass.IndirectOffsetOnAxis(ap=istage[:, h, u:u + 1], axis=0),
                                in_=pstage[:, h, u, :], in_offset=None, bounds_check=LIST_BLOCKS * SLOT + SLOT - 1,
                                oob_is_err=False).then_inc(scattered[h], 16)
                assert SCATTER_ROUNDS % 2 == 0
                stage(0, 0)
                body(0)
                with pool.Fori(1, SCATTER_ROUNDS // 2 - 1) as i:
                    body(i)
                body(SCATTER_ROUNDS // 2 - 1, final=True)
                for g in range(2):
                    pool.wait_ge(scattered[g], 8 * SCATTER_TILES * SCATTER_ROUNDS)
                pool.sem_inc(staged, 4)

            @block.vector
            def _(dve):
                STEPS_OF = 27
                start = 1

                def fields(c, i, p):
                    dve.wait_ge(loaded[p], i * 32 + 32)
                    dve.tensor_tensor(fld[:, p], cur[:, p, :, 0:NEXT], prev[:, p, :, NEXT:2 * NEXT], ALU.add).then_inc(writes, 1)
                    c.then(dve.tensor_scalar(reach[:], prev[:, p, :, EVENT], -1.0, part[:, 0:1], ALU.mult, ALU.add))
                    for u in U:
                        c.up(dve.scalar_tensor_tensor(mask[:, u, :], iota[:, 0:128], reach[:, u:u + 1], iota1[:], ALU.is_lt, ALU.mult))

                def references(c, i, p):
                    dve.wait_ge(writes, 2 * i + p + 1)
                    dve.wait_ge(rows, 2 * i + p + 1)
                    dve.wait_ge(dv, c.base + c.n)
                    for u in U:
                        W = ps_w[p][:, u * 128:u * 128 + 128]
                        f = fld[:, p, u, :]
                        for o in range(2):
                            c.up(dve.scalar_tensor_tensor(key[:, u, o, :], W, f[:, R1 + o:R1 + o + 1], mask[:, u, :], ALU.is_equal, ALU.mult))
                        c.up(dve.scalar_tensor_tensor(late[:, u, :], W, f[:, WR:WR + 1], after[:], ALU.is_equal, ALU.mult,
                                                      accum_out=later[:, u:u + 1]))
                    dve.wait_ge(dv, c.base + c.n)
                    c.up(dve.tensor_reduce(near[:], key[:], AX.X, ALU.max))
                    for u in U:
                        for h in range(2):
                            c.up(dve.tensor_scalar(owt[:, p, u, h, :], ps_w[p][:, u * 128:u * 128 + 128], part[:, h:h + 1], None, ALU.is_equal))
                    dve.wait_ge(dv, c.base + c.n)
                    c.up(dve.tensor_scalar(level_of[:], near[:], 0.5, None, ALU.max))
                    c.up(dve.scalar_tensor_tensor(outer[:], near[:], 0.5, fld[:, p, :, ALPHA:BETA + 1], ALU.is_lt, ALU.mult))
                    c.then(dve.tensor_scalar(final[:], later[:], 0.5, None, ALU.is_lt))

                def matrices(c, i, p):
                    for u in U:
                        f = fld[:, p, u, :]
                        for o in range(2):
                            c.up(dve.tensor_scalar(lt[:, u, o, :], key[:, u, o, :], level_of[:, u, o:o + 1], f[:, ALPHA + o:ALPHA + o + 1],
                                                   ALU.is_equal, ALU.mult))
                        for o in range(2):
                            c.up(dve.tensor_scalar(gat[:, p, u, o, :], iota[:], f[:, R1 + o:R1 + o + 1], outer[:, u, o:o + 1],
                                                   ALU.is_equal, ALU.mult))
                    dve.wait_ge(dv, c.base + c.n)
                    dve.tensor_tensor(neu[:, p, :, 2, :], lt[:, :, 0, :], lt[:, :, 1, :], ALU.add)
                    dve.tensor_tensor(gat[:, p, :, 0, :], gat[:, p, :, 0, :], gat[:, p, :, 1, :], ALU.add).then_inc(built, 1)

                def lasts(c, i, p):
                    for u in U:
                        c.up(dve.tensor_scalar(last[:, p, u, :], iota[:], fld[:, p, u, WR:WR + 1], final[:, u:u + 1], ALU.is_equal, ALU.mult))

                def changes(m, q):
                    dve.wait_ge(fset, m + 1)
                    dve.tensor_tensor(ft[:], ps_a[:].rearrange("p (u x) -> p u x", u=UB)[:, :, 0:256].rearrange("p u (h t) -> p u h t", h=2),
                                      owt[:, q], ALU.subtract).then_inc(fsub, 1)

                def add(m, u):
                    at = m * UB + u + 1
                    dve.wait_ge(mset, at)
                    dve.tensor_tensor(M[:], M[:], ps_m[:].rearrange("p (h c) -> p h c", h=2), ALU.add).then_inc(applied, 1)
                    dve.wait_ge(applied, at)

                def build(c, i, p):
                    fields(c, i, p)
                    references(c, i, p)
                    matrices(c, i, p)
                    lasts(c, i, p)

                def body(i):
                    for p in range(2):
                        n = 2 * i + p
                        j, q = following(i, p)
                        c = Tally(dve, dv, (n + 1) * STEPS_OF + start)
                        if started(i, p):
                            changes(n - 1, q)
                        fields(c, j, q)
                        for u in U:
                            dve.wait_ge(evac[u], n * STAGES + 1)
                        dve.tensor_tensor(neu[:, p, :, 0, :], neu[:, p, :, 1, :], ident[:].unsqueeze(1).to_broadcast([128, UB, 128]), ALU.add).then_inc(zset, 1)
                        references(c, j, q)
                        if started(i, p):
                            add(n - 1, 0)
                        matrices(c, j, q)
                        if started(i, p):
                            for u in range(1, UB):
                                add(n - 1, u)
                        lasts(c, j, q)
                        assert c.n == STEPS_OF, c.n

                dve.memset(M[:], 0.0).then_inc(dv, 1)
                dve.wait_ge(dv, 1)
                dve.tensor_copy(M[:, 0, 0:128], ident[:])
                dve.tensor_copy(M[:, 1, 128:256], ident[:]).then_inc(minit, 1)
                dve.wait_ge(minit, 1)
                build(Tally(dve, dv, start), 0, 0)
                more = count(dve)
                peeled(dve, more + 1, body)
                changes(2 * more + 1, 1)
                for u in U:
                    add(2 * more + 1, u)
                dve.wait_ge(tset, 1)
                dve.tensor_copy(MT[:], ps_w[0][:].rearrange("p (h c) -> p h c", h=2)).then_inc(tset, 1)

            @block.scalar
            def _(act):
                def changed(m, u):
                    act.wait_ge(vset, m * UB + u + 1)
                    act.copy(ub[:, u, :], ps_a[:, u * 512 + 256:u * 512 + 512]).then_inc(vcp, 1)

                def body(i):
                    for p in range(2):
                        n = 2 * i + p
                        act.wait_ge(uset, n + 1)
                        for u in U:
                            act.copy(neu[:, p, u, 1, :], ps_w[p][:, 256 + u * 128:384 + u * 128]).then_inc(evac[u], 1)
                        for k in range(LEVELS):
                            parts = slice(1, 3) if k == 0 else slice(0, 1) if k == LEVELS - 1 else slice(0, 3, 2) if k == LEVELS - 2 else slice(0, 3)
                            if k == 0:
                                act.wait_ge(zset, n + 1)
                            for u in U:
                                act.wait_ge(level[u], n * LEVELS + k + 1)
                                act.copy(neu[:, p, u, parts, :], ps_n[u][:, 0:384].rearrange("p (a c) -> p a c", a=3)[:, parts, :]).then_inc(evac[u], 1)
                            if started(i, p) and k in VERSIONS_AFTER:
                                changed(n - 1, VERSIONS_AFTER.index(k))
                more = count(act)
                peeled(act, more + 1, body)
                for u in U:
                    changed(2 * more + 1, u)

            @block.tensor
            def _(pe):
                def written(i, p):
                    pe.wait_ge(writes, 2 * i + p + 1)
                    for u in U:
                        mm = pe.matmul(ps_w[p][:, u * 128:u * 128 + 128], fld[:, p, u, WR:WR + 1].to_broadcast([128, 128]), ident[:],
                                       start=True, stop=True)
                    mm.then_inc(rows, 1)

                def raise_level(n, p, k):
                    for u in U:
                        pe.wait_ge(evac[u], n * STAGES + k + 1)
                        z, up, lo = (neu[:, p, u, x, :] for x in range(3))
                        to = [ps_n[u][:, x * 128:x * 128 + 128] for x in range(3)]
                        if k:
                            pe.matmul(to[0], lo, z, start=True, stop=False)
                            mm = pe.matmul(to[0], ident[:], z, start=False, stop=True)
                        if k < LEVELS - 2:
                            pe.matmul(to[1], lo, up, start=True, stop=True)
                        if k < LEVELS - 1:
                            mm = pe.matmul(to[2], up, lo, start=True, stop=True)
                        mm.then_inc(level[u], 1)

                def versions(m, u, fresh=False):
                    pe.wait_ge(fsub, m + 1)
                    if not fresh:
                        pe.wait_ge(applied, m * UB + u)
                    for h in range(2):
                        mm = pe.matmul(ps_a[:, u * 512 + 256:u * 512 + 512], ft[:, u, h, :], M[:, h, :], start=(h == 0), stop=(h == 1))
                    mm.then_inc(vset, 1)

                def rows_of(m, q, u):
                    pe.wait_ge(vcp, m * UB + u + 1)
                    for h in range(2):
                        mm = pe.matmul(ps_m[:, h * 256:h * 256 + 256], last[:, q, u, h * 128:h * 128 + 128], ub[:, u, :], start=True, stop=True)
                    mm.then_inc(mset, 1)

                def body(i):
                    for p in range(2):
                        n = 2 * i + p
                        pe.wait_ge(built, n + 1)
                        for u in U:
                            mm = pe.transpose(ps_w[p][:, 256 + u * 128:384 + u * 128], neu[:, p, u, 2, :], ident[:])
                        mm.then_inc(uset, 1)
                        for k in range(LEVELS):
                            if k == 1:
                                pe.wait_ge(zset, n + 1)
                            raise_level(n, p, k)
                            if k == 0:
                                written(*following(i, p))
                            if started(i, p) and k in VERSIONS_AFTER:
                                u = VERSIONS_AFTER.index(k)
                                versions(n - 1, u, fresh=opening(i) and u == 0)
                            if started(i, p) and k in ROWS_AFTER:
                                rows_of(n - 1, 1 - p, ROWS_AFTER.index(k))
                        for u in U:
                            pe.wait_ge(evac[u], (n + 1) * STAGES)
                            for h in range(2):
                                mm = pe.matmul(ps_a[:, u * 512 + h * 128:u * 512 + h * 128 + 128], gat[:, p, u, 0, h * 128:h * 128 + 128],
                                               neu[:, p, u, 0, :], start=True, stop=True)
                        mm.then_inc(fset, 1)
                more = count(pe)
                written(0, 0)
                pe.wait_ge(minit, 1)
                peeled(pe, more + 1, body)
                for u in U:
                    versions(2 * more + 1, u)
                    rows_of(2 * more + 1, 1, u)
                pe.wait_ge(applied, 2 * UB * more + 2 * UB)
                for a in range(2):
                    for b in range(2):
                        mm = pe.transpose(ps_w[0][:, a * 256 + b * 128:a * 256 + b * 128 + 128], M[:, b, a * 128:a * 128 + 128], ident[:])
                mm.then_inc(tset, 1)


PAIR = 2
USED = (ET // PAIR + NT - 1) * PAIR
CH = 16
STEPS = USED
assert STEPS % (4 * CH) == 0
SQ = STEPS // 4
CT = STEPS // CH
CE = CT * P
BIG = 2.0 ** 90
AW = 272
G = 4
GP = G // PAIR
ROUND = 4
STAIRS = ROUND * GP
WORDS = STEPS // (ROUND * G)
FIELD_AT = [0]
for _stair in range(1, STAIRS):
    FIELD_AT.append(5 if _stair == 1 else FIELD_AT[-1] + (_stair - 1).bit_length())
assert NT <= 32 and FIELD_AT[-1] + (STAIRS - 1).bit_length() <= 24
EPS = 1e-5


def graph_phase(nc, con, g, src2, dst2, dst_e, live, rows, loads):
    with phase(nc) as ph:
        sb = lambda n, s, d=F32: ph.enter_context(nc.sbuf_tensor(n, s, d))
        sem = lambda n: ph.sem(n)
        ident, ones, part = con["ident"], con["ones"], con["part"]
        B = NT - 1
        lasti, lastf, lt = sb("g_lasti", [B, ET], I32), sb("g_lastf", [B, ET]), sb("g_lt", [B, ET // PAIR])
        cut = sb("g_cut", [B, 4])
        stepi, stepf, comp = sb("g_stepi", [B, STEPS], I32), sb("g_stepf", [B, STEPS]), sb("g_comp", [B, STEPS])
        trow = sb("g_trow", [1, STEPS])
        away = sb("g_away", [1, WORDS, STAIRS])
        lv, la = sb("g_lv", [SQ, 4, P]), sb("g_la", [SQ, 4, P])
        minus = sb("g_minus", [1, 2])
        tcol, kcol, kidx = sb("g_tcol", [SQ, 4]), sb("g_kcol", [SQ, 4]), sb("g_kidx", [SQ, 4], I32)
        got, gf = sb("g_got", [SQ, 2, 4, P], I32), sb("g_gf", [SQ, 2, 4, P])
        places = sb("g_places", [SQ, 2, 4, P], BF16)
        tq, tr, tw = (sb(f"g_t{n}", [SQ, 4, P]) for n in "qrw")
        tqi = sb("g_tqi", [SQ, 4, P], I32)
        dn = sb("g_dn", [128, CE + 2])
        flag = sb("g_flag", [128, 2])
        ps_t = ph.enter_context(nc.psum_tensor("g_pst", [128, 512], F32))
        ps_c = ph.enter_context(nc.psum_tensor("g_psc", [128, 512], F32))
        ps_x = [ph.enter_context(nc.psum_tensor(f"g_psx{a}", [128, 512], F32)) for a in range(3)]
        ps_f = ph.enter_context(nc.psum_tensor("g_psf", [128, 512], F32))
        dv, iot, loaded, dset, compared, counted, kset, gathered, turned, flagged, flagrow = (
            sem(f"g_{n}") for n in ("dve", "iota", "loaded", "dset", "compared", "counted", "kset", "gathered",
                                    "turned", "flagged", "flagrow"))
        lived, written, divided, brought = sem("g_lived"), sem("g_written"), sem("g_divided"), sem("g_brought")
        with nc.Block() as block:
            @block.sync
            def _(sp):
                sp.dma_start(lasti[:], dst_e[P - 1:P, :].to_broadcast([B, ET])).then_inc(loaded, 16)
                for to, at in loads:
                    sp.dma_start(to, at).then_inc(brought, 16)
                sp.wait_ge(brought, 16 * len(loads))
                sp.wait_ge(lived, 1)
                body = live[1:1 + STEPS * P].rearrange("(j p e) -> p j e", j=4, e=P)
                sp.dma_start(body, lv[:]).then_inc(written, 16)
                ends = bass.AP(live.tensor, live.offset, [[STEPS * P + 2, 1], [STEPS * P + 1, 2], [1, 1]])
                sp.dma_start(ends, minus[:].rearrange("a (b c) -> a b c", c=1), allow_slow_non_contiguous=True).then_inc(written, 16)
                sp.wait_ge(written, 32)
                sp.wait_ge(divided, 1)
                for a in range(2):
                    spread = bass.AP(rows.tensor, rows.offset + a * P, [[2 * P, SQ], [SQ * 2 * P, 4], [1, P]])
                    sp.dma_start(spread, places[:, a]).then_inc(written, 16)
                sp.wait_ge(written, 64)
                windows = bass.AP(live.tensor, live.offset, [[CE, CH], [1, CE + 2]])
                for h in range(H):
                    sp.dma_start(dn[h:128 - H + h + 1:H, :], windows).then_inc(dset, 16)

            @block.gpsimd
            def _(pool):
                pool.iota(stepi[:].rearrange("b (i j) -> b i j", j=PAIR), [[1, STEPS // PAIR], [0, PAIR]], base=0, channel_multiplier=0).then_inc(iot, 1)
                pool.wait_ge(kset, 1)
                for j in range(4):
                    for a, table in enumerate((src2, dst2)):
                        pool.indirect_dma_start(out=got[:, a, j, :], out_offset=None, in_=table,
                                                in_offset=bass.IndirectOffsetOnAxis(ap=kidx[:, j:j + 1], axis=0)).then_inc(gathered, 16)

            @block.tensor
            def _(pe):
                pe.wait_ge(compared, 1)
                pe.matmul(ps_t[0:1, 0:STEPS], ones[0:B, 0:1], comp[:], start=True, stop=True)
                for j in range(4):
                    mm = pe.matmul(ps_c[0:SQ, j:j + 1], comp[:, j * SQ:(j + 1) * SQ], ones[0:B, 0:1], start=True, stop=True)
                mm.then_inc(counted, 1)
                pe.wait_ge(divided, 1)
                for a, x in enumerate((gf[:, 0], gf[:, 1], tq[:])):
                    for j in range(4):
                        mm = pe.transpose(ps_x[a][0:P, j * SQ:(j + 1) * SQ], x[:, j, :], ident[0:SQ, 0:SQ])
                mm.then_inc(turned, 1)
                pe.wait_ge(flagged, 1)
                for a in range(2):
                    mm = pe.transpose(ps_f[0:1, a * 128:a * 128 + 128], flag[:, a:a + 1], ident[:])
                mm.then_inc(flagrow, 1)

            @block.vector
            def _(dve):
                c = Tally(dve, dv)
                c.up(dve.memset(minus[:], -1.0))
                dve.wait_ge(loaded, 16)
                dve.wait_ge(iot, 1)
                c.up(dve.tensor_copy(stepf[:], stepi[:]))
                c.then(dve.tensor_copy(lastf[:], lasti[:]))
                c.then(dve.tensor_scalar(cut[:, 0:1], part[0:B, 0:1], float(P), float(P), ALU.mult, ALU.add))
                c.then(dve.tensor_scalar(lt[:], lastf[:, PAIR - 1::PAIR], cut[:, 0:1], None, ALU.is_lt))
                c.then(dve.tensor_reduce(cut[:, 1:2], lt[:], AX.X, ALU.add))
                c.then(dve.tensor_scalar(cut[:, 2:3], cut[:, 1:2], float(ET // PAIR - 1), part[0:B, 0:1], ALU.min, ALU.add))
                dve.tensor_scalar(comp[:], stepf[:], cut[:, 2:3], None, ALU.is_gt).then_inc(compared, 1)
                dve.wait_ge(counted, 1)
                c.up(dve.tensor_copy(trow[:], ps_t[0:1, 0:STEPS]))
                c.then(dve.tensor_copy(tcol[:], ps_c[0:SQ, 0:4]))
                c.then(dve.tensor_scalar(kcol[:], tcol[:], -float(PAIR), None, ALU.mult))
                for j in range(4):
                    c.up(dve.tensor_scalar(kcol[:, j:j + 1], kcol[:, j:j + 1], part[0:SQ, 0:1], float(j * SQ), ALU.add, ALU.add))
                dve.wait_ge(dv, c.n)
                c.then(dve.tensor_scalar(kcol[:], kcol[:], float(ET - 1), None, ALU.min))
                dve.tensor_copy(kidx[:], kcol[:]).then_inc(kset, 1)
                tg = trow[:].rearrange("a (r j) -> a r j", j=PAIR * STAIRS)[:, :, ::PAIR]
                c.then(dve.tensor_tensor(away[:], tg, tg[:, :, 0:1].to_broadcast([1, WORDS, STAIRS]), ALU.subtract))
                for j in range(STAIRS - 1, 0, -1):
                    below = away[:, :, j - 1] if j > 1 else tg[:, :, 0]
                    scale = float(1 << (FIELD_AT[j] - (FIELD_AT[j - 1] if j > 1 else 0)))
                    c.then(dve.scalar_tensor_tensor(away[:, :, j - 1], away[:, :, j], scale, below, ALU.mult, ALU.add))
                c.then(dve.tensor_copy(g["stairs"][:], away[:, :, 0]))
                dve.wait_ge(gathered, 128)
                c.then(dve.tensor_copy(gf[:], got[:]))
                c.up(dve.tensor_scalar(lv[:], gf[:, 1], 1.0, None, ALU.add))
                c.then(dve.tensor_scalar(kcol[:], tcol[:], -float(P), None, ALU.mult))
                for j in range(4):
                    c.up(dve.tensor_scalar(gf[:, 1, j, :], gf[:, 1, j, :], kcol[:, j:j + 1], None, ALU.add))
                dve.wait_ge(dv, c.n)
                c.then(dve.tensor_scalar(la[:], gf[:, 1], 0.0, None, ALU.is_ge))
                c.then(dve.scalar_tensor_tensor(la[:], gf[:, 1], float(P), la[:], ALU.is_lt, ALU.mult))
                c.then(dve.tensor_tensor(lv[:], lv[:], la[:], ALU.mult))
                dve.tensor_scalar(lv[:], lv[:], 1.0, None, ALU.subtract).then_inc(lived, 1)
                c.then(dve.tensor_scalar(tqi[:], gf[:, 0], 1.0 / P, None, ALU.mult))
                c.then(dve.tensor_copy(tq[:], tqi[:]))
                c.then(dve.scalar_tensor_tensor(tr[:], tq[:], -float(P), gf[:, 0], ALU.mult, ALU.add))
                c.then(dve.tensor_scalar(tw[:], tr[:], 0.0, None, ALU.is_lt))
                c.then(dve.tensor_tensor(tq[:], tq[:], tw[:], ALU.subtract))
                c.then(dve.scalar_tensor_tensor(tr[:], tw[:], float(P), tr[:], ALU.mult, ALU.add))
                c.then(dve.tensor_scalar(tw[:], tr[:], float(P), None, ALU.is_ge))
                c.then(dve.tensor_tensor(tq[:], tq[:], tw[:], ALU.add))
                c.then(dve.scalar_tensor_tensor(tr[:], tw[:], -float(P), tr[:], ALU.mult, ALU.add))
                c.up(dve.tensor_copy(places[:, 0], tr[:]))
                dve.tensor_copy(places[:, 1], gf[:, 1]).then_inc(divided, 1)
                dve.wait_ge(dset, 16 * H)
                c.up(dve.tensor_tensor(g["startf"][:], dn[:, 1:CE + 1], dn[:, 0:CE], ALU.not_equal))
                c.then(dve.tensor_tensor(g["endf"][:], dn[:, 1:CE + 1], dn[:, 2:CE + 2], ALU.not_equal))
                c.up(dve.tensor_scalar(g["keep"][:], g["startf"][:], -1.0, 1.0, ALU.mult, ALU.add))
                c.up(dve.tensor_scalar(g["endf"][:], g["endf"][:], -BIG, None, ALU.mult))
                dve.wait_ge(dv, c.n)
                c.then(dve.tensor_scalar(g["startf"][:], g["startf"][:], -BIG, None, ALU.mult))
                c.up(dve.tensor_reduce(flag[:, 0:1], g["startf"][:], AX.X, ALU.min))
                dve.tensor_reduce(flag[:, 1:2], g["endf"][:], AX.X, ALU.min).then_inc(flagged, 1)
                dve.wait_ge(turned, 1)
                c.up(dve.tensor_copy(g["srcs"][:], ps_x[0][0:P, 0:STEPS]))
                c.up(dve.tensor_copy(g["dstl"][:], ps_x[1][0:P, 0:STEPS]))
                c.up(dve.tensor_copy(g["src_tile"][:], ps_x[2][0:P, 0:STEPS]))
                dve.wait_ge(flagrow, 1)
                row = g["chunk"]
                for a in range(2):
                    c.up(dve.tensor_copy(row[:, a].rearrange("a (h c) -> a h c", h=H),
                                         ps_f[0:1, a * 128:a * 128 + 128].rearrange("a (c h) -> a h c", h=H)))
                dve.wait_ge(dv, c.n)
                c.up(dve.memset(row[:, 0].rearrange("a (h c) -> a h c", h=H)[:, :, 0:1], -BIG))
                c.then(dve.memset(row[:, 1].rearrange("a (h c) -> a h c", h=H)[:, :, CH - 1:CH], -BIG))
                c.then(dve.tensor_scalar(row[:, 2], row[:, 0], 1.0 / BIG, 1.0, ALU.mult, ALU.add))


def dense_phase(nc, con, layer, X, acc, ntab, weight, width, bias, tables):
    U = 5
    with phase(nc) as ph:
        sb = lambda n, s, d=F32: ph.enter_context(nc.sbuf_tensor(f"d{layer}_{n}", s, d))
        sem = lambda n: ph.sem(f"d{layer}_{n}")
        ident = con["ident"]
        st = sb("st", [P, NT, 6])
        mean, dif, var, rstd, nb = (sb(n, [P, NT]) for n in ("mean", "dif", "var", "rstd", "nb"))
        hn, ht = sb("hn", [P, U, D]), sb("ht", [128, U, 2, P])
        stage = sb("stage", [P, U, width])
        banks = -(-width // 512)
        ps_t = [ph.enter_context(nc.psum_tensor(f"d{layer}_pst{b}", [128, 512], F32)) for b in range(2)]
        ps_o = [ph.enter_context(nc.psum_tensor(f"d{layer}_pso{b}", [128, 512 * banks], F32)) for b in range(3)]
        dv, spread, rooted, ready, hset, tset, tcopied, mmdone, evac = (
            sem(n) for n in ("dve", "spread", "rooted", "ready", "hset", "tset", "tcopied", "mmdone", "evac"))
        stored = [sem(f"stored{u}") for u in range(U)]
        stores = len(tables)
        with nc.Block() as block:
            @block.vector
            def _(dve):
                with dve.Fori(0, NT) as n:
                    dve.bn_stats(st[:, bass.ds(n, 1), :].rearrange("p a s -> p (a s)"),
                                 X[:, bass.ds(n, 1), :].rearrange("p a d -> p (a d)")).then_inc(dv, 1)
                dve.wait_ge(dv, NT)
                c = Tally(dve, dv, NT)
                me, mo = st[:, :, 1], st[:, :, 4]
                c.up(dve.tensor_tensor(mean[:], me, mo, ALU.add))
                c.up(dve.tensor_tensor(dif[:], me, mo, ALU.subtract))
                c.then(dve.tensor_tensor(var[:], st[:, :, 2], st[:, :, 5], ALU.add))
                c.up(dve.tensor_scalar(mean[:], mean[:], 0.5, None, ALU.mult))
                c.then(dve.scalar_tensor_tensor(dif[:], dif[:], 0.25, dif[:], ALU.mult, ALU.mult))
                c.then(dve.scalar_tensor_tensor(var[:], var[:], 1.0 / D, dif[:], ALU.mult, ALU.add))
                dve.tensor_scalar(var[:], var[:], EPS, None, ALU.add).then_inc(spread, 1)
                dve.wait_ge(rooted, 1)
                c.then(dve.reciprocal(rstd[:], dif[:]))
                dve.scalar_tensor_tensor(nb[:], mean[:], -1.0, rstd[:], ALU.mult, ALU.mult).then_inc(ready, 1)

                def body(i):
                    for u in range(U):
                        n = i * U + u
                        x = X[:, bass.ds(n, 1), :].rearrange("p a d -> p (a d)")
                        dve.wait_ge(mmdone, n + 1)
                        if stores and not isinstance(i, int):
                            dve.wait_ge(stored[u], 16 * stores * i)
                        o = ps_o[u % 3][0:P, 0:width]
                        if layer == 0:
                            dve.tensor_tensor(x, x, o, ALU.add).then_inc(evac, 1)
                        elif layer == 1:
                            dve.tensor_tensor(stage[:, u, :], o, bias[:], ALU.add).then_inc(evac, 1)
                            dve.wait_ge(evac, n + 1)
                            dve.tensor_copy(ntab[:, bass.ds(n, 1), 0:D].rearrange("p a d -> p (a d)"), stage[:, u, 0:D]).then_inc(dv, 1)
                            dve.tensor_tensor(x, x, stage[:, u, 3 * D:4 * D], ALU.add).then_inc(dv, 1)
                        else:
                            if layer == 3:
                                dve.tensor_tensor(acc[:, bass.ds(n, 1), 0:D].rearrange("p a d -> p (a d)"), hn[:, u, :], bias[:], ALU.add).then_inc(dv, 1)
                            dve.tensor_copy(stage[:, u, :], o).then_inc(evac, 1)
                            dve.wait_ge(evac, n + 1)
                            dve.tensor_copy(ntab[:, bass.ds(n, 1), 0:H].rearrange("p a d -> p (a d)"), stage[:, u, D + H:]).then_inc(dv, 1)
                            dve.tensor_copy(ntab[:, bass.ds(n, 1), 2 * H:3 * H].rearrange("p a d -> p (a d)"), stage[:, u, D:D + H]).then_inc(dv, 1)
                            if layer == 2:
                                dve.tensor_tensor(ntab[:, bass.ds(n, 1), H:2 * H].rearrange("p a d -> p (a d)"), stage[:, u, D + H:],
                                                  stage[:, u, D:D + H], ALU.add).then_inc(dv, 1)
                dve.wait_ge(ready, 1)
                peeled(dve, NT // U, body)

            @block.scalar
            def _(act):
                act.wait_ge(spread, 1)
                act.activation(dif[:], var[:], ACT.Sqrt).then_inc(rooted, 1)
                act.wait_ge(ready, 1)

                def body(i):
                    for u in range(U):
                        n = i * U + u
                        if not isinstance(i, int):
                            act.wait_ge(evac, n - U + 1)
                        act.activation(hn[:, u, :], X[:, bass.ds(n, 1), :].rearrange("p a d -> p (a d)"), ACT.Relu,
                                       bias=nb[:, bass.ds(n, 1)], scale=rstd[:, bass.ds(n, 1)]).then_inc(hset, 1)
                    for u in range(U):
                        n = i * U + u
                        act.wait_ge(tset, n + 1)
                        act.copy(ht[:, u], ps_t[u % 2][:, 0:2 * P].rearrange("p (a m) -> p a m", a=2)).then_inc(tcopied, 1)
                peeled(act, NT // U, body)

            @block.tensor
            def _(pe):
                def turn(i, u):
                    n = i * U + u
                    pe.wait_ge(hset, n + 1)
                    if u >= 2 or not isinstance(i, int):
                        pe.wait_ge(tcopied, n if u == 0 else n - 1)
                    for a in range(2):
                        mm = pe.transpose(ps_t[u % 2][:, a * P:(a + 1) * P], hn[:, u, a * 128:(a + 1) * 128], ident[0:P, 0:P])
                    mm.then_inc(tset, 1)

                def multiply(i, u):
                    n = i * U + u
                    pe.wait_ge(tcopied, n + 1)
                    if u >= 3 or not isinstance(i, int):
                        pe.wait_ge(evac, n - 2 if u >= 3 else n - 1)
                    for lo in range(0, width, 512):
                        hi = min(width, lo + 512)
                        for a in range(2):
                            mm = pe.matmul(ps_o[u % 3][0:P, lo:hi], ht[:, u, a, :], weight[:, a, lo:hi], start=(a == 0), stop=(a == 1))
                    mm.then_inc(mmdone, 1)

                def body(i):
                    for u in range(U):
                        turn(i, u)
                        if u:
                            multiply(i, u - 1)
                    multiply(i, U - 1)
                peeled(pe, NT // U, body)

            if stores:
                @block.sync
                def _(sp):
                    def body(i):
                        for u in range(U):
                            n = i * U + u
                            sp.wait_ge(evac, n + 1)
                            for table, lo, hi in tables:
                                sp.dma_start(table[bass.ds(n * P, P), :], stage[:, u, lo:hi]).then_inc(stored[u], 16)
                    peeled(sp, NT // U, body)
                    for u in range(U):
                        sp.wait_ge(stored[u], 16 * stores * (NT // U))


def load_stairs(eng, g, at):
    return eng.value_load(g["stairs"][0:1, bass.ds(at, 1)], min_val=0, max_val=(1 << 24) - 1)


def behind(word, j):
    return (word >> FIELD_AT[j]) & ((1 << j.bit_length()) - 1)


def node_tiles(nc, word, b):
    first = word & 31
    tiles = [first + behind(word, j) if j else first for j in range(b * GP, b * GP + GP)]
    return [nc.s_assert_within(t, 0, NT - 1, skip_runtime_bounds_check_because="a count of NT - 1 borders") for t in tiles]


def load_attributes(nc, sp, i, b, word, attr, attr_t, done):
    first = (i * STAIRS - (word & 31)) * (PAIR * P)
    for v in range(GP):
        j = b * GP + v
        edge = first + j * PAIR * P if j == 0 else first + j * PAIR * P - behind(word, j) * (PAIR * P)
        edge = nc.s_assert_within(edge, 0, E - PAIR * P, skip_runtime_bounds_check_because="the staircase stays inside the edge tiles")
        sp.dma_start(attr[:, b, v * PAIR:(v + 1) * PAIR, :].rearrange("p u e -> p (u e)"), attr_t[:, bass.ds(edge, PAIR * P)]).then_inc(done, 16)


def gather_rows(pool, g, istage, staged, table, rows, gathered, wait_free):
    def stage(r, h):
        pool.tensor_copy(istage[:, h], g["srcs"][:, bass.ds(r * ROUND * G, ROUND * G)]).then_inc(staged, 1)

    def body(i, last=False):
        for h in range(2):
            r = 2 * i + h
            for b in range(ROUND):
                if h or not opening(i):
                    wait_free(r, b)
                if b == 0:
                    pool_wait(pool, staged, r + 1)
                if b == ROUND - 1 and not (last and h):
                    stage(r + 1, 1 - h)
                for u in range(G):
                    at = b * G + u
                    pool.indirect_dma_start(out=rows[:, b, u, 0:D], out_offset=None, in_=table,
                                            in_offset=bass.IndirectOffsetOnAxis(ap=istage[:, h, at:at + 1], axis=0)).then_inc(gathered[b], 16)
    assert WORDS % 2 == 0
    stage(0, 0)
    body(0)
    with pool.Fori(1, WORDS // 2 - 1) as i:
        body(i)
    body(WORDS // 2 - 1, last=True)


def score_phase(nc, con, g, alpha, by_src, queries, places_of, attr_t, we, we3, edge3):
    B = ROUND
    ROUNDS = STEPS // (B * G)
    with phase(nc) as ph:
        sb = lambda n, s, d=F32: ph.enter_context(nc.sbuf_tensor(f"s1_{n}", s, d))
        sem = lambda n: ph.sem(f"s1_{n}")
        psum = lambda n, w: ph.enter_context(nc.psum_tensor(f"s1_{n}", [128, w], F32))
        istage = sb("istage", [P, 2, B * G], I32)
        rows = sb("rows", [P, B, G, D])
        parts = sb("parts", [P, STEPS, H])
        attr = sb("attr", [ED, B, G, P])
        places = sb("places", [1, B, G, 2, P], BF16)
        one, minus = sb("one", [1, P], BF16), sb("minus", [128, 1])
        hot = sb("hot", [P, 2, G, P])
        ps_b = [psum(f"psb{b}", 512) for b in range(2)]
        ps_q = psum("psq", 1024)
        ps_e = [psum(f"pse{b}", 1024) for b in range(2)]
        staged, spreadset, away, hset, eset, added, qset, multiplied, kept, used = (
            sem(n) for n in ("staged", "spreadset", "away", "hset", "eset", "added", "qset", "multiplied", "kept", "used"))
        setup, stored = sem("setup"), sem("stored")
        gathered, attrset, loaded = ([sem(f"{n}{b}") for b in range(B)] for n in ("gathered", "attrset", "loaded"))

        with nc.Block() as block:
            @block.gpsimd
            def _(pool):
                gather_rows(pool, g, istage, staged, by_src, rows, gathered, lambda r, b: pool_wait(pool, used, (r - 1) * B + b + 1))

            @block.sync
            def _(sp):
                def body(i):
                    word = load_stairs(sp, g, i)
                    for b in range(B):
                        n = i * B + b
                        if not isinstance(i, int):
                            sp.wait_ge(qset, n - B + 1)
                            sp.nop(nofuse=True)
                        sp.dma_start(places[:, b].rearrange("o u a e -> o (u a e)"),
                                     places_of[:, bass.ds(n * G * 2 * P, G * 2 * P)]).then_inc(loaded[b], 16)
                        load_attributes(nc, sp, i, b, word, attr, attr_t, attrset[b])
                peeled(sp, ROUNDS, body)
                sp.wait_ge(kept, B * ROUNDS)
                sp.dma_start(edge3, parts[:].rearrange("p s h -> p (s h)")).then_inc(stored, 16)
                sp.wait_ge(stored, 16)

            @block.scalar
            def _(act):
                act.wait_ge(setup, 2)

                def body(i):
                    for b in range(B):
                        n = i * B + b
                        act.wait_ge(spreadset, n + 1)
                        if b >= 2 or not opening(i):
                            act.wait_ge(qset, n - 1)
                        h = hot[:, b % 2].rearrange("p u e -> p (u e)")
                        act.activation(h, ps_b[b % 2][0:P, 0:G * P], ACT.Abs, bias=minus[0:P, :]).then_inc(away, 1)
                        act.wait_ge(away, n + 1)
                        act.activation(h, h, ACT.Relu, scale=-1.0, bias=con["ones"][0:P, 0:1]).then_inc(hset, 1)
                peeled(act, ROUNDS, body)

            @block.tensor
            def _(pe):
                def spread(i, b):
                    n = i * B + b
                    pe.wait_ge(loaded[b], 16 * i + 16)
                    if b >= 2 or not opening(i):
                        pe.wait_ge(kept, n - 1)
                    pe.matmul(ps_b[b % 2][0:P, 0:G * P], one[:], places[:, b, :, 1, :], start=True, stop=True).then_inc(spreadset, 1)

                def edges(i, b):
                    n = i * B + b
                    pe.wait_ge(attrset[b], 16 * GP * i + 16 * GP)
                    if b >= 2 or not opening(i):
                        pe.wait_ge(added, n - 1)
                    for u in range(G):
                        mm = pe.matmul(ps_e[b % 2][0:P, u * D:(u + 1) * D], attr[:, b, u, :], we, start=True, stop=True)
                    mm.then_inc(eset, 1)

                def targets(i, b, word):
                    n = i * B + b
                    ts = node_tiles(nc, word, b)
                    pe.wait_ge(hset, n + 1)
                    for u in range(G):
                        pe.matmul(ps_b[b % 2][0:P, u * H:(u + 1) * H], attr[:, b, u, :], we3, start=True, stop=True)
                    if b or not opening(i):
                        pe.wait_ge(multiplied, n)
                    for u in range(G):
                        t = ts[u // PAIR]
                        mm = pe.matmul(ps_q[0:P, u * D:(u + 1) * D], hot[:, b % 2, u, :],
                                       queries[:, bass.ds(t, 1), 0:D].rearrange("p a d -> p (a d)"), start=True, stop=True)
                    mm.then_inc(qset, 1)

                def body(i, last=False):
                    word = load_stairs(pe, g, i)
                    for b in range(B):
                        ahead = (i, b + 1) if b < B - 1 else (i + 1, 0)
                        if b < B - 1 or not last:
                            spread(*ahead)
                        targets(i, b, word)
                        if b < B - 1 or not last:
                            edges(*ahead)
                pe.wait_ge(setup, 2)
                spread(0, 0)
                edges(0, 0)
                body(0)
                with pe.Fori(1, ROUNDS - 1) as i:
                    body(i)
                body(ROUNDS - 1, last=True)

            @block.vector
            def _(dve):
                def body(i):
                    for b in range(B):
                        n = i * B + b
                        at = n * G
                        s = rows[:, b]
                        dve.wait_ge(gathered[b], 64 * i + 64)
                        dve.wait_ge(eset, n + 1)
                        dve.tensor_tensor(s, s, ps_e[b % 2][0:P, :].rearrange("p (u d) -> p u d", u=G), ALU.add).then_inc(added, 1)
                        dve.wait_ge(added, n + 1)
                        dve.wait_ge(qset, n + 1)
                        dve.tensor_tensor(s, s, ps_q[0:P, :].rearrange("p (u d) -> p u d", u=G), ALU.mult).then_inc(multiplied, 1)
                        dve.tensor_copy(parts[:, bass.ds(at, G), :], ps_b[b % 2][0:P, 0:G * H].rearrange("p (u h) -> p u h", u=G)).then_inc(kept, 1)
                        dve.wait_ge(multiplied, n + 1)
                        dve.tensor_reduce(alpha[:, bass.ds(at, G), :], s.rearrange("p u (h c) -> p u h c", h=H), AX.X, ALU.add).then_inc(used, 1)
                dve.memset(one[:], 1.0).then_inc(setup, 1)
                dve.tensor_scalar(minus[:], con["part"][:, 0:1], -1.0, None, ALU.mult).then_inc(setup, 1)
                peeled(dve, ROUNDS, body)


def node_score_phase(nc, con, g, layer, alpha, selfs, ntab, rows, edge3, acc):
    edges = layer == 3
    nwidth = 2 * H if layer == 2 else H
    B = ROUND
    ROUNDS = STEPS // (B * G)
    with phase(nc) as ph:
        sb = lambda n, s, d=F32: ph.enter_context(nc.sbuf_tensor(f"s{layer}_{n}", s, d))
        sem = lambda n: ph.sem(f"s{layer}_{n}")
        psum = lambda n, w: ph.enter_context(nc.psum_tensor(f"s{layer}_{n}", [128, w], F32))
        places = sb("places", [1, B, G, 2, P], BF16)
        one = sb("one", [1, P], BF16)
        minus = sb("minus", [128, 1])
        hot = sb("hot", [P, 2, G, 2, P])
        tile_mask = sb("tile_mask", [P, 2, G, NT])
        masked = sb("masked", [P, G, NT, H])
        picked = sb("picked", [P, G, H])
        ps_b = psum("psb", 1024)
        ps_s = [psum(f"pss{b}", 1024) for b in range(2)]
        ps_q = [psum(f"psq{b}", 512) for b in range(2)]
        setup, away, masks, products, picks, spreadset, hset, qset, used = (
            sem(n) for n in ("setup", "away", "masks", "products", "picks", "spreadset", "hset", "qset", "used"))
        loaded = [sem(f"loaded{b}") for b in range(B)]
        partsset, summed, cleared = sem("partsset"), sem("summed"), sem("cleared")

        with nc.Block() as block:
            if acc is not None:
                @block.gpsimd
                def _(pool):
                    pool.memset(acc[:], 0.0).then_inc(cleared, 1)
                    pool.wait_ge(cleared, 1)

            @block.sync
            def _(sp):
                def body(i):
                    for b in range(B):
                        n = i * B + b
                        if not isinstance(i, int):
                            sp.wait_ge(spreadset, n - B + 1)
                            sp.nop(nofuse=True)
                        sp.dma_start(places[:, b].rearrange("o u a e -> o (u a e)"),
                                     rows[:, bass.ds(n * G * 2 * P, G * 2 * P)]).then_inc(loaded[b], 16)
                if edges:
                    sp.dma_start(selfs[:].rearrange("p s h -> p (s h)"), edge3).then_inc(partsset, 16)
                peeled(sp, ROUNDS, body)

            @block.scalar
            def _(act):
                act.wait_ge(setup, 2)

                def body(i):
                    for b in range(B):
                        n = i * B + b
                        act.wait_ge(spreadset, n + 1)
                        if b >= 2 or not opening(i):
                            act.wait_ge(qset, n - 1)
                        h = hot[:, b % 2].rearrange("p (k u) a e -> p k (u a e)", k=2)
                        act.activation(h, ps_b[0:P, :].rearrange("p (k x) -> p k x", k=2)[:, :, 0:4 * P], ACT.Abs,
                                       bias=minus[0:P, :]).then_inc(away, 1)
                        act.wait_ge(away, n + 1)
                        act.activation(h, h, ACT.Relu, scale=-1.0, bias=con["ones"][0:P, 0:1]).then_inc(hset, 1)
                peeled(act, ROUNDS, body)

            @block.tensor
            def _(pe):
                def spread(i, b):
                    n = i * B + b
                    pe.wait_ge(loaded[b], 16 * i + 16)
                    if not (opening(i) and b == 0):
                        pe.wait_ge(away, n)
                    for k in range(2):
                        mm = pe.matmul(ps_b[0:P, k * 512:k * 512 + 4 * P], one[:],
                                       places[:, b, 2 * k:2 * k + 2].rearrange("o u a e -> o (u a e)"), start=True, stop=True)
                    mm.then_inc(spreadset, 1)

                def multiply(i, b, word):
                    n = i * B + b
                    ts = node_tiles(nc, word, b)
                    if b >= 2 or not opening(i):
                        pe.wait_ge(used, n - 1)
                    pe.wait_ge(hset, n + 1)
                    for u in range(G):
                        at = u // 2 * 512 + u % 2 * 256
                        pe.matmul(ps_s[b % 2][0:P, at:at + NT * H], hot[:, b % 2, u, 0, :], ntab[:, :, 2 * H:3 * H], start=True, stop=True)
                    for u in range(G):
                        o = ps_q[b % 2][0:P, u * nwidth:(u + 1) * nwidth]
                        t = ts[u // PAIR]
                        mm = pe.matmul(o, hot[:, b % 2, u, 1, :], ntab[:, bass.ds(t, 1), 0:nwidth].rearrange("p a d -> p (a d)"),
                                       start=True, stop=True)
                    mm.then_inc(qset, 1)

                def body(i, last=False):
                    word = load_stairs(pe, g, i)
                    for b in range(B):
                        if b < B - 1:
                            spread(i, b + 1)
                        elif not last:
                            spread(i + 1, 0)
                        multiply(i, b, word)
                pe.wait_ge(setup, 2)
                spread(0, 0)
                body(0)
                with pe.Fori(1, ROUNDS - 1) as i:
                    body(i)
                body(ROUNDS - 1, last=True)

            @block.vector
            def _(dve):
                def mask(i, b):
                    dve.tensor_tensor(tile_mask[:, b % 2], con["iota"][0:P, 0:NT].unsqueeze(1).to_broadcast([P, G, NT]),
                                      g["src_tile"][:, bass.ds((i * B + b) * G, G)].unsqueeze(2).to_broadcast([P, G, NT]),
                                      ALU.is_equal).then_inc(masks, 1)

                def add(b, n):
                    q = ps_q[b % 2][0:P, 0:G * nwidth].rearrange("p (u d) -> p u d", u=G)
                    if not edges:
                        dve.tensor_copy(selfs[:, bass.ds(n * G, G), :], q[:, :, H:])
                    dve.wait_ge(picks, n + 1)
                    dve.tensor_tensor(alpha[:, bass.ds(n * G, G), :], picked[:], q[:, :, 0:H], ALU.add).then_inc(used, 1)

                def body(i, last=False):
                    for b in range(B):
                        n = i * B + b
                        if b or not opening(i):
                            add(b + 1, n - 1)
                        dve.wait_ge(masks, n + 1)
                        dve.wait_ge(qset, n + 1)
                        dve.tensor_tensor(masked[:], ps_s[b % 2][0:P, :].rearrange("p (u x) -> p u x", u=G)[:, :, 0:NT * H].rearrange("p u (t h) -> p u t h", h=H),
                                          tile_mask[:, b % 2].unsqueeze(3).to_broadcast([P, G, NT, H]), ALU.mult).then_inc(products, 1)
                        if b < B - 1:
                            mask(i, b + 1)
                        elif not last:
                            mask(i + 1, 0)
                        dve.wait_ge(products, n + 1)
                        dve.tensor_reduce(picked[:], masked[:].rearrange("p u t h -> p u h t"), AX.X, ALU.add).then_inc(picks, 1)
                dve.memset(one[:], 1.0).then_inc(setup, 1)
                dve.tensor_scalar(minus[:], con["part"][:, 0:1], -1.0, None, ALU.mult).then_inc(setup, 1)
                mask(0, 0)
                body(0)
                with dve.Fori(1, ROUNDS - 1) as i:
                    body(i)
                body(ROUNDS - 1, last=True)
                add(1, B * ROUNDS - 1)
                if edges:
                    dve.wait_ge(partsset, 16)
                    dve.wait_ge(used, B * ROUNDS)
                    dve.tensor_tensor(alpha[:], alpha[:], selfs[:], ALU.add).then_inc(summed, 1)


def softmax_phase(nc, con, g, layer, alpha, selfs):
    with_self = layer == 2
    with phase(nc) as ph:
        sb = lambda n, s, d=F32: ph.enter_context(nc.sbuf_tensor(f"m{layer}_{n}", s, d))
        sem = lambda n: ph.sem(f"m{layer}_{n}")
        ident = con["ident"]
        at = sb("at", [128, CE])
        run_w, back_w = (sb(n, [128, STEPS * H]) for n in ("run", "back"))
        run, back = run_w[:, 0:CE], back_w[:, 0:CE]
        own = sb("own", [128, CE]) if with_self else None
        row, carry, shift, init = sb("row", [1, 128]), sb("carry", [1, 128]), sb("shift", [1, 128]), sb("init", [128, 1])
        ps = [ph.enter_context(nc.psum_tensor(f"m{layer}_ps{b}", [128, 512], F32)) for b in range(4)]
        ps_r = ph.enter_context(nc.psum_tensor(f"m{layer}_psr", [128, 512], F32))
        ps_c = ph.enter_context(nc.psum_tensor(f"m{layer}_psc", [128, 512], F32))
        dv, turned, copied, ended, rowed, shifted, colled, shiftd, powered, weighed, back_t, back_c = (
            sem(n) for n in ("dve", "turned", "copied", "ended", "rowed", "shifted", "colled", "shiftd", "powered", "weighed",
                             "back_t", "back_c"))
        arrays = [(alpha, at, back_w)] + ([(selfs, own, run_w)] if with_self else [])
        by_step = lambda x: x[0:P, :].rearrange("p (s m) -> p s m", s=CT)
        groups = [(a, s0, min(4, CT - s0)) for a in range(len(arrays)) for s0 in range(0, CT, 4)]
        scale = 1.0 / math.sqrt(C) if layer == 1 else 1.0
        chains = 4
        regrouped = sem("regrouped")

        with nc.Block() as block:
            @block.tensor
            def _(pe):
                pe.wait_ge(regrouped, len(arrays))
                for n, (a, s0, k) in enumerate(groups):
                    if n >= 4:
                        pe.wait_ge(copied, n - 3)
                    for j in range(k):
                        mm = pe.transpose(ps[n % 4][:, j * P:(j + 1) * P], by_step(arrays[a][2])[:, s0 + j], ident[0:P, 0:P])
                    mm.then_inc(turned, 1)
                for n in range(chains):
                    pe.wait_ge(ended, n + 1)
                    v = (run[:, CE - 1:CE] if n % 2 == 0 else back[:, 0:1])
                    pe.transpose(ps_r[0:1, 0:128], v, ident[:]).then_inc(rowed, 1)
                    pe.wait_ge(shifted, n + 1)
                    pe.transpose(ps_c[:, 0:1], shift[:], ident[0:1, 0:1]).then_inc(colled, 1)
                pe.wait_ge(weighed, 1)
                for n, (a, s0, k) in enumerate(groups):
                    if n >= 4:
                        pe.wait_ge(back_c, n - 3)
                    for j in range(k):
                        mm = pe.transpose(ps[n % 4][0:P, j * 128:(j + 1) * 128], arrays[a][1][:, (s0 + j) * P:(s0 + j + 1) * P], ident[:])
                    mm.then_inc(back_t, 1)

            @block.scalar
            def _(act):
                for n, (a, s0, k) in enumerate(groups):
                    act.wait_ge(turned, n + 1)
                    act.mul(arrays[a][1][:, s0 * P:(s0 + k) * P], ps[n % 4][:, 0:k * P], scale).then_inc(copied, 1)
                act.wait_ge(shiftd, 1)
                act.activation(at[:], at[:], ACT.Exp).then_inc(powered, 1)
                if with_self:
                    act.activation(own[:], own[:], ACT.Exp).then_inc(powered, 1)
                for n, (a, s0, k) in enumerate(groups):
                    act.wait_ge(back_t, n + 1)
                    view = arrays[a][0][:].rearrange("p (c s) h -> p s c h", c=CH)
                    act.copy(view[:, s0:s0 + k], ps[n % 4][0:P, 0:k * 128].rearrange("p (s c h) -> p s c h", s=k, h=H)).then_inc(back_c, 1)

            @block.vector
            def _(dve):
                c = Tally(dve, dv)
                for x, _, by in arrays:
                    dve.tensor_copy(by_step(by).rearrange("p s (c h) -> p s c h", h=H),
                                    x[:].rearrange("p (c s) h -> p s c h", c=CH)).then_inc(regrouped, 1)
                dve.wait_ge(copied, len(groups))
                if layer != 1:
                    for _, x, _ in arrays:
                        c.up(dve.scalar_tensor_tensor(x[:], x[:], 0.2, x[:], ALU.mult, ALU.max))
                    dve.wait_ge(dv, c.n)
                peak = at
                if with_self:
                    c.then(dve.tensor_tensor(back[:], at[:], own[:], ALU.max))
                    peak = back

                def scan(n, out, flags, src, start, op0, op1, flip):
                    o, f, s = (x[:, ::-1] if flip else x[:, :] for x in (out, flags, src))
                    dve.tensor_tensor_scan(o, f, s, start, op0, op1).then_inc(ended, 1)
                    dve.wait_ge(rowed, n + 1)
                    c.then(dve.tensor_copy(row[:].rearrange("a (h c) -> a h c", h=H), ps_r[0:1, 0:128].rearrange("a (c h) -> a h c", h=H)))
                    fl = g["chunk"][:, 1 if flip else (2 if op0 == ALU.mult else 0)]
                    r, y = (row[:, ::-1], carry[:, ::-1]) if flip else (row[:, :], carry[:, :])
                    c.up(dve.tensor_tensor_scan(y, fl[:, ::-1] if flip else fl, r, start, op0, op1))
                    c.then(dve.memset(shift[:], start))
                    y3 = carry[:].rearrange("a (h c) -> a c h", h=H)
                    s3 = shift[:].rearrange("a (c h) -> a c h", h=H)
                    if flip:
                        dve.tensor_copy(s3[:, 0:CH - 1], y3[:, 1:CH]).then_inc(shifted, 1)
                    else:
                        dve.tensor_copy(s3[:, 1:CH], y3[:, 0:CH - 1]).then_inc(shifted, 1)
                    dve.wait_ge(colled, n + 1)
                    c.then(dve.tensor_copy(init[:], ps_c[:, 0:1]))
                    c.then(dve.tensor_tensor_scan(o, f, s, init[:], op0, op1))

                scan(0, run, g["startf"], peak, -BIG, ALU.add, ALU.max, False)
                scan(1, back, g["endf"], run, -BIG, ALU.add, ALU.max, True)
                if with_self:
                    c.up(dve.tensor_tensor(own[:], own[:], back[:], ALU.subtract))
                c.up(dve.tensor_tensor(at[:], at[:], back[:], ALU.subtract))
                dve.wait_ge(dv, c.n)
                dve.sem_inc(shiftd, 1)
                dve.wait_ge(powered, 2 if with_self else 1)
                scan(2, run, g["keep"], at, 0.0, ALU.mult, ALU.add, False)
                scan(3, back, g["endf"], run, -BIG, ALU.add, ALU.max, True)
                if with_self:
                    c.then(dve.tensor_tensor(back[:], back[:], own[:], ALU.add))
                c.then(dve.tensor_scalar(back[:], back[:], 1e-16, None, ALU.add))
                c.then(dve.reciprocal(back[:], back[:]))
                c.up(dve.tensor_tensor(at[:], at[:], back[:], ALU.mult))
                if with_self:
                    c.then(dve.tensor_tensor(own[:], own[:], back[:], ALU.mult))
                    c.up(dve.scalar_tensor_tensor(own[:], g["endf"][:], -1.0 / BIG, own[:], ALU.mult, ALU.mult))
                dve.wait_ge(dv, c.n)
                dve.sem_inc(weighed, 1)


def message_phase(nc, con, g, layer, acc, weights, selfs, table, attr_t, we):
    first, with_self = layer == 1, layer == 2
    mw = D + H + 1 if with_self else D
    pitch = 512 if with_self else D
    B = ROUND
    ROUNDS = STEPS // (B * G)
    with phase(nc) as ph:
        sb = lambda n, s, d=F32: ph.enter_context(nc.sbuf_tensor(f"a{layer}_{n}", s, d))
        sem = lambda n: ph.sem(f"a{layer}_{n}")
        istage = sb("istage", [P, 2, B * G], I32)
        msg = sb("msg", [P, B, G, mw])
        away, hot = sb("away", [P, 2, G, P]), sb("hot", [P, B, G, P])
        attr = sb("attr", [ED, B, G, P]) if first else None
        ps_o = [ph.enter_context(nc.psum_tensor(f"a{layer}_pso{s}", [128, GP * pitch], F32)) for s in range(2)]
        ps_e = [ph.enter_context(nc.psum_tensor(f"a{layer}_pse{s}", [128, G * D], F32)) for s in range(2)] if first else None
        staged, edone, setup, added, distant = sem("staged"), sem("edone"), sem("setup"), sem("added"), sem("distant")
        gathered, oset, aset, eset, hset, mset, summed = (
            [sem(f"{n}{b}") for b in range(B)] for n in ("gathered", "oset", "aset", "eset", "hset", "mset", "summed"))

        with nc.Block() as block:
            @block.gpsimd
            def _(pool):
                gather_rows(pool, g, istage, staged, table, msg, gathered, lambda r, b: pool_wait(pool, summed[b], r))

            if first:
                @block.sync
                def _(sp):
                    def body(i):
                        word = load_stairs(sp, g, i)
                        for b in range(B):
                            if not isinstance(i, int):
                                sp.wait_ge(eset[b], i)
                                sp.nop(nofuse=True)
                            load_attributes(nc, sp, i, b, word, attr, attr_t, aset[b])
                    peeled(sp, ROUNDS, body)

            @block.scalar
            def _(act):
                def body(i):
                    for b in range(B):
                        n = i * B + b
                        if not isinstance(i, int):
                            act.wait_ge(summed[b], i)
                        if with_self:
                            act.copy(msg[:, b, :, D:D + H], selfs[:, bass.ds(n * G, G), :]).then_inc(oset[b], 1)
                        if b >= 2:
                            act.wait_ge(hset[b - 2], i + 1)
                        elif not isinstance(i, int):
                            act.wait_ge(hset[b + 2], i)
                        for u in range(G):
                            act.activation(away[:, b % 2, u, :], con["iota"][0:P, 0:P], ACT.Abs, scale=-1.0,
                                           bias=g["dstl"][:, bass.ds(n * G + u, 1)]).then_inc(distant, 1)
                        act.wait_ge(distant, (n + 1) * G)
                        act.activation(hot[:, b], away[:, b % 2], ACT.Relu, scale=-1.0, bias=con["ones"][0:P, 0:1]).then_inc(hset[b], 1)
                peeled(act, ROUNDS, body)

            @block.vector
            def _(dve):
                def message(i, b):
                    n = i * B + b
                    v = msg[:, b, :, 0:D]
                    dve.wait_ge(gathered[b], 16 * G * i + 16 * G)
                    if first:
                        dve.wait_ge(eset[b], i + 1)
                        dve.tensor_tensor(v, v, ps_e[b % 2][0:P, :].rearrange("p (u d) -> p u d", u=G), ALU.add).then_inc(edone, 1)
                        dve.wait_ge(edone, n + 1)
                    v = v.rearrange("p u (h c) -> p u h c", h=H)
                    dve.tensor_tensor(v, v, weights[:, bass.ds(n * G, G), :].unsqueeze(3).to_broadcast([P, G, H, C]), ALU.mult).then_inc(mset[b], 1)

                def add(i, b, n, word):
                    ts = node_tiles(nc, word, b)
                    dve.wait_ge(summed[b], i + 1)
                    for v in range(GP):
                        row = acc[:, bass.ds(ts[v], 1), 0:mw].rearrange("p a d -> p (a d)")
                        dve.tensor_tensor(row, row, ps_o[b % 2][0:P, v * pitch:v * pitch + mw], ALU.add).then_inc(added, 1)
                        dve.wait_ge(added, n * GP + v + 1)

                def body(i):
                    for b in range(B):
                        if b == 2:
                            word = load_stairs(dve, g, i)
                        elif b == 0 and not isinstance(i, int):
                            word = load_stairs(dve, g, i - 1)
                        message(i, b)
                        if b >= 2:
                            add(i, b - 2, i * B + b - 2, word)
                        elif not isinstance(i, int):
                            add(i - 1, b + 2, i * B + b - 2, word)
                if with_self:
                    dve.memset(msg[:, :, :, D + H:], 1.0).then_inc(setup, 1)
                peeled(dve, ROUNDS, body)
                word = load_stairs(dve, g, ROUNDS - 1)
                for b in (B - 2, B - 1):
                    add(ROUNDS - 1, b, (ROUNDS - 1) * B + b, word)

            @block.tensor
            def _(pe):
                def edges(i, b):
                    n = i * B + b
                    pe.wait_ge(aset[b], 16 * GP * i + 16 * GP)
                    if b >= 2 or not opening(i):
                        pe.wait_ge(edone, n - 1)
                    for u in range(G):
                        mm = pe.matmul(ps_e[b % 2][0:P, u * D:(u + 1) * D], attr[:, b, u, :], we, start=True, stop=True)
                    mm.then_inc(eset[b], 1)

                def total(i, b):
                    n = i * B + b
                    pe.wait_ge(hset[b], i + 1)
                    pe.wait_ge(mset[b], i + 1)
                    if with_self:
                        pe.wait_ge(oset[b], i + 1)
                    if b >= 2 or not opening(i):
                        pe.wait_ge(added, (n - 1) * GP)
                    for u in range(G):
                        at = u // PAIR * pitch
                        mm = pe.matmul(ps_o[b % 2][0:P, at:at + mw], hot[:, b, u, :], msg[:, b, u, :],
                                       start=u % PAIR == 0, stop=u % PAIR == PAIR - 1)
                    mm.then_inc(summed[b], 1)

                def body(i, last=False):
                    for b in range(B):
                        total(i, b)
                        if first and b < 2:
                            edges(i, b + 2)
                        elif first and not last:
                            edges(i + 1, b - 2)
                if first:
                    edges(0, 0)
                    edges(0, 1)
                if with_self:
                    pe.wait_ge(setup, 1)
                body(0)
                with pe.Fori(1, ROUNDS - 1) as i:
                    body(i)
                body(ROUNDS - 1, last=True)


def attention_end_phase(nc, con, X, acc, table, bias):
    U = 5
    with phase(nc) as ph:
        sb = lambda n, s, d=F32: ph.enter_context(nc.sbuf_tensor(f"e_{n}", s, d))
        sem = lambda n: ph.sem(f"e_{n}")
        h2, neg = sb("h2", [P, U, D]), sb("neg", [P, U, D])
        ws = sb("ws", [P, NT, H])
        alone = sb("alone", [P, NT])
        dv, low, powered, done = (sem(n) for n in ("dve", "low", "powered", "done"))
        loaded, elu = ([sem(f"{n}{u}") for u in range(U)] for n in ("loaded", "elu"))
        with nc.Block() as block:
            @block.sync
            def _(sp):
                def body(i):
                    for u in range(U):
                        n = i * U + u
                        if not isinstance(i, int):
                            sp.wait_ge(done, n - U + 1)
                        sp.dma_start(h2[:, u, :], table[bass.ds(n * P, P), :]).then_inc(loaded[u], 16)
                peeled(sp, NT // U, body)

            @block.scalar
            def _(act):
                def body(i):
                    for u in range(U):
                        act.wait_ge(low, i * U + u + 1)
                        act.activation(neg[:, u, :], neg[:, u, :], ACT.Exp).then_inc(powered, 1)
                peeled(act, NT // U, body)

            @block.vector
            def _(dve):
                c = Tally(dve, dv)
                c.then(dve.tensor_scalar(alone[:], acc[:, :, D + H], 0.5, None, ALU.is_lt))
                c.then(dve.tensor_tensor(ws[:], acc[:, :, D:D + H], alone[:].unsqueeze(2).to_broadcast([P, NT, H]), ALU.add))
                start = c.n
                PER = 3 * U

                def body(i):
                    c = Tally(dve, dv, i * PER + start)
                    for u in range(U):
                        n = i * U + u
                        z = acc[:, bass.ds(n, 1), 0:D].rearrange("p a d -> p (a d)")
                        m = h2[:, u, :]
                        dve.wait_ge(loaded[u], 16 * i + 16)
                        c.then(dve.tensor_tensor(m.rearrange("p (h c) -> p h c", h=H), m.rearrange("p (h c) -> p h c", h=H),
                                                 ws[:, bass.ds(n, 1), :].rearrange("p a h -> p (a h)").unsqueeze(2).to_broadcast([P, H, C]), ALU.mult))
                        c.then(dve.tensor_tensor(m, m, bias[:], ALU.add))
                        c.then(dve.tensor_tensor(z, z, m, ALU.add))
                        if not isinstance(i, int):
                            dve.wait_ge(done, n - U + 1)
                        dve.tensor_scalar(neg[:, u, :], z, 0.0, None, ALU.min).then_inc(low, 1)
                    for u in range(U):
                        n = i * U + u
                        z = acc[:, bass.ds(n, 1), 0:D].rearrange("p a d -> p (a d)")
                        x = X[:, bass.ds(n, 1), :].rearrange("p a d -> p (a d)")
                        dve.wait_ge(powered, n + 1)
                        dve.scalar_tensor_tensor(z, z, 0.0, neg[:, u, :], ALU.max, ALU.add).then_inc(elu[u], 1)
                        dve.wait_ge(elu[u], i + 1)
                        dve.scalar_tensor_tensor(x, z, -1.0, x, ALU.add, ALU.add).then_inc(done, 1)
                peeled(dve, NT // U, body)


def final_phase(nc, con, X, acc, gamma, beta, out):
    U = 5
    with phase(nc) as ph:
        sb = lambda n, s, d=F32: ph.enter_context(nc.sbuf_tensor(f"f_{n}", s, d))
        sem = lambda n: ph.sem(f"f_{n}")
        st = sb("st", [P, NT, 6])
        mean, dif, var, rstd, nb = (sb(n, [P, NT]) for n in ("mean", "dif", "var", "rstd", "nb"))
        y = sb("y", [P, U, D])
        dv, spread, rooted, ready, normed, done = (sem(n) for n in ("dve", "spread", "rooted", "ready", "normed", "done"))
        stored = [sem(f"stored{u}") for u in range(U)]
        with nc.Block() as block:
            @block.vector
            def _(dve):
                with dve.Fori(0, NT) as n:
                    dve.bn_stats(st[:, bass.ds(n, 1), :].rearrange("p a s -> p (a s)"),
                                 acc[:, bass.ds(n, 1), 0:D].rearrange("p a d -> p (a d)")).then_inc(dv, 1)
                dve.wait_ge(dv, NT)
                c = Tally(dve, dv, NT)
                me, mo = st[:, :, 1], st[:, :, 4]
                c.up(dve.tensor_tensor(mean[:], me, mo, ALU.add))
                c.up(dve.tensor_tensor(dif[:], me, mo, ALU.subtract))
                c.then(dve.tensor_tensor(var[:], st[:, :, 2], st[:, :, 5], ALU.add))
                c.up(dve.tensor_scalar(mean[:], mean[:], 0.5, None, ALU.mult))
                c.then(dve.scalar_tensor_tensor(dif[:], dif[:], 0.25, dif[:], ALU.mult, ALU.mult))
                c.then(dve.scalar_tensor_tensor(var[:], var[:], 1.0 / D, dif[:], ALU.mult, ALU.add))
                dve.tensor_scalar(var[:], var[:], EPS, None, ALU.add).then_inc(spread, 1)
                dve.wait_ge(rooted, 1)
                c.then(dve.reciprocal(rstd[:], dif[:]))
                dve.scalar_tensor_tensor(nb[:], mean[:], -1.0, rstd[:], ALU.mult, ALU.mult).then_inc(ready, 1)
                start = NT + c.n

                def body(i):
                    c = Tally(dve, dv, i * 2 * U + start)
                    for u in range(U):
                        n = i * U + u
                        dve.wait_ge(normed, n + 1)
                        c.then(dve.tensor_tensor(y[:, u, :], y[:, u, :], gamma[:], ALU.mult))
                        c.then(dve.tensor_tensor(y[:, u, :], y[:, u, :], beta[:], ALU.add))
                        dve.tensor_tensor(y[:, u, :], y[:, u, :], X[:, bass.ds(n, 1), :].rearrange("p a d -> p (a d)"), ALU.add).then_inc(done, 1)
                peeled(dve, NT // U, body)

            @block.scalar
            def _(act):
                act.wait_ge(spread, 1)
                act.activation(dif[:], var[:], ACT.Sqrt).then_inc(rooted, 1)
                act.wait_ge(ready, 1)

                def body(i):
                    for u in range(U):
                        n = i * U + u
                        if not isinstance(i, int):
                            act.wait_ge(stored[u], 16 * i)
                        act.activation(y[:, u, :], acc[:, bass.ds(n, 1), 0:D].rearrange("p a d -> p (a d)"), ACT.Identity,
                                       bias=nb[:, bass.ds(n, 1)], scale=rstd[:, bass.ds(n, 1)]).then_inc(normed, 1)
                peeled(act, NT // U, body)

            @block.sync
            def _(sp):
                def body(i):
                    for u in range(U):
                        n = i * U + u
                        sp.wait_ge(done, n + 1)
                        sp.dma_start(out[bass.ds(n * P, P), :], y[:, u, :]).then_inc(stored[u], 16)
                peeled(sp, NT // U, body)
                for u in range(U):
                    sp.wait_ge(stored[u], 16 * (NT // U))


def weights_phase(nc, con, a, w):
    with phase(nc) as ph:
        sb = lambda n, s, d=F32: ph.enter_context(nc.sbuf_tensor(f"w_{n}", s, d))
        att = {n: sb(n, [128, D]) for n in ("l2s", "l2d", "l3s", "l3d", "l3e")}
        wedge = sb("wedge", [ED, D])
        prod = sb("prod", [128, 9, D])
        loaded, folded = ph.sem("w_loaded"), ph.sem("w_folded")
        with nc.Block() as block:
            @block.sync
            def _(sp):
                rows = lambda x: x.rearrange("(a p) n -> p a n", p=128)
                loads = [(w["l2"][:, :, 0:D], rows(a["w2"])), (w["l3"][:, :, 0:D], rows(a["w3"])),
                         (wedge[:], a["we3"]), (w["x"][:], a["x"].rearrange("(n p) d -> p n d", p=P))]
                for k in ("b2", "b3", "gamma", "beta"):
                    loads.append((w[k][:], a[k].to_broadcast([P, a[k].shape[1]])))
                for k in att:
                    loads.append((att[k][:], a[k].to_broadcast([128, D])))
                for dst, src in loads:
                    sp.dma_start(dst, src).then_inc(loaded, 16)
                con["loads"] = len(loads)

            @block.vector
            def _(dve):
                dve.wait_ge(loaded, 16 * con["loads"])
                jobs = []
                for name, s, d in (("l2", "l2s", "l2d"), ("l3", "l3s", "l3d")):
                    for half in range(2):
                        for j, v in enumerate((s, d)):
                            jobs.append((w[name][:, half, 0:D], att[v][:], w[name][:, half, D + j * H:D + (j + 1) * H], 128))
                jobs.append((wedge[:], att["l3e"][0:ED, :], w["we3"][:], ED))
                for n, (x, v, o, p) in enumerate(jobs):
                    dve.tensor_tensor(prod[0:p, n, :], x, v, ALU.mult).then_inc(folded, 1)
                dve.wait_ge(folded, len(jobs))
                for n, (x, v, o, p) in enumerate(jobs):
                    dve.tensor_reduce(o, prod[0:p, n, :].rearrange("p (h c) -> p h c", h=H), AX.X, ALU.add).then_inc(folded, 1)


def program(nc, a, out):
    with ExitStack() as ctx:
        sb = lambda n, s, d=F32: ctx.enter_context(nc.sbuf_tensor(n, s, d))
        dram = lambda n, r, c: nc.dram_tensor(n, (r, c), F32, kind="Internal").ap()
        con = {k: sb("con_" + k, [128, n]) for k, n in
               (("ident", 128), ("iota", 256), ("iota1", 128), ("after", 128), ("ones", 128), ("part", 2))}
        con["rounds"] = sb("con_rounds", [1, 1], I32)
        w = {"l2": sb("wt2", [128, 2, D + 2 * H]), "l3": sb("wt3", [128, 2, D + 2 * H]),
             "we3": sb("we3", [ED, H]), "x": sb("x", [P, NT, D])}
        for k, n in (("b2", D), ("b3", D), ("gamma", D), ("beta", D)):
            w[k] = sb("row_" + k, [P, n])
        X = w["x"]
        rlist = dram("rotation_list", (LIST_BLOCKS + 1) * SLOT, FIELDS)
        constants_phase(nc, con)
        weights_phase(nc, con, a, w)
        with ExitStack() as lists:
            lsb = lambda n, s, d=F32: lists.enter_context(nc.sbuf_tensor(n, s, d))
            pay, pos, due = lsb("list_fields", [P, ET, FIELDS]), lsb("list_place", [P, ET], I32), lsb("list_due", [1, GROUPS], I32)
            MT = lsb("MT", [128, 2, ROT])
            rotation_list_phase(nc, con, a["w_e"], a["src_e"], a["dst_e"], rlist, pay, pos, due)
            rotation_phase(nc, con, rlist, MT, pay, pos, due)
            dense_phase(nc, con, 0, X, None, None, MT, ROT, None, [])

        acc = sb("acc", [P, NT, AW])
        g = {"srcs": sb("g_srcs", [P, STEPS], I32), "dstl": sb("g_dstl", [P, STEPS]), "src_tile": sb("g_src_tile", [P, STEPS]),
             "stairs": sb("g_stairs", [1, WORDS], I32),
             "startf": sb("g_start", [128, CE]), "endf": sb("g_end", [128, CE]), "keep": sb("g_keep", [128, CE]),
             "chunk": sb("g_chunk", [1, 3, 128])}
        rows2 = lambda x: x.rearrange("(k p) -> k p", p=P)
        live = nc.dram_tensor("live_targets", (STEPS * P + 2,), F32, kind="Internal").ap()
        places = nc.dram_tensor("places", (1, STEPS * 2 * P), BF16, kind="Internal").ap()
        alpha = sb("alpha", [P, STEPS, H])
        edge3 = dram("edge_parts_3", P, STEPS * H)
        with ExitStack() as first:
            fsb = lambda n, s, d=F32: first.enter_context(nc.sbuf_tensor(n, s, d))
            w1, we1, b1 = fsb("wt1", [128, 2, 4 * D]), fsb("we1", [ED, D]), fsb("row_b1", [P, 4 * D])
            loads = [(w1[:], a["w1"].rearrange("(a p) n -> p a n", p=128)), (we1[:], a["we1"]), (b1[:], a["b1"].to_broadcast([P, 4 * D]))]
            graph_phase(nc, con, g, rows2(a["src"]), rows2(a["dst"]), a["dst_e"], live, places, loads)

            tk, tv = dram("table_k", N, D), dram("table_v", N, D)
            dense_phase(nc, con, 1, X, None, acc, w1, 4 * D, b1, [(tk, D, 2 * D), (tv, 2 * D, 3 * D)])
            score_phase(nc, con, g, alpha, tk, acc, places, a["attr_t"], we1[:], w["we3"][:], edge3)
            softmax_phase(nc, con, g, 1, alpha, None)
            message_phase(nc, con, g, 1, X, alpha, None, tv, a["attr_t"], we1[:])

        selfs, ntab = sb("selfs", [P, STEPS, H]), sb("node_scores", [P, NT, 3 * H])
        t2 = dram("table_h2", N, D)
        dense_phase(nc, con, 2, X, None, ntab, w["l2"], D + 2 * H, None, [(t2, 0, D)])
        node_score_phase(nc, con, g, 2, alpha, selfs, ntab, places, None, acc)
        softmax_phase(nc, con, g, 2, alpha, selfs)
        message_phase(nc, con, g, 2, acc, alpha, selfs, t2, None, None)
        attention_end_phase(nc, con, X, acc, t2, w["b2"])

        t3 = dram("table_h3", N, D)
        dense_phase(nc, con, 3, X, acc, ntab, w["l3"], D + 2 * H, w["b3"], [(t3, 0, D)])
        node_score_phase(nc, con, g, 3, alpha, selfs, ntab, places, edge3, None)
        softmax_phase(nc, con, g, 3, alpha, None)
        message_phase(nc, con, g, 3, acc, alpha, None, t3, None, None)
        final_phase(nc, con, X, acc, w["gamma"], w["beta"], out)


def kernel(**inp):
    import concourse.bacc as _bacc
    from concourse.bass_utils import run_bass_kernel_spmd as _run
    nc = _bacc.Bacc("TRN2", target_bir_lowering=False, num_devices=1)
    inp = {k: np.asarray(v) for k, v in inp.items()}
    row = lambda x: x.reshape(1, -1)
    tiles = lambda x: x.reshape(ET, P).T
    host = {
        "x": inp["x"], "src": inp["src"], "dst": inp["dst"],
        "src_e": tiles(inp["src"]), "dst_e": tiles(inp["dst"]), "w_e": tiles(inp["edge_weight"]),
        "attr_t": inp["edge_attr_64"].T,
        "w1": np.concatenate([inp[f"L1_gnn_W{k}"].T for k in ("q", "k", "v", "skip")], axis=1),
        "b1": np.concatenate([row(inp[f"L1_gnn_b{k}"]) for k in ("q", "k", "v", "skip")], axis=1),
        "we1": inp["L1_gnn_We"].T, "w2": inp["L2_gnn_W0"].T, "b2": row(inp["L2_gnn_b0"]),
        "l2s": row(inp["L2_gnn_att_src0"]), "l2d": row(inp["L2_gnn_att_dst0"]),
        "w3": inp["L3_gnn_W"], "we3": inp["L3_gnn_W_e"], "l3s": row(inp["L3_gnn_att_src"]), "l3d": row(inp["L3_gnn_att_dst"]),
        "l3e": row(inp["L3_gnn_att_edge"]), "b3": row(inp["L3_gnn_bias"]), "gamma": row(inp["L3_gnn_gamma"]),
        "beta": row(inp["L3_gnn_beta"]),
    }
    arrays, args = {}, {}
    for n, x in host.items():
        x = np.ascontiguousarray(x)
        arrays[f"in_{n}"] = x
        args[n] = nc.dram_tensor(f"in_{n}", x.shape, mybir.dt.from_np(x.dtype), kind="ExternalInput").ap()
    out = nc.dram_tensor("out_0", (N, D), F32, kind="ExternalOutput").ap()
    program(nc, args, out)
    r = _run(nc, [arrays], core_ids=[0])
    return r.results[0]["out_0"]
```
